# Optimizing a Trainium2 kernel written in Bass

```python
import numpy as np
import jax
import jax.numpy as jnp

def _softmax(x, axis=-1):
    return jax.nn.softmax(x, axis=axis)

def _gelu(x):
    return jax.nn.gelu(x, approximate=True)

def _silu(x):
    return jax.nn.silu(x)

def _sigmoid(x):
    return jax.nn.sigmoid(x)

def _layernorm(x, axis=-1, eps=1e-05):
    m = jnp.mean(x, axis=axis, keepdims=True)
    v = jnp.var(x, axis=axis, keepdims=True)
    return (x - m) / jnp.sqrt(v + eps)

def _scatter_add(tgt, idx, src, axis=0):
    return tgt.at[idx].add(src)

def _segment_sum(src, seg, n):
    return jax.ops.segment_sum(src, seg, n)
kernel_name = 'mk_adj_ffn_d4_adj_r2_426295'

def setup_inputs(seed: int=0):
    np.random.seed(seed)
    _w = jnp.asarray

    def _rec_inputs():
        import jax
        import jax.numpy as jnp
        _gk = jax.random.key(seed)
        x = -0.0002928 + 1 * jax.random.normal(jax.random.fold_in(_gk, 1), (16, 512, 128), jnp.float32)
        _w = (1.0 + jnp.arange(512, dtype=jnp.float32)) ** (-0.5)
        _w = _w / _w.mean()
        _pij = jnp.clip(0.03125 * _w[:, None] * _w[None, :], 0.0, 1.0)
        _a = jax.random.uniform(jax.random.fold_in(_gk, 2), (16, 512, 512)) < _pij
        adj = _a.astype(jnp.int32)
        return (x, adj)
    x, adj = _rec_inputs()

    def _L0_gnn_setup():
        import jax, jax.numpy as jnp
        import numpy as np
        OUT = 128
        NUM_LAYERS = 3

        def _gru_cell(inp, h, w_ih, w_hh, b_ih, b_hh):
            gi = inp @ w_ih.T + b_ih
            gh = h @ w_hh.T + b_hh
            i_r, i_z, i_n = jnp.split(gi, 3, axis=-1)
            h_r, h_z, h_n = jnp.split(gh, 3, axis=-1)
            r = jax.nn.sigmoid(i_r + h_r)
            z = jax.nn.sigmoid(i_z + h_z)
            n = jnp.tanh(i_n + r * h_n)
            return (1.0 - z) * n + z * h
        key = jax.random.key(seed)
        ks = jax.random.split(key, 8)
        B, N, D = (32, 256, 128)
        x = jax.random.normal(ks[0], (B, N, D), dtype=jnp.float32)
        adj = jax.random.randint(ks[1], (B, N, N), 0, 2, dtype=jnp.int32)
        s = 1.0 / np.sqrt(OUT)
        weight = jax.random.uniform(ks[2], (NUM_LAYERS, OUT, OUT), jnp.float32, -s, s)
        w_ih = jax.random.uniform(ks[3], (3 * OUT, OUT), jnp.float32, -s, s)
        w_hh = jax.random.uniform(ks[4], (3 * OUT, OUT), jnp.float32, -s, s)
        b_ih = jax.random.uniform(ks[5], (3 * OUT,), jnp.float32, -s, s)
        b_hh = jax.random.uniform(ks[6], (3 * OUT,), jnp.float32, -s, s)
        return {'x': x, 'adj': adj, 'weight': weight, 'w_ih': w_ih, 'w_hh': w_hh, 'b_ih': b_ih, 'b_hh': b_hh}
    _L0_gnn_all = _L0_gnn_setup()
    _L0_gnn_in = {k: v for k, v in _L0_gnn_all.items() if k in ('weight', 'w_ih', 'w_hh', 'b_ih', 'b_hh')}
    del _L0_gnn_all

    def _L0_ffn_setup():
        import jax, jax.numpy as jnp
        import numpy as np
        E = 8
        K = 2
        D = 128
        H = 256
        DOUT = 128
        EPS = 1e-05
        key = jax.random.key(seed)
        ks = jax.random.split(key, 9)
        s = 0.02
        return {'x': jax.random.normal(ks[0], (4, 4096, D), jnp.float32), 'gamma': 1.0 + 0.05 * jax.random.normal(ks[1], (D,), jnp.float32), 'beta': 0.05 * jax.random.normal(ks[2], (D,), jnp.float32), 'Wr': 0.01 * jax.random.normal(ks[3], (D, E), jnp.float32), 'br': jnp.zeros((E,), jnp.float32), 'W1': s * jax.random.normal(ks[4], (E, D, H), jnp.float32), 'b1': s * jax.random.normal(ks[5], (E, H), jnp.float32), 'W2': s * jax.random.normal(ks[6], (E, H, DOUT), jnp.float32), 'b2': s * jax.random.normal(ks[7], (E, DOUT), jnp.float32)}
    _L0_ffn_all = _L0_ffn_setup()
    _L0_ffn_in = {k: v for k, v in _L0_ffn_all.items() if k in ('gamma', 'beta', 'Wr', 'br', 'W1', 'b1', 'W2', 'b2')}
    del _L0_ffn_all

    def _L1_gnn_setup():
        import jax, jax.numpy as jnp
        import numpy as np
        NEG_INF = -1000000000.0
        LEAKY_ALPHA = 0.2
        key = jax.random.key(seed)
        k1, k2, k3, k4 = jax.random.split(key, 4)
        B, N, Din, Dout = (16, 1024, 128, 128)
        h = jax.random.normal(k1, (B, N, Din), dtype=jnp.float32)
        adj = jax.random.randint(k2, (B, N, N), 0, 2, dtype=jnp.int32)
        W = jax.random.normal(k3, (Din, Dout), dtype=jnp.float32) * (1.0 / np.sqrt(Din))
        a = jax.random.normal(k4, (2 * Dout,), dtype=jnp.float32) * (1.0 / np.sqrt(2 * Dout))
        return {'h': h, 'adj': adj, 'W': W, 'a': a}
    _L1_gnn_all = _L1_gnn_setup()
    _L1_gnn_in = {k: v for k, v in _L1_gnn_all.items() if k in ('W', 'a')}
    del _L1_gnn_all

    def _L1_ffn_setup():
        import jax, jax.numpy as jnp
        import numpy as np
        DIM = 128
        H = 8
        D = 64
        G = 64
        INNER = H * D
        SCALE = D ** (-0.5)
        key = jax.random.key(seed)
        ks = jax.random.split(key, 12)
        B, N = (4, 8192)
        x = jax.random.normal(ks[0], (B, N, DIM), dtype=jnp.float32)
        s = lambda fan_in: 1.0 / np.sqrt(fan_in)
        W_fx = jax.random.normal(ks[1], (DIM, INNER), dtype=jnp.float32) * s(DIM)
        b_fx = jnp.zeros((INNER,), dtype=jnp.float32)
        W_x = jax.random.normal(ks[2], (DIM, INNER), dtype=jnp.float32) * s(DIM)
        b_x = jnp.zeros((INNER,), dtype=jnp.float32)
        A = jax.random.normal(ks[3], (G, D), dtype=jnp.float32)
        Q, _ = jnp.linalg.qr(A.T)
        W_slice = Q[:, :G].astype(jnp.float32)
        b_slice = jnp.zeros((G,), dtype=jnp.float32)
        W_q = jax.random.normal(ks[4], (D, D), dtype=jnp.float32) * s(D)
        W_k = jax.random.normal(ks[5], (D, D), dtype=jnp.float32) * s(D)
        W_v = jax.random.normal(ks[6], (D, D), dtype=jnp.float32) * s(D)
        W_out = jax.random.normal(ks[7], (INNER, DIM), dtype=jnp.float32) * s(INNER)
        b_out = jnp.zeros((DIM,), dtype=jnp.float32)
        temperature = jnp.ones((1, H, 1, 1), dtype=jnp.float32) * 0.5
        return {'x': x, 'W_fx': W_fx, 'b_fx': b_fx, 'W_x': W_x, 'b_x': b_x, 'W_slice': W_slice, 'b_slice': b_slice, 'W_q': W_q, 'W_k': W_k, 'W_v': W_v, 'W_out': W_out, 'b_out': b_out, 'temperature': temperature}
    _L1_ffn_all = _L1_ffn_setup()
    _L1_ffn_in = {k: v for k, v in _L1_ffn_all.items() if k in ('W_fx', 'b_fx', 'W_x', 'b_x', 'W_slice', 'b_slice', 'W_q', 'W_k', 'W_v', 'W_out', 'b_out', 'temperature')}
    del _L1_ffn_all

    def _L2_gnn_setup():
        import jax, jax.numpy as jnp
        import numpy as np
        key = jax.random.key(seed)
        k1, k2, k3, k4 = jax.random.split(key, 4)
        B, N, F, U = (8, 1024, 128, 128)
        x = jax.random.normal(k1, (B, N, F), dtype=jnp.float32)
        adj = jax.random.randint(k2, (B, N, N), 0, 2, dtype=jnp.int32)
        W_msg = jax.random.normal(k3, (F, U), dtype=jnp.float32) / np.sqrt(F)
        W_upd = jax.random.normal(k4, (F, U), dtype=jnp.float32) / np.sqrt(F)
        bias = jnp.zeros((U,), dtype=jnp.float32)
        return {'x': x, 'adj': adj, 'W_msg': W_msg, 'W_upd': W_upd, 'bias': bias}
    _L2_gnn_all = _L2_gnn_setup()
    _L2_gnn_in = {k: v for k, v in _L2_gnn_all.items() if k in ('W_msg', 'W_upd', 'bias')}
    del _L2_gnn_all

    def _L2_ffn_setup():
        import jax, jax.numpy as jnp
        import numpy as np
        D_MODEL = 128
        D_STATE = 64
        D_CONV = 4
        EXPAND = 2
        HEADDIM = 64
        D_INNER = EXPAND * D_MODEL
        NHEADS = D_INNER // HEADDIM
        CONV_DIM = D_INNER + 2 * D_STATE
        D_IN_PROJ = 2 * D_INNER + 2 * D_STATE + NHEADS
        CHUNK = 128
        EPS = 1e-05

        def segsum(a):
            T = a.shape[-1]
            cs = jnp.cumsum(a, axis=-1)
            ss = cs[..., :, None] - cs[..., None, :]
            mask = jnp.tril(jnp.ones((T, T), dtype=bool))
            return jnp.where(mask, ss, -jnp.inf)

        def mamba2_block(x, W_in, conv_w, conv_b, dt_bias, A_log, D, norm_w, W_out, W_lin, b_lin):
            Bsz, L, _ = x.shape
            zxbcdt = x @ W_in
            z, xBC, dt = jnp.split(zxbcdt, [D_INNER, D_INNER + CONV_DIM], axis=-1)
            xp = jnp.pad(xBC, ((0, 0), (D_CONV - 1, 0), (0, 0)))
            conv = conv_b + sum((xp[:, k:k + L, :] * conv_w[:, k] for k in range(D_CONV)))
            xBC = jax.nn.silu(conv)
            xh, Bmat, Cmat = jnp.split(xBC, [D_INNER, D_INNER + D_STATE], axis=-1)
            dt = jax.nn.softplus(dt + dt_bias)
            A = -jnp.exp(A_log)
            nc = L // CHUNK
            xh = xh.reshape(Bsz, nc, CHUNK, NHEADS, HEADDIM)
            Bc = Bmat.reshape(Bsz, nc, CHUNK, D_STATE)
            Cc = Cmat.reshape(Bsz, nc, CHUNK, D_STATE)
            dtc = dt.reshape(Bsz, nc, CHUNK, NHEADS)
            dA = jnp.einsum('bclh,h->bhcl', dtc, A)
            A_cum = jnp.cumsum(dA, axis=-1)
            Lmat = jnp.exp(segsum(dA))
            xdt = xh * dtc[..., None]
            Y_diag = jnp.einsum('bcln,bcsn,bhcls,bcshp->bclhp', Cc, Bc, Lmat, xdt)
            decay_states = jnp.exp(A_cum[..., -1:] - A_cum)
            states = jnp.einsum('bcln,bhcl,bclhp->bchpn', Bc, decay_states, xdt)
            chunk_decay = jnp.exp(A_cum[..., -1])

            def step(h, inp):
                s, d = inp
                return (h * d[..., None, None] + s, h)
            _, prevs = jax.lax.scan(step, jnp.zeros_like(states[:, 0]), (jnp.moveaxis(states, 1, 0), jnp.moveaxis(chunk_decay, 2, 0)))
            prevs = jnp.moveaxis(prevs, 0, 1)
            Y_off = jnp.einsum('bcln,bchpn,bhcl->bclhp', Cc, prevs, jnp.exp(A_cum))
            Y = (Y_diag + Y_off + xh * D[:, None]).reshape(Bsz, L, D_INNER)
            Y = Y * jax.nn.silu(z)
            Y = Y * jax.lax.rsqrt(jnp.mean(Y * Y, axis=-1, keepdims=True) + EPS) * norm_w
            out = Y @ W_out
            return out @ W_lin + b_lin
        key = jax.random.key(seed)
        ks = jax.random.split(key, 12)
        B, L = (8, 2048)

        def gauss(k, shape, scale):
            return jax.random.normal(k, shape, dtype=jnp.float32) * scale
        return {'x': gauss(ks[0], (B, L, D_MODEL), 1.0), 'W_in': gauss(ks[1], (D_MODEL, D_IN_PROJ), D_MODEL ** (-0.5)), 'conv_w': gauss(ks[2], (CONV_DIM, D_CONV), 0.3), 'conv_b': gauss(ks[3], (CONV_DIM,), 0.1), 'dt_bias': jax.random.uniform(ks[4], (NHEADS,), minval=-4.0, maxval=-1.0), 'A_log': jnp.log(jax.random.uniform(ks[5], (NHEADS,), minval=1.0, maxval=16.0)), 'D': jnp.ones((NHEADS,), jnp.float32), 'norm_w': jnp.ones((D_INNER,), jnp.float32), 'W_out': gauss(ks[6], (D_INNER, D_MODEL), D_INNER ** (-0.5)), 'W_lin': gauss(ks[7], (D_MODEL, D_MODEL), D_MODEL ** (-0.5)), 'b_lin': jnp.zeros((D_MODEL,), jnp.float32)}
    _L2_ffn_all = _L2_ffn_setup()
    _L2_ffn_in = {k: v for k, v in _L2_ffn_all.items() if k in ('W_in', 'conv_w', 'conv_b', 'dt_bias', 'A_log', 'D', 'norm_w', 'W_out', 'W_lin', 'b_lin')}
    del _L2_ffn_all

    def _L3_gnn_setup():
        import jax, jax.numpy as jnp
        import numpy as np
        NEG_INF = -1000000000.0
        N_HEADS = 4

        def _graph_mha(x, adj_mask, Wq, bq, Wk, bk, Wv, bv):
            B, N, _ = x.shape
            Hd = Wq.shape[1]
            d = Hd // N_HEADS
            q = (x @ Wq + bq).reshape(B, N, N_HEADS, d)
            k = (x @ Wk + bk).reshape(B, N, N_HEADS, d)
            v = (x @ Wv + bv).reshape(B, N, N_HEADS, d)
            scale = 1.0 / d ** 0.5
            scores = jnp.einsum('bqhd,bkhd->bhqk', q, k) * scale
            scores = jnp.where(adj_mask[:, None, :, :], scores, NEG_INF)
            attn = jax.nn.softmax(scores, axis=-1)
            out = jnp.einsum('bhqk,bkhd->bqhd', attn, v).reshape(B, N, Hd)
            return out
        key = jax.random.key(seed)
        ks = jax.random.split(key, 16)
        B, N, D = (16, 512, 128)
        s = 0.05
        inp = {'nodes_embed': jax.random.normal(ks[0], (B, N, D), jnp.float32), 'node_adj': jax.random.randint(ks[1], (B, N, N), 0, 2, jnp.int32), 'Wq0': jax.random.normal(ks[2], (D, D), jnp.float32) * s, 'bq0': jnp.zeros((D,), jnp.float32), 'Wk0': jax.random.normal(ks[3], (D, D), jnp.float32) * s, 'bk0': jnp.zeros((D,), jnp.float32), 'Wv0': jax.random.normal(ks[4], (D, D), jnp.float32) * s, 'bv0': jnp.zeros((D,), jnp.float32), 'Wq1': jax.random.normal(ks[5], (2 * D, D), jnp.float32) * s, 'bq1': jnp.zeros((D,), jnp.float32), 'Wk1': jax.random.normal(ks[6], (2 * D, D), jnp.float32) * s, 'bk1': jnp.zeros((D,), jnp.float32), 'Wv1': jax.random.normal(ks[7], (2 * D, D), jnp.float32) * s, 'bv1': jnp.zeros((D,), jnp.float32), 'Wout': jax.random.normal(ks[8], (3 * D, D), jnp.float32) * s, 'bout': jnp.zeros((D,), jnp.float32)}
        return inp
    _L3_gnn_all = _L3_gnn_setup()
    _L3_gnn_in = {k: v for k, v in _L3_gnn_all.items() if k in ('Wq0', 'bq0', 'Wk0', 'bk0', 'Wv0', 'bv0', 'Wq1', 'bq1', 'Wk1', 'bk1', 'Wv1', 'bv1', 'Wout', 'bout')}
    del _L3_gnn_all

    def _L3_ffn_setup():
        import jax, jax.numpy as jnp
        import numpy as np
        B, S, D = (8, 2048, 128)
        H = 4 * D
        CAPACITY = 0.5
        key = jax.random.key(seed)
        ks = jax.random.split(key, 6)
        x = jax.random.normal(ks[0], (B, S, D), dtype=jnp.float32)
        attention_mask = jnp.zeros((B, 1, 1, S), dtype=jnp.float32)
        wr = jax.random.normal(ks[1], (D, 1), dtype=jnp.float32) * 0.02
        br = jnp.zeros((1,), dtype=jnp.float32)
        w1 = jax.random.normal(ks[2], (D, H), dtype=jnp.float32) * 0.02
        b1 = jnp.zeros((H,), dtype=jnp.float32)
        w2 = jax.random.normal(ks[3], (H, D), dtype=jnp.float32) * 0.02
        b2 = jnp.zeros((D,), dtype=jnp.float32)
        return {'x': x, 'attention_mask': attention_mask, 'wr': wr, 'br': br, 'w1': w1, 'b1': b1, 'w2': w2, 'b2': b2}
    _L3_ffn_all = _L3_ffn_setup()
    _L3_ffn_in = {k: v for k, v in _L3_ffn_all.items() if k in ('attention_mask', 'wr', 'br', 'w1', 'b1', 'w2', 'b2')}
    del _L3_ffn_all
    return {'x': x, 'adj': adj, 'L0_gnn_weight': _L0_gnn_in['weight'], 'L0_gnn_w_ih': _L0_gnn_in['w_ih'], 'L0_gnn_w_hh': _L0_gnn_in['w_hh'], 'L0_gnn_b_ih': _L0_gnn_in['b_ih'], 'L0_gnn_b_hh': _L0_gnn_in['b_hh'], 'L0_ffn_gamma': _L0_ffn_in['gamma'], 'L0_ffn_beta': _L0_ffn_in['beta'], 'L0_ffn_Wr': _L0_ffn_in['Wr'], 'L0_ffn_br': _L0_ffn_in['br'], 'L0_ffn_W1': _L0_ffn_in['W1'], 'L0_ffn_b1': _L0_ffn_in['b1'], 'L0_ffn_W2': _L0_ffn_in['W2'], 'L0_ffn_b2': _L0_ffn_in['b2'], 'L1_gnn_W': _L1_gnn_in['W'], 'L1_gnn_a': _L1_gnn_in['a'], 'L1_ffn_W_fx': _L1_ffn_in['W_fx'], 'L1_ffn_b_fx': _L1_ffn_in['b_fx'], 'L1_ffn_W_x': _L1_ffn_in['W_x'], 'L1_ffn_b_x': _L1_ffn_in['b_x'], 'L1_ffn_W_slice': _L1_ffn_in['W_slice'], 'L1_ffn_b_slice': _L1_ffn_in['b_slice'], 'L1_ffn_W_q': _L1_ffn_in['W_q'], 'L1_ffn_W_k': _L1_ffn_in['W_k'], 'L1_ffn_W_v': _L1_ffn_in['W_v'], 'L1_ffn_W_out': _L1_ffn_in['W_out'], 'L1_ffn_b_out': _L1_ffn_in['b_out'], 'L1_ffn_temperature': _L1_ffn_in['temperature'], 'L2_gnn_W_msg': _L2_gnn_in['W_msg'], 'L2_gnn_W_upd': _L2_gnn_in['W_upd'], 'L2_gnn_bias': _L2_gnn_in['bias'], 'L2_ffn_W_in': _L2_ffn_in['W_in'], 'L2_ffn_conv_w': _L2_ffn_in['conv_w'], 'L2_ffn_conv_b': _L2_ffn_in['conv_b'], 'L2_ffn_dt_bias': _L2_ffn_in['dt_bias'], 'L2_ffn_A_log': _L2_ffn_in['A_log'], 'L2_ffn_D': _L2_ffn_in['D'], 'L2_ffn_norm_w': _L2_ffn_in['norm_w'], 'L2_ffn_W_out': _L2_ffn_in['W_out'], 'L2_ffn_W_lin': _L2_ffn_in['W_lin'], 'L2_ffn_b_lin': _L2_ffn_in['b_lin'], 'L3_gnn_Wq0': _L3_gnn_in['Wq0'], 'L3_gnn_bq0': _L3_gnn_in['bq0'], 'L3_gnn_Wk0': _L3_gnn_in['Wk0'], 'L3_gnn_bk0': _L3_gnn_in['bk0'], 'L3_gnn_Wv0': _L3_gnn_in['Wv0'], 'L3_gnn_bv0': _L3_gnn_in['bv0'], 'L3_gnn_Wq1': _L3_gnn_in['Wq1'], 'L3_gnn_bq1': _L3_gnn_in['bq1'], 'L3_gnn_Wk1': _L3_gnn_in['Wk1'], 'L3_gnn_bk1': _L3_gnn_in['bk1'], 'L3_gnn_Wv1': _L3_gnn_in['Wv1'], 'L3_gnn_bv1': _L3_gnn_in['bv1'], 'L3_gnn_Wout': _L3_gnn_in['Wout'], 'L3_gnn_bout': _L3_gnn_in['bout'], 'L3_ffn_attention_mask': _L3_ffn_in['attention_mask'], 'L3_ffn_wr': _L3_ffn_in['wr'], 'L3_ffn_br': _L3_ffn_in['br'], 'L3_ffn_w1': _L3_ffn_in['w1'], 'L3_ffn_b1': _L3_ffn_in['b1'], 'L3_ffn_w2': _L3_ffn_in['w2'], 'L3_ffn_b2': _L3_ffn_in['b2']}

def reference(x, adj, L0_gnn_weight, L0_gnn_w_ih, L0_gnn_w_hh, L0_gnn_b_ih, L0_gnn_b_hh, L0_ffn_gamma, L0_ffn_beta, L0_ffn_Wr, L0_ffn_br, L0_ffn_W1, L0_ffn_b1, L0_ffn_W2, L0_ffn_b2, L1_gnn_W, L1_gnn_a, L1_ffn_W_fx, L1_ffn_b_fx, L1_ffn_W_x, L1_ffn_b_x, L1_ffn_W_slice, L1_ffn_b_slice, L1_ffn_W_q, L1_ffn_W_k, L1_ffn_W_v, L1_ffn_W_out, L1_ffn_b_out, L1_ffn_temperature, L2_gnn_W_msg, L2_gnn_W_upd, L2_gnn_bias, L2_ffn_W_in, L2_ffn_conv_w, L2_ffn_conv_b, L2_ffn_dt_bias, L2_ffn_A_log, L2_ffn_D, L2_ffn_norm_w, L2_ffn_W_out, L2_ffn_W_lin, L2_ffn_b_lin, L3_gnn_Wq0, L3_gnn_bq0, L3_gnn_Wk0, L3_gnn_bk0, L3_gnn_Wv0, L3_gnn_bv0, L3_gnn_Wq1, L3_gnn_bq1, L3_gnn_Wk1, L3_gnn_bk1, L3_gnn_Wv1, L3_gnn_bv1, L3_gnn_Wout, L3_gnn_bout, L3_ffn_attention_mask, L3_ffn_wr, L3_ffn_br, L3_ffn_w1, L3_ffn_b1, L3_ffn_w2, L3_ffn_b2):
    import jax
    import jax.numpy as jnp

    def _L0_gnn_ref(x, adj, weight, w_ih, w_hh, b_ih, b_hh):
        import jax, jax.numpy as jnp
        import numpy as np
        OUT = 128
        NUM_LAYERS = 3

        def _gru_cell(inp, h, w_ih, w_hh, b_ih, b_hh):
            gi = inp @ w_ih.T + b_ih
            gh = h @ w_hh.T + b_hh
            i_r, i_z, i_n = jnp.split(gi, 3, axis=-1)
            h_r, h_z, h_n = jnp.split(gh, 3, axis=-1)
            r = jax.nn.sigmoid(i_r + h_r)
            z = jax.nn.sigmoid(i_z + h_z)
            n = jnp.tanh(i_n + r * h_n)
            return (1.0 - z) * n + z * h
        A = (adj != 0).astype(x.dtype)
        h = x
        L = weight.shape[0]
        for i in range(L):
            m = jnp.einsum('bnd,de->bne', h, weight[i])
            aggr = jnp.einsum('bst,bsd->btd', A, m)
            h = _gru_cell(aggr, h, w_ih, w_hh, b_ih, b_hh)
        return h

    def _L0_ffn_ref(x, gamma, beta, Wr, br, W1, b1, W2, b2):
        import jax, jax.numpy as jnp
        import numpy as np
        E = 8
        K = 2
        D = 128
        H = 256
        DOUT = 128
        EPS = 1e-05
        mu = jnp.mean(x, axis=-1, keepdims=True)
        var = jnp.mean(jnp.square(x - mu), axis=-1, keepdims=True)
        xn = (x - mu) * jax.lax.rsqrt(var + EPS) * gamma + beta
        logits = jnp.einsum('bsd,de->bse', xn, Wr) + br
        top_vals, top_idx = jax.lax.top_k(logits, K)
        w = jax.nn.softmax(top_vals, axis=-1)
        w_full = jnp.einsum('bsk,bske->bse', w, jax.nn.one_hot(top_idx, E, dtype=w.dtype))
        y = jnp.zeros(x.shape[:-1] + (DOUT,), x.dtype)
        for e in range(E):
            h = jax.nn.gelu(jnp.einsum('bsd,dh->bsh', xn, W1[e]) + b1[e], approximate=False)
            y_e = jnp.einsum('bsh,hd->bsd', h, W2[e]) + b2[e]
            y = y + y_e * w_full[..., e, None]
        return y

    def _L1_gnn_ref(h, adj, W, a):
        import jax, jax.numpy as jnp
        import numpy as np
        NEG_INF = -1000000000.0
        LEAKY_ALPHA = 0.2
        Wh = jnp.einsum('bnd,de->bne', h, W)
        Dout = Wh.shape[-1]
        a1, a2 = (a[:Dout], a[Dout:])
        f_i = Wh @ a1
        f_j = Wh @ a2
        e = f_i[:, :, None] + f_j[:, None, :]
        e = jax.nn.leaky_relu(e, negative_slope=LEAKY_ALPHA)
        e = jnp.where(adj > 0, e, NEG_INF)
        alpha = jax.nn.softmax(e, axis=-1)
        out = jnp.einsum('bij,bjd->bid', alpha, Wh)
        return jax.nn.elu(out)

    def _L1_ffn_ref(x, W_fx, b_fx, W_x, b_x, W_slice, b_slice, W_q, W_k, W_v, W_out, b_out, temperature):
        import jax, jax.numpy as jnp
        import numpy as np
        DIM = 128
        H = 8
        D = 64
        G = 64
        INNER = H * D
        SCALE = D ** (-0.5)
        B, N, _ = x.shape
        fx_mid = (x @ W_fx + b_fx).reshape(B, N, H, D).transpose(0, 2, 1, 3)
        x_mid = (x @ W_x + b_x).reshape(B, N, H, D).transpose(0, 2, 1, 3)
        temp = jnp.clip(temperature, 0.1, 5.0)
        slice_weights = jax.nn.softmax((x_mid @ W_slice + b_slice) / temp, axis=-1)
        slice_norm = slice_weights.sum(axis=2)
        slice_token = jnp.einsum('bhnc,bhng->bhgc', fx_mid, slice_weights)
        slice_token = slice_token / (slice_norm[..., None] + 1e-05)
        q = slice_token @ W_q
        k = slice_token @ W_k
        v = slice_token @ W_v
        attn = jax.nn.softmax(jnp.einsum('bhgc,bhkc->bhgk', q, k) * SCALE, axis=-1)
        out_slice = jnp.einsum('bhgk,bhkc->bhgc', attn, v)
        out_x = jnp.einsum('bhgc,bhng->bhnc', out_slice, slice_weights)
        out_x = out_x.transpose(0, 2, 1, 3).reshape(B, N, INNER)
        return out_x @ W_out + b_out

    def _L2_gnn_ref(x, adj, W_msg, W_upd, bias):
        import jax, jax.numpy as jnp
        import numpy as np
        a = adj.astype(x.dtype)
        h = jnp.einsum('bnf,fu->bnu', x, W_msg)
        msg_sum = jnp.einsum('bij,biu->bju', a, h)
        deg = jnp.sum(a, axis=1)
        messages = jnp.where(deg[..., None] > 0, msg_sum / jnp.maximum(deg, 1.0)[..., None], 0.0)
        out = jnp.einsum('bnf,fu->bnu', x, W_upd) + messages + bias
        return jax.nn.relu(out)

    def _L2_ffn_ref(x, W_in, conv_w, conv_b, dt_bias, A_log, D, norm_w, W_out, W_lin, b_lin):
        import jax, jax.numpy as jnp
        import numpy as np
        D_MODEL = 128
        D_STATE = 64
        D_CONV = 4
        EXPAND = 2
        HEADDIM = 64
        D_INNER = EXPAND * D_MODEL
        NHEADS = D_INNER // HEADDIM
        CONV_DIM = D_INNER + 2 * D_STATE
        D_IN_PROJ = 2 * D_INNER + 2 * D_STATE + NHEADS
        CHUNK = 128
        EPS = 1e-05

        def segsum(a):
            T = a.shape[-1]
            cs = jnp.cumsum(a, axis=-1)
            ss = cs[..., :, None] - cs[..., None, :]
            mask = jnp.tril(jnp.ones((T, T), dtype=bool))
            return jnp.where(mask, ss, -jnp.inf)

        def mamba2_block(x, W_in, conv_w, conv_b, dt_bias, A_log, D, norm_w, W_out, W_lin, b_lin):
            Bsz, L, _ = x.shape
            zxbcdt = x @ W_in
            z, xBC, dt = jnp.split(zxbcdt, [D_INNER, D_INNER + CONV_DIM], axis=-1)
            xp = jnp.pad(xBC, ((0, 0), (D_CONV - 1, 0), (0, 0)))
            conv = conv_b + sum((xp[:, k:k + L, :] * conv_w[:, k] for k in range(D_CONV)))
            xBC = jax.nn.silu(conv)
            xh, Bmat, Cmat = jnp.split(xBC, [D_INNER, D_INNER + D_STATE], axis=-1)
            dt = jax.nn.softplus(dt + dt_bias)
            A = -jnp.exp(A_log)
            nc = L // CHUNK
            xh = xh.reshape(Bsz, nc, CHUNK, NHEADS, HEADDIM)
            Bc = Bmat.reshape(Bsz, nc, CHUNK, D_STATE)
            Cc = Cmat.reshape(Bsz, nc, CHUNK, D_STATE)
            dtc = dt.reshape(Bsz, nc, CHUNK, NHEADS)
            dA = jnp.einsum('bclh,h->bhcl', dtc, A)
            A_cum = jnp.cumsum(dA, axis=-1)
            Lmat = jnp.exp(segsum(dA))
            xdt = xh * dtc[..., None]
            Y_diag = jnp.einsum('bcln,bcsn,bhcls,bcshp->bclhp', Cc, Bc, Lmat, xdt)
            decay_states = jnp.exp(A_cum[..., -1:] - A_cum)
            states = jnp.einsum('bcln,bhcl,bclhp->bchpn', Bc, decay_states, xdt)
            chunk_decay = jnp.exp(A_cum[..., -1])

            def step(h, inp):
                s, d = inp
                return (h * d[..., None, None] + s, h)
            _, prevs = jax.lax.scan(step, jnp.zeros_like(states[:, 0]), (jnp.moveaxis(states, 1, 0), jnp.moveaxis(chunk_decay, 2, 0)))
            prevs = jnp.moveaxis(prevs, 0, 1)
            Y_off = jnp.einsum('bcln,bchpn,bhcl->bclhp', Cc, prevs, jnp.exp(A_cum))
            Y = (Y_diag + Y_off + xh * D[:, None]).reshape(Bsz, L, D_INNER)
            Y = Y * jax.nn.silu(z)
            Y = Y * jax.lax.rsqrt(jnp.mean(Y * Y, axis=-1, keepdims=True) + EPS) * norm_w
            out = Y @ W_out
            return out @ W_lin + b_lin
        return mamba2_block(x, W_in, conv_w, conv_b, dt_bias, A_log, D, norm_w, W_out, W_lin, b_lin)

    def _L3_gnn_ref(nodes_embed, node_adj, Wq0, bq0, Wk0, bk0, Wv0, bv0, Wq1, bq1, Wk1, bk1, Wv1, bv1, Wout, bout):
        import jax, jax.numpy as jnp
        import numpy as np
        NEG_INF = -1000000000.0
        N_HEADS = 4

        def _graph_mha(x, adj_mask, Wq, bq, Wk, bk, Wv, bv):
            B, N, _ = x.shape
            Hd = Wq.shape[1]
            d = Hd // N_HEADS
            q = (x @ Wq + bq).reshape(B, N, N_HEADS, d)
            k = (x @ Wk + bk).reshape(B, N, N_HEADS, d)
            v = (x @ Wv + bv).reshape(B, N, N_HEADS, d)
            scale = 1.0 / d ** 0.5
            scores = jnp.einsum('bqhd,bkhd->bhqk', q, k) * scale
            scores = jnp.where(adj_mask[:, None, :, :], scores, NEG_INF)
            attn = jax.nn.softmax(scores, axis=-1)
            out = jnp.einsum('bhqk,bkhd->bqhd', attn, v).reshape(B, N, Hd)
            return out
        adj_mask = node_adj > 0
        h0 = _graph_mha(nodes_embed, adj_mask, Wq0, bq0, Wk0, bk0, Wv0, bv0)
        x1 = jnp.concatenate((nodes_embed, h0), axis=-1)
        h1 = _graph_mha(x1, adj_mask, Wq1, bq1, Wk1, bk1, Wv1, bv1)
        x2 = jnp.concatenate((x1, h1), axis=-1)
        out = jax.nn.relu(x2 @ Wout + bout)
        return out

    def _L3_ffn_ref(x, attention_mask, wr, br, w1, b1, w2, b2):
        import jax, jax.numpy as jnp
        import numpy as np
        B, S, D = (8, 2048, 128)
        H = 4 * D
        CAPACITY = 0.5
        b, s, d = x.shape
        weights = (jnp.einsum('bsd,do->bso', x, wr) + br)[..., 0]
        k = max(1, int(CAPACITY * s))
        kk = k - 1 if k > 1 else 1
        _, idx = jax.lax.top_k(weights, k)
        sel_idx = idx[:, :kk]
        sel = jnp.take_along_axis(x, sel_idx[:, :, None], axis=1)
        h = jax.nn.gelu(jnp.einsum('bkd,dh->bkh', sel, w1) + b1)
        y = jnp.einsum('bkh,hd->bkd', h, w2) + b2
        w_sel = jnp.take_along_axis(weights, sel_idx, axis=1)
        y = y * w_sel[..., None]
        batch_idx = jnp.arange(b)[:, None]
        processed = jnp.zeros_like(x).at[batch_idx, sel_idx].set(y)
        return processed + x
    x = x + _L0_gnn_ref(_layernorm(x, axis=-1), adj, L0_gnn_weight, L0_gnn_w_ih, L0_gnn_w_hh, L0_gnn_b_ih, L0_gnn_b_hh)
    x = x + _L0_ffn_ref(_layernorm(x, axis=-1), L0_ffn_gamma, L0_ffn_beta, L0_ffn_Wr, L0_ffn_br, L0_ffn_W1, L0_ffn_b1, L0_ffn_W2, L0_ffn_b2)
    x = x + _L1_gnn_ref(_layernorm(x, axis=-1), adj, L1_gnn_W, L1_gnn_a)
    x = x + _L1_ffn_ref(_layernorm(x, axis=-1), L1_ffn_W_fx, L1_ffn_b_fx, L1_ffn_W_x, L1_ffn_b_x, L1_ffn_W_slice, L1_ffn_b_slice, L1_ffn_W_q, L1_ffn_W_k, L1_ffn_W_v, L1_ffn_W_out, L1_ffn_b_out, L1_ffn_temperature)
    x = x + _L2_gnn_ref(_layernorm(x, axis=-1), adj, L2_gnn_W_msg, L2_gnn_W_upd, L2_gnn_bias)
    x = x + _L2_ffn_ref(_layernorm(x, axis=-1), L2_ffn_W_in, L2_ffn_conv_w, L2_ffn_conv_b, L2_ffn_dt_bias, L2_ffn_A_log, L2_ffn_D, L2_ffn_norm_w, L2_ffn_W_out, L2_ffn_W_lin, L2_ffn_b_lin)
    x = x + _L3_gnn_ref(_layernorm(x, axis=-1), adj, L3_gnn_Wq0, L3_gnn_bq0, L3_gnn_Wk0, L3_gnn_bk0, L3_gnn_Wv0, L3_gnn_bv0, L3_gnn_Wq1, L3_gnn_bq1, L3_gnn_Wk1, L3_gnn_bk1, L3_gnn_Wv1, L3_gnn_bv1, L3_gnn_Wout, L3_gnn_bout)
    x = x + _L3_ffn_ref(_layernorm(x, axis=-1), L3_ffn_attention_mask, L3_ffn_wr, L3_ffn_br, L3_ffn_w1, L3_ffn_b1, L3_ffn_w2, L3_ffn_b2)
    return x

_drawn_inputs = setup_inputs


def setup_inputs(seed=0):
    import zlib

    import numpy as np

    out = dict(_drawn_inputs(seed))
    spreads = {'L0_ffn_br': (0.0, 0.1),
     'L1_ffn_b_fx': (0.0, 0.1),
     'L1_ffn_b_x': (0.0, 0.8),
     'L1_ffn_b_slice': (0.0, 0.8),
     'L1_ffn_b_out': (0.0, 0.1),
     'L1_ffn_temperature': (0.5, 0.6),
     'L2_gnn_bias': (0.0, 0.1),
     'L2_ffn_D': (1.0, 0.2),
     'L2_ffn_norm_w': (1.0, 0.2),
     'L2_ffn_b_lin': (0.0, 0.1),
     'L3_gnn_bq0': (0.0, 0.8),
     'L3_gnn_bk0': (0.0, 0.8),
     'L3_gnn_bv0': (0.0, 0.345),
     'L3_gnn_bq1': (0.0, 0.8),
     'L3_gnn_bk1': (0.0, 0.8),
     'L3_gnn_bv1': (0.0, 0.401),
     'L3_gnn_bout': (0.0, 0.1),
     'L3_ffn_b1': (0.0, 0.8),
     'L3_ffn_b2': (0.0, 0.8)}
    factors = {'L0_ffn_gamma': 8.0,
     'L0_ffn_beta': 8.0,
     'L0_ffn_Wr': 3.532,
     'L0_ffn_b1': 8.0,
     'L0_ffn_b2': 3.103,
     'L1_ffn_W_x': 3.975,
     'L1_ffn_W_slice': 5.362,
     'L1_ffn_W_q': 8.0,
     'L1_ffn_W_k': 8.0,
     'L2_ffn_A_log': 8.0,
     'L3_gnn_Wq0': 5.894,
     'L3_gnn_Wk0': 5.791,
     'L3_gnn_Wq1': 5.707,
     'L3_gnn_Wk1': 5.689,
     'L3_ffn_wr': 8.0,
     'L3_ffn_w1': 8.0,
     'L3_ffn_w2': 8.0}
    for name, (base, spread) in spreads.items():
        noise = np.random.default_rng([zlib.crc32(name.encode()), seed]).standard_normal(out[name].shape)
        drawn = base * np.exp(spread * noise) if base else spread * noise
        out[name] = jnp.asarray(drawn.astype(out[name].dtype))
    for name, factor in factors.items():
        out[name] = (out[name] * factor).astype(out[name].dtype)
    return out
```

```python
from contextlib import ExitStack

import concourse.bass as bass
import numpy as np
from concourse import mybir

F32 = mybir.dt.float32
BF16 = mybir.dt.bfloat16
I32 = mybir.dt.int32
ALU = mybir.AluOpType
ACT = mybir.ActivationFunctionType
AX = mybir.AxisListType.X

P = 128
LANES = 2
D = 128
N = 512
T = N // P
EPS = 1e-5
GNN0_STEPS = 3
EXPERTS, EXPERT_H = 8, 256
SH, SG, SD = 8, 64, 64
PAIRS = SH // 2
MH, MD, MS = 4, 64, 64
MI = MH * MD
TAPS = 4
AH, AD = 4, 32
FH = 512
KEPT = N // 2 - 1
BIG = 2.0 ** 60
SCRATCH = 9216

WEIGHTS = [
    ("ident", P, P), ("tri", P, P), ("lower", P, P), ("ones", P, 1), ("before", P, 64), ("own_head", P, PAIRS * SH),
    ("g0_w", P, GNN0_STEPS * D), ("g0_wih", P, 3 * D), ("g0_whh", P, 3 * D), ("g0_bih", P, 3), ("g0_bhh", P, 3),
    ("f0_gamma", P, 1), ("f0_beta", P, 1), ("f0_wr", P, EXPERTS), ("f0_br", P, EXPERTS),
    ("f0_w1", P, EXPERTS * EXPERT_H), ("f0_b1", P, EXPERTS * 2), ("f0_w2", P, EXPERTS * 2 * D), ("f0_b2", EXPERTS, D),
    ("g1_w", P, D),
    ("f1_wfx", P, SH * SD), ("f1_bfx", SH, SD), ("f1_bout", P, D),
    ("g2_wmsg", P, D), ("g2_wupd", P, D), ("g2_bias", P, D),
    ("f2_win", P, 2 * MI + 2 * MS + MH), ("f2_convw", P, 3 * TAPS), ("f2_convb", P, 3), ("f2_dtb", P, MH),
    ("f2_d", P, 2), ("f2_blin", P, D),
    ("g3_wk0", P, D), ("g3_wv0", P, D), ("g3_wk1", P, 2 * D), ("g3_wv1", P, 2 * D),
    ("g3_bk0", P, 1), ("g3_bk1", P, 1), ("g3_bv0", P, D), ("g3_bv1", P, D), ("g3_wout", P, 3 * D), ("g3_bout", P, D),
    ("f3_wr", P, 1), ("f3_br", P, 1), ("f3_w1", P, FH), ("f3_b1", P, FH // P), ("f3_w2", P, FH), ("f3_b2", P, D),
]
RAW = [
    ("g1_wT", P, D), ("g1_a", P, 2),
    ("f1_wxT", SD, SH * D), ("f1_wslice", SD, SG), ("f1_bx", SD, SH), ("f1_bslice", P, SG), ("f1_temp", P, SH),
    ("f1_wqT", SD, SD), ("f1_wkT", SD, SD), ("f1_wvT", SD, SD), ("f1_wout", SD, SH * D),
    ("f2_woutT", P, MI), ("f2_wlin", P, D), ("f2_normw", P, 2), ("f2_alog", P, MH),
    ("g3_wq0", P, D), ("g3_wq1", P, 2 * D), ("g3_bq0", P, 1), ("g3_bq1", P, 1),
]
MADE = [
    ("g0_brz", 2), ("g1_wa", 2), ("g1_wa2", P), ("f1_ws", SH * SG), ("f1_bs", SH * SG), ("f1_wqk", SD),
    ("f1_wvo", SH * D), ("f2_wol", 2 * D), ("f2_nega", MH), ("g3_wq0", D), ("g3_wq1", 2 * D), ("g3_bq0", 1), ("g3_bq1", 1),
    ("f1_rtemp", SH),
]


def columns_of(table):
    at, out = 0, {}
    for entry in table:
        out[entry[0]] = (at, entry[-1])
        at += entry[-1]
    return out, at


class Steps:

    def __init__(self, eng, sem):
        self.eng, self.sem, self.n = eng, sem, 0

    def __call__(self, ins):
        self.n += 1
        ins.then_inc(self.sem, 1)

    def wait(self):
        self.eng.wait_ge(self.sem, self.n)


def nth(k, b):
    return LANES * k + b + 1


def build(nc, x, adj, weights, raw, out):
    graphs = x.shape[0]
    x_rows = x.rearrange("g (t p) d -> g p t d", p=P)
    adj_rows = adj.rearrange("g (t p) n -> g p t n", p=P)
    out_rows = out.rearrange("g (t p) d -> g p t d", p=P)
    w_at, w_cols = columns_of(WEIGHTS)
    raw_at, raw_cols = columns_of(RAW)
    made_at, made_cols = columns_of(MADE)
    assert raw_cols <= SCRATCH

    ctx = ExitStack()
    with ctx:
        def sb(name, shape, dt=F32):
            return ctx.enter_context(nc.sbuf_tensor(name, shape, dt))

        def sem(name):
            return ctx.enter_context(nc.semaphore(name))

        weights_sb = sb("weights_sb", [P, w_cols])
        made_sb = sb("made_sb", [P, made_cols])
        ident_big = sb("ident_big", [P, P], BF16)
        minus_half = sb("minus_half", [P, T])
        X = [sb(f"x{b}", [P, T, D]) for b in range(LANES)]
        XN = [sb(f"xn{b}", [P, T, 132]) for b in range(LANES)]
        XT = [sb(f"xT{b}", [P, N]) for b in range(LANES)]
        ADJ = [sb(f"adj{b}", [P, T, N], I32) for b in range(LANES)]
        AF = [sb(f"adjf{b}", [P, T, N]) for b in range(LANES)]
        NM = [sb(f"nomask{b}", [P, T, N], BF16) for b in range(LANES)]
        stats = [sb(f"stats{b}", [P, T, 6]) for b in range(LANES)]
        mv = [sb(f"mv{b}", [P, T, 2]) for b in range(LANES)]
        ve = [sb(f"ve{b}", [P, T]) for b in range(LANES)]
        rstd = [sb(f"rstd{b}", [P, T]) for b in range(LANES)]
        SC = [sb(f"scratch{b}", [P, SCRATCH]) for b in range(LANES)]
        PS = [[ctx.enter_context(nc.psum_tensor(f"ps{b}_{i}", [P, 512], F32)) for i in range(4)] for b in range(LANES)]

        def W(name, rows=P):
            a, n = w_at[name]
            return weights_sb[0:rows, a:a + n]

        def R(name, rows=P):
            a, n = raw_at[name]
            return SC[0][0:rows, a:a + n]

        def M(name, rows=P):
            a, n = made_at[name]
            return made_sb[0:rows, a:a + n]

        def cut(b, at, n, rows=P):
            return SC[b][0:rows, at:at + n]

        def ps(b, i, n=512, rows=P, at=0):
            return PS[b][i][0:rows, at:at + n]

        def tile(t, n=P):
            return slice(t * n, (t + 1) * n)

        def spread(ap, axis, shape):
            return ap.unsqueeze(axis).to_broadcast(shape)

        ident = W("ident")

        G0_M, G0_AG, G0_R, G0_Z, G0_U = (512 * k for k in range(5))
        F0_HID, F0_LG, F0_GT, F0_EQ, F0_RK, F0_SEL, F0_LS, F0_S, F0_TH, F0_GATE, F0_GATET = (
            0, 1024, 1088, 1344, 1600, 1632, 1664, 1696, 1704, 1736, 1792)
        G1_WH, G1_F, G1_Z, G1_U, G1_P, G1_PT, G1_MX, G1_SUM, G1_RI, G1_POS, G1_NEG = (
            0, 512, 1024, 2048, 3072, 4096, 6144, 6148, 6152, 6160, 6672)
        F1_SW, F1_SWT, F1_MX, F1_SUM, F1_RI, F1_SN, F1_DEN, F1_RD, F1_RAT, F1_RM, F1_ST, F1_RR, F1_TK, F1_QP, F1_TV = (
            0, 2048, 4096, 4128, 4160, 4192, 4704, 4708, 4712, 4716, 4748, 5260, 5772, 6284, 6796)
        F1_E, F1_EMX, F1_ES, F1_ER, F1_ET, F1_U = 7820, 8076, 8080, 8084, 8088, 8600
        G2_UP, G2_DEG, G2_RD, G2_POS, G2_C, G2_O = 0, 512, 516, 520, 524, 528
        PAD = TAPS - 1
        CW = N + PAD + 1
        F2_CIN, F2_XS, F2_CC, F2_Z, F2_XD, F2_BB, F2_GM, F2_MT, F2_CE, F2_XDD, F2_PV, F2_S = (
            0, 1548, 3084, 3596, 4620, 5644, 6156, 6668, 7180, 7436, 7692, 7948)
        F2_DD, F2_RE, F2_E, F2_YG, F2_SQ = 0, 512, 1024, 0, 4620
        G3_QZ, G3_K, G3_V, G3_P, G3_PT, G3_H, G3_MX, G3_SUM, G3_RI = 0, 2048, 2560, 3072, 5120, 7168, 8192, 8224, 8256
        G3_RING = 4
        G3_O = 3072
        F3_HID, F3_W, F3_CMP, F3_CNT, F3_SC, F3_Y = 0, 2048, 2056, 4616, 4640, 4650
        lanes = range(LANES)

        loaded, prep_pe, prep_dve, prep_act = sem("weights_loaded"), sem("prep_pe"), sem("prep_dve"), sem("prep_act")
        with nc.Block() as block:
            @block.sync
            def _(sp):
                sp.dma_start(SC[0][:, 0:raw_cols], raw).then_inc(loaded, 16)
                sp.dma_start(weights_sb[:, :], weights).then_inc(loaded, 16)

            @block.tensor
            def _(pe):
                pe.wait_ge(loaded, 32)
                pe.matmul(ps(0, 0, 2), R("g1_wT"), R("g1_a"), start=True, stop=True)
                pe.matmul(ps(0, 0, SD, SD, 64), R("f1_wqT", SD), R("f1_wkT", SD), start=True, stop=True)
                for k in range(2):
                    pe.matmul(ps(0, 3, D, P, k * D), R("f2_woutT")[:, tile(k)], R("f2_wlin"), start=True, stop=True)
                for h in range(SH):
                    pe.matmul(ps(0, 1, SG, P, h * SG), R("f1_wxT", SD)[:, tile(h)], R("f1_wslice", SD), start=True, stop=True)
                    pe.matmul(ps(0, 2, SG, P, h * SG), R("f1_bx", SD)[:, h:h + 1].to_broadcast([SD, P]),
                              R("f1_wslice", SD), start=True, stop=True)
                    last = pe.matmul(ps(1, h // 4, D, SD, (h % 4) * D), R("f1_wvT", SD), R("f1_wout", SD)[:, tile(h)],
                                     start=True, stop=True)
                last.then_inc(prep_pe, 1)

            @block.vector
            def _(v):
                v.memset(minus_half[:, :], -0.5)
                for b in lanes:
                    v.memset(XN[b][:, :, D:132], 1.0)
                v.wait_ge(loaded, 32)
                v.tensor_scalar(ident_big[:, :], ident, BIG, None, ALU.mult)
                v.tensor_tensor(M("g0_brz"), W("g0_bih")[:, 0:2], W("g0_bhh")[:, 0:2], ALU.add)
                v.tensor_scalar(M("f1_rtemp"), R("f1_temp"), 0.1, 5.0, ALU.max, ALU.min).then_inc(prep_dve, 1)
                v.wait_ge(prep_dve, 1)
                v.reciprocal(M("f1_rtemp"), M("f1_rtemp")).then_inc(prep_dve, 1)
                for q in ("g3_wq0", "g3_wq1", "g3_bq0", "g3_bq1"):
                    v.tensor_scalar(M(q), R(q), AD ** -0.5, None, ALU.mult)
                v.wait_ge(prep_pe, 1)
                v.tensor_copy(M("g1_wa"), ps(0, 0, 2))
                v.tensor_copy(M("g1_wa2"), ps(0, 0, 1, P, 1).to_broadcast([P, P]))
                v.tensor_scalar(M("f1_wqk", SD), ps(0, 0, SD, SD, 64), SD ** -0.5, None, ALU.mult)
                for k in range(2):
                    v.tensor_scalar(M("f2_wol")[:, tile(k)], ps(0, 3, D, P, k * D), R("f2_normw")[:, k:k + 1], None, ALU.mult)
                    v.tensor_copy(M("f1_wvo", SD)[:, tile(k, 512)], ps(1, k, 512, SD))
                v.wait_ge(prep_dve, 2)
                rtemp = spread(M("f1_rtemp"), 2, [P, SH, SG])
                v.tensor_tensor(M("f1_ws").rearrange("p (h g) -> p h g", h=SH), ps(0, 1).rearrange("p (h g) -> p h g", h=SH),
                                rtemp, ALU.mult)
                bs = M("f1_bs").rearrange("p (h g) -> p h g", h=SH)
                v.tensor_tensor(bs, ps(0, 2).rearrange("p (h g) -> p h g", h=SH), spread(R("f1_bslice"), 1, [P, SH, SG]),
                                ALU.add).then_inc(prep_dve, 1)
                v.wait_ge(prep_dve, 3)
                v.tensor_tensor(bs, bs, rtemp, ALU.mult)
                v.wait_ge(prep_act, 1)
                v.tensor_scalar(M("f2_nega"), M("f2_nega"), -1.0, None, ALU.mult)

            @block.scalar
            def _(act):
                act.wait_ge(loaded, 32)
                act.activation(M("f2_nega"), R("f2_alog"), ACT.Exp).then_inc(prep_act, 1)

        names = [
            "x_loaded0", "x_loaded1", "adj_loaded0", "adj_loaded1",
            "v_step", "g_step", "a_step",
            "x_new", "var_ready0", "var_ready1", "rstd_ready0", "rstd_ready1", "xn_ready", "xT_psum", "xT_ready", "masks_ready", "stored",
            "m_psum", "m_ready", "aggr_psum", "aggr_ready", "rz_psum", "n_psum", "r_ready", "z_ready", "u_ready", "n_ready",
            "h_ready", "h_back",
            "logit_psum", "half_gap", "gate_tanh", "gate_ready", "gT_psum", "gT_ready", "b2_psum", "b2_added", "hid_psum", "hid_ready", "y_psum", "combined",
            "wh_psum", "wh_ready", "f_ready", "z1_psum", "z1_ready", "u1_ready", "p1_ready", "p1T_psum", "p1T_ready",
            "o1_psum", "o1_neg", "elu_exp",
            "sl_psum", "sl_biased", "sl_shifted", "sl_exp", "sl_rsum", "sw_ready", "swT_psum", "swT_ready", "tok_psum",
            "sn_ready", "sT_psum", "sT_ready", "ratio_psum", "ratio_ready", "tk_psum", "tk_ready", "qp_psum", "qp_ready",
            "tv_ready", "sc_psum", "sc_shifted", "sc_exp", "sc_sum", "eT_psum", "eT_ready", "u_psum", "us_ready", "so_psum", "bout_added",
            "adjf_ready", "h2_psum", "h2_ready", "upd_psum", "msg_psum",
            "xbc_psum", "dt_psum", "dt_v", "dt_e", "dt_u", "dt_ln", "xbc_ready", "zg_psum", "zg_ready", "conv_ready", "silu_ready", "cc_ready0", "cc_ready1",
            "da_ready", "ac_psum", "ac_ready", "xs_T", "xd_ready", "gt_psum", "gm_ready", "row_psum", "dd_ready", "re_ready", "e_ready",
            "mt_ready", "st_psum", "pv_ready", "yt_psum", "yg_ready", "sq_ready", "ym_psum", "ms_ready", "rs_ready", "blin_added",
            "qkv_psum", "q_ready", "kv_ready", "qz_zero", "att_psum", "att_max", "att_exp", "att_rsum", "att_p", "pT_psum", "pT_even", "pT_odd",
            "pv_psum", "h3_ready", "g3_psum",
            "w3_psum", "w3_ready", "row3_psum", "scale3_ready", "hid3_psum", "hid3_ready", "y3_psum", "xn_added",
        ]
        s = {name: sem(name) for name in names}
        first_sem, last_sem = s[names[0]].num, s[names[-1]].num
        assert last_sem - first_sem == len(names) - 1

        def turned(eng, b, layer, n):
            eng.wait_ge(s["pT_odd" if n % 2 else "pT_even"], nth((layer * T * AH + n) // 2, b))

        G0, F0, G1, F1, G2, F2, G3, F3 = range(8)
        LN_OF = {G0: 0, F0: 2, G1: 3, F1: 4, G2: 5, F2: 6, G3: 7, F3: 8}

        with nc.Fori(0, graphs // LANES) as i:
            with nc.Block() as block:
                @block.sync
                def _(sp):
                    for b in lanes:
                        g = bass.ds(i * LANES + b, 1)
                        sp.dma_start(X[b][:, :, :], x_rows[g].rearrange("a p t d -> (a p) t d")).then_inc(s[f"x_loaded{b}"], 16)
                    for b in lanes:
                        g = bass.ds(i * LANES + b, 1)
                        sp.dma_start(ADJ[b][:, :, :], adj_rows[g].rearrange("a p t n -> (a p) t n")).then_inc(s[f"adj_loaded{b}"], 16)
                    for b in lanes:
                        c_rows = SC[b][MS:P, F2_XS + 2 * N:F2_XS + 3 * N]
                        sp.wait_ge(s["silu_ready"], nth(0, b))
                        sp.dma_start(cut(b, F2_CC, N, MS), c_rows).then_inc(s[f"cc_ready{b}"], 16)
                        sp.dma_start(SC[b][MS:P, F2_CC:F2_CC + N], c_rows).then_inc(s[f"cc_ready{b}"], 16)
                    for b in lanes:
                        g = bass.ds(i * LANES + b, 1)
                        sp.wait_ge(s["x_new"], nth(8 - 1, b))
                        sp.dma_start(out_rows[g].rearrange("a p t d -> (a p) t d"), X[b][:, :, :]).then_inc(s["stored"], 16)
                    sp.wait_ge(s["stored"], 16 * LANES)

                @block.tensor
                def _(pe):
                    def mm(o, lhsT, rhs, start=True, stop=True, **k):
                        return pe.matmul(o, lhsT, rhs, start=start, stop=stop, **k)

                    def to_columns(b, k):
                        pe.wait_ge(s["xn_ready"], nth(k, b))
                        for t in range(T):
                            last = pe.transpose(ps(b, 0, P, P, t * P), XN[b][:, t, 0:D], ident)
                        last.then_inc(s["xT_psum"], 1)

                    def g0_messages(b, k):
                        if k == 0:
                            pe.wait_ge(s["xT_ready"], nth(G0, b))
                        else:
                            pe.wait_ge(s["h_ready"], nth(k - 1, b))
                        h = XT[b]
                        for t in range(T):
                            last = mm(ps(b, 1, D, P, t * D), h[:, tile(t)], W("g0_w")[:, tile(k)])
                        last.then_inc(s["m_psum"], 1)
                        for gate in range(2):
                            mm(ps(b, 2 + gate), W("g0_whh")[:, tile(gate)], h[:, :], stop=False)
                        mm(ps(b, 0), W("g0_whh")[:, tile(2)], h[:, :])
                        pe.wait_ge(s["m_ready"], nth(k, b))
                        if k == 0:
                            pe.wait_ge(s["masks_ready"], b + 1)
                        for t in range(T):
                            last = mm(ps(b, 1), cut(b, G0_M, N)[:, tile(t)], AF[b][:, t, :], start=t == 0, stop=t == T - 1)
                        last.then_inc(s["aggr_psum"], 1)

                    def g0_gates(b, k):
                        pe.wait_ge(s["aggr_ready"], nth(k, b))
                        ag = cut(b, G0_AG, N)
                        for gate in range(2):
                            last = mm(ps(b, 2 + gate), W("g0_wih")[:, tile(gate)], ag, start=False)
                        last.then_inc(s["rz_psum"], 1)
                        mm(ps(b, 1), W("g0_wih")[:, tile(2)], ag).then_inc(s["n_psum"], 1)

                    def g0_back(b):
                        pe.wait_ge(s["h_ready"], nth(GNN0_STEPS - 1, b))
                        for t in range(T):
                            last = pe.transpose(ps(b, 0, P, P, t * P), XT[b][:, tile(t)], ident)
                        last.then_inc(s["h_back"], 1)

                    def f0_logits(b):
                        to_columns(b, F0)
                        pe.wait_ge(s["xT_ready"], nth(F0, b))
                        for t in range(T):
                            last = mm(ps(b, 3, EXPERTS, P, t * EXPERTS), XT[b][:, tile(t)], W("f0_wr"))
                        last.then_inc(s["logit_psum"], 1)

                    def f0_bias(b):
                        pe.wait_ge(s["gate_ready"], b + 1)
                        gate = cut(b, F0_GATE, T * EXPERTS)
                        for t in range(T):
                            last = pe.transpose(ps(b, 3, P, EXPERTS, t * P), gate[:, tile(t, EXPERTS)], ident)
                        last.then_inc(s["gT_psum"], 1)
                        pe.wait_ge(s["gT_ready"], b + 1)
                        for t in range(T):
                            last = mm(ps(b, 2, D, P, t * D), cut(b, F0_GATET, N, EXPERTS)[:, tile(t)], W("f0_b2", EXPERTS))
                        last.then_inc(s["b2_psum"], 1)

                    def f0_hidden(b, e):
                        if e:
                            pe.wait_ge(s["hid_ready"], nth(e - 1, b))
                        for k in range(2):
                            last = mm(ps(b, k), W("f0_w1")[:, tile(2 * e + k)], XT[b][:, :])
                        last.then_inc(s["hid_psum"], 1)

                    def f0_out(b, e):
                        pe.wait_ge(s["hid_ready"], nth(e, b))
                        if e == 1:
                            pe.wait_ge(s["b2_added"], b + 1)
                        if e >= 2:
                            pe.wait_ge(s["combined"], nth(e - 2, b))
                        for t in range(T):
                            for k in range(2):
                                last = mm(ps(b, 3 - e % 2, D, P, t * D), cut(b, F0_HID + k * N, N)[:, tile(t)],
                                          W("f0_w2")[:, tile(2 * e + k)], start=k == 0, stop=k == 1)
                        last.then_inc(s["y_psum"], 1)

                    def g1_project(b):
                        to_columns(b, G1)
                        pe.wait_ge(s["xT_ready"], nth(G1, b))
                        for t in range(T):
                            mm(ps(b, 1, D, P, t * D), XT[b][:, tile(t)], W("g1_w"))
                            last = mm(ps(b, 2, 2, P, 2 * t), XT[b][:, tile(t)], M("g1_wa"))
                        last.then_inc(s["wh_psum"], 1)

                    def g1_scores(b, t):
                        if t == 0:
                            pe.wait_ge(s["wh_ready"], b + 1)
                            pe.wait_ge(s["f_ready"], b + 1)
                        if t >= 2:
                            pe.wait_ge(s["z1_ready"], nth(t - 2, b))
                        mm(ps(b, t % 2), M("g1_wa2"), XT[b][:, :], stop=False)
                        mm(ps(b, t % 2), ident_big[:, :], NM[b][:, t, :], start=False).then_inc(s["z1_psum"], 1)

                    def g1_turn(b, t):
                        pe.wait_ge(s["p1_ready"], nth(t, b))
                        if t >= 2:
                            pe.wait_ge(s["p1T_ready"], nth(t - 2, b))
                        for j in range(T):
                            last = pe.transpose(ps(b, 2 + t % 2, P, P, j * P), cut(b, G1_P + t % 2 * N, N)[:, tile(j)], ident)
                        last.then_inc(s["p1T_psum"], 1)

                    def g1_out(b):
                        pe.wait_ge(s["p1T_ready"], nth(T - 1, b))
                        for t in range(T):
                            for j in range(T):
                                last = mm(ps(b, 0, D, P, t * D), cut(b, G1_PT + j * N, N)[:, tile(t)],
                                          cut(b, G1_WH, N)[:, tile(j)], start=j == 0, stop=j == T - 1)
                        last.then_inc(s["o1_psum"], 1)

                    def f1_logits(b, t):
                        if t == 0:
                            to_columns(b, F1)
                            pe.wait_ge(s["xT_ready"], nth(F1, b))
                        if t >= 2:
                            pe.wait_ge(s["sl_biased"], nth(t - 2, b))
                        mm(ps(b, t % 2), XT[b][:, tile(t)], M("f1_ws")).then_inc(s["sl_psum"], 1)

                    def f1_turn(b, t):
                        pe.wait_ge(s["sw_ready"], nth(t, b))
                        if t >= 2:
                            pe.wait_ge(s["swT_ready"], nth(t - 2, b))
                        for k in range(PAIRS):
                            last = pe.transpose(ps(b, 2 + t % 2, P, P, k * P), cut(b, F1_SW + t * N, N)[:, tile(k)], ident)
                        last.then_inc(s["swT_psum"], 1)

                    def f1_tokens(b):
                        pe.wait_ge(s["sl_biased"], nth(T - 1, b))
                        for k in range(PAIRS):
                            for t in range(T):
                                last = mm(ps(b, k // 2, D + 1, P, k % 2 * 256), cut(b, F1_SW + t * N, N)[:, tile(k)],
                                          XN[b][:, t, 0:D + 1], start=t == 0, stop=t == T - 1)
                        last.then_inc(s["tok_psum"], 1)

                    def f1_project(b):
                        pe.wait_ge(s["sn_ready"], b + 1)
                        pe.wait_ge(s["swT_ready"], nth(T - 1, b))
                        for k in range(PAIRS):
                            last = pe.transpose(ps(b, 2, P, P, k * P), cut(b, F1_SN, N)[:, tile(k)], ident)
                        last.then_inc(s["sT_psum"], 1)
                        for k in range(PAIRS):
                            last = mm(ps(b, 3, P, SH, k * P), cut(b, F1_RM, PAIRS * SH)[:, tile(k, SH)], ident)
                        last.then_inc(s["ratio_psum"], 1)
                        pe.wait_ge(s["ratio_ready"], b + 1)
                        pe.wait_ge(s["sT_ready"], b + 1)
                        mm(ps(b, 0, N, SD), W("f1_bfx", SH), cut(b, F1_RR, N, SH), stop=False)
                        for h in range(SH):
                            last = mm(ps(b, 0, SG, SD, h * SG), W("f1_wfx")[:, tile(h, SD)], cut(b, F1_ST, N)[:, tile(h, SG)],
                                      start=False, stop=h == SH - 1)
                        last.then_inc(s["tk_psum"], 1)

                    def f1_attend(b):
                        pe.wait_ge(s["tk_ready"], b + 1)
                        tk = cut(b, F1_TK, N, SD)
                        mm(ps(b, 1, N, SD), M("f1_wqk", SD), tk).then_inc(s["qp_psum"], 1)
                        for h in range(SH):
                            last = mm(ps(b, 2 + h // 4, D, SD, h % 4 * D), tk[:, tile(h, SG)], M("f1_wvo", SD)[:, tile(h)])
                        last.then_inc(s["tok_psum"], 1)
                        pe.wait_ge(s["qp_ready"], b + 1)
                        for h in range(SH):
                            half = SG * (h % 2)
                            last = mm(PS[b][0][half:half + SG, h // 2 * SG:(h // 2 + 1) * SG], cut(b, F1_QP, N, SD)[:, tile(h, SG)],
                                      tk[:, tile(h, SG)], tile_position=(0, half))
                        last.then_inc(s["sc_psum"], 1)

                    def f1_mix(b):
                        pe.wait_ge(s["sc_exp"], b + 1)
                        for k in range(PAIRS):
                            last = pe.transpose(ps(b, 1, P, SG, k * P), cut(b, F1_E, PAIRS * SG)[:, tile(k, SG)], ident)
                        last.then_inc(s["eT_psum"], 1)
                        pe.wait_ge(s["eT_ready"], b + 1)
                        pe.wait_ge(s["tv_ready"], b + 1)
                        for h in range(SH):
                            half = SG * (h % 2)
                            last = mm(PS[b][0][half:half + SG, tile(h // 2)], cut(b, F1_ET, N, SG)[:, tile(h, SG)],
                                      cut(b, F1_TV, SH * D, SG)[:, tile(h)], tile_position=(0, half))
                        last.then_inc(s["u_psum"], 1)

                    def f1_out(b):
                        pe.wait_ge(s["us_ready"], b + 1)
                        for t in range(T):
                            for k in range(PAIRS):
                                last = mm(ps(b, 1, D, P, t * D), cut(b, F1_SWT + k * N, N)[:, tile(t)],
                                          cut(b, F1_U, N)[:, tile(k)], start=k == 0, stop=k == PAIRS - 1)
                        last.then_inc(s["so_psum"], 1)

                    def g2_project(b):
                        to_columns(b, G2)
                        pe.wait_ge(s["xT_ready"], nth(G2, b))
                        for t in range(T):
                            last = mm(ps(b, 1, D, P, t * D), XT[b][:, tile(t)], W("g2_wmsg"))
                        last.then_inc(s["h2_psum"], 1)
                        for t in range(T):
                            last = mm(ps(b, 2, D, P, t * D), XT[b][:, tile(t)], W("g2_wupd"))
                        last.then_inc(s["upd_psum"], 1)

                    def g2_messages(b):
                        pe.wait_ge(s["h2_ready"], b + 1)
                        pe.wait_ge(s["adjf_ready"], b + 1)
                        for j in range(T):
                            for t in range(T):
                                last = mm(ps(b, 3 * (j // 2), D + 1, P, j % 2 * 256), AF[b][:, t, tile(j)],
                                          XN[b][:, t, 0:D + 1], start=t == 0, stop=t == T - 1)
                        last.then_inc(s["msg_psum"], 1)

                    def f2_project(b):
                        to_columns(b, F2)
                        pe.wait_ge(s["xT_ready"], nth(F2, b))
                        for k in range(3):
                            mm(ps(b, 1 + k), W("f2_win")[:, tile(2 + k)], XT[b][:, :]).then_inc(s["xbc_psum"], 1)
                        for t in range(T):
                            last = mm(ps(b, 0, MH, P, t * MH), XT[b][:, tile(t)], W("f2_win")[:, 2 * MI + 2 * MS:])
                        last.then_inc(s["dt_psum"], 1)

                    def f2_gate(b):
                        pe.wait_ge(s["xbc_ready"], b + 1)
                        for k in range(2):
                            last = mm(ps(b, 1 + k), W("f2_win")[:, tile(k)], XT[b][:, :])
                        last.then_inc(s["zg_psum"], 1)

                    def f2_cumulate(b):
                        pe.wait_ge(s["da_ready"], b + 1)
                        mm(ps(b, 0, T * MH), W("tri"), cut(b, F2_S + 8 * 16, T * MH)).then_inc(s["ac_psum"], 1)

                    def f2_turn(b):
                        pe.wait_ge(s["zg_ready"], b + 1)
                        pe.wait_ge(s["silu_ready"], nth(0, b))
                        for k in range(3):
                            for c in range(T):
                                last = pe.transpose(ps(b, 1 + k, P, P, c * P), cut(b, F2_XS + k * N, N)[:, tile(c)], ident)
                        last.then_inc(s["xs_T"], 1)
                        pe.wait_ge(s[f"cc_ready{b}"], 32)
                        pe.wait_ge(s["ac_ready"], b + 1)
                        for c in range(T):
                            last = mm(ps(b, 0, P, P, c * P), cut(b, F2_XS + 2 * N, N, MS)[:, tile(c)], cut(b, F2_CC, N, MS)[:, tile(c)])
                        last.then_inc(s["gt_psum"], 1)

                    def f2_rows(b, c):
                        if c == 0:
                            pe.wait_ge(s["xd_ready"], b + 1)
                        else:
                            pe.wait_ge(s["dd_ready"], nth(c - 1, b))
                            pe.wait_ge(s["re_ready"], nth(c - 1, b))
                        for h in range(MH):
                            a = F2_S + 9 * 16 + c * MH + h
                            last = pe.transpose(ps(b, 1, P, P, h * P), SC[b][:, a:a + 1].to_broadcast([P, P]), ident)
                        last.then_inc(s["row_psum"], 1)

                    def f2_chunk(b, c):
                        pe.wait_ge(s["mt_ready"], nth(c, b))
                        if c == 0:
                            pe.wait_ge(s["gm_ready"], b + 1)
                        else:
                            pe.wait_ge(s["pv_ready"], nth(c - 1, b))
                        for k in range(2):
                            last = mm(ps(b, 0, P, P, k * P), cut(b, F2_BB, N)[:, tile(c)], cut(b, F2_XDD, MI)[:, tile(k)])
                        last.then_inc(s["st_psum"], 1)
                        for k in range(2):
                            mm(ps(b, 2 + k, P, P, c * P), cut(b, F2_PV, MI)[:, tile(k)], cut(b, F2_CE, MI)[:, tile(k)], stop=False)
                            for q in range(2):
                                h = 2 * k + q
                                last = mm(PS[b][2 + k][q * MD:(q + 1) * MD, tile(c)], cut(b, F2_XD, T * MI)[:, tile(c * MH + h, MD)],
                                          cut(b, F2_MT, MH * P)[:, tile(h)], start=False, tile_position=(0, q * MD))
                        last.then_inc(s["yt_psum"], 1)

                    def f2_out(b):
                        pe.wait_ge(s["yg_ready"], b + 1)
                        pe.wait_ge(s["pv_ready"], nth(T - 1, b))
                        for t in range(T):
                            for k in range(2):
                                last = mm(ps(b, 0, D, P, t * D), cut(b, F2_YG + k * N, N)[:, tile(t)], M("f2_wol")[:, tile(k)],
                                          start=k == 0, stop=k == 1)
                        pe.wait_ge(s["sq_ready"], b + 1)
                        for t in range(T):
                            for k in range(2):
                                last = mm(ps(b, 1, 1, P, t), cut(b, F2_SQ + k * N, N)[:, tile(t)], W("ones"), start=k == 0, stop=k == 1)
                        last.then_inc(s["ym_psum"], 1)

                    def g3_project(b, layer):
                        if layer == 0:
                            to_columns(b, G3)
                            pe.wait_ge(s["xT_ready"], nth(G3, b))
                            ins = [XT[b][:, :]]
                        else:
                            pe.wait_ge(s["h3_ready"], nth(0, b))
                            turned(pe, b, 0, T * AH - 1)
                            ins = [XT[b][:, :], cut(b, G3_H, N)]
                        wq, wk, wv = M(f"g3_wq{layer}"), W(f"g3_wk{layer}"), W(f"g3_wv{layer}")
                        for bank, w in ((1, wq), (2, wk)):
                            for n, a in enumerate(ins):
                                mm(ps(b, bank), w[:, tile(n)], a, start=n == 0, stop=n == layer)
                        for t in range(T):
                            for n, a in enumerate(ins):
                                last = mm(ps(b, 3, D, P, t * D), a[:, tile(t)], wv[:, tile(n)], start=n == 0, stop=n == layer)
                        last.then_inc(s["qkv_psum"], 1)

                    def g3_scores(b, layer, n):
                        q, h = divmod(n, AH)
                        k = layer * T * AH + n
                        if n == 0:
                            pe.wait_ge(s["q_ready"], nth(layer, b))
                            pe.wait_ge(s["kv_ready"], nth(layer, b))
                        if n >= 2:
                            pe.wait_ge(s["att_exp"], nth(k - 2, b))
                        mm(ps(b, n % 2), cut(b, G3_QZ + h * N, N)[:, tile(q)], cut(b, G3_K, N), stop=False)
                        mm(ps(b, n % 2), ident_big[:, :], NM[b][:, q, :], start=False).then_inc(s["att_psum"], 1)

                    def g3_turn(b, layer, n):
                        k = layer * T * AH + n
                        pe.wait_ge(s["att_p"], nth(k, b))
                        if n >= 1:
                            turned(pe, b, layer, n - 1)
                        for j in range(T):
                            last = pe.transpose(ps(b, 2, P, P, j * P), cut(b, G3_P + n % G3_RING * N, N)[:, tile(j)], ident)
                        last.then_inc(s["pT_psum"], 1)

                    def g3_values(b, layer, q):
                        turned(pe, b, layer, AH * q + AH - 2)
                        turned(pe, b, layer, AH * q + AH - 1)
                        pt = cut(b, G3_PT, T * AH * P)
                        for j in range(T):
                            for h in range(AH):
                                last = mm(PS[b][3][h * AD:(h + 1) * AD, tile(q)], cut(b, G3_V + j * D, D)[:, tile(h, AD)],
                                          pt[:, tile(j * AH + h)], start=j == 0, stop=j == T - 1, tile_position=(0, h * AD))
                        last.then_inc(s["pv_psum"], 1)

                    def g3_out(b):
                        pe.wait_ge(s["h3_ready"], nth(1, b))
                        ins = [XT[b][:, :], cut(b, G3_H, N), cut(b, G3_H + N, N)]
                        for t in range(T):
                            for n, a in enumerate(ins):
                                last = mm(ps(b, 0, D, P, t * D), a[:, tile(t)], W("g3_wout")[:, tile(n)], start=n == 0, stop=n == 2)
                        last.then_inc(s["g3_psum"], 1)

                    def f3_router(b):
                        to_columns(b, F3)
                        pe.wait_ge(s["xT_ready"], nth(F3, b))
                        for t in range(T):
                            last = mm(ps(b, 3, 1, P, t), XT[b][:, tile(t)], W("f3_wr"))
                        last.then_inc(s["w3_psum"], 1)

                    def f3_hidden(b, k):
                        if k >= 2:
                            pe.wait_ge(s["hid3_ready"], nth(k - 2, b))
                        mm(ps(b, k % 2), W("f3_w1")[:, tile(k)], XT[b][:, :]).then_inc(s["hid3_psum"], 1)

                    def f3_rank(b):
                        pe.wait_ge(s["w3_ready"], b + 1)
                        for t in range(T):
                            last = pe.transpose(ps(b, 2, P, P, t * P), cut(b, F3_W + t, 1).to_broadcast([P, P]), ident)
                        last.then_inc(s["row3_psum"], 1)

                    def f3_out(b):
                        pe.wait_ge(s["hid3_ready"], nth(3, b))
                        for t in range(T):
                            for k in range(FH // P):
                                last = mm(ps(b, 3, D, P, t * D), cut(b, F3_HID + k * N, N)[:, tile(t)], W("f3_w2")[:, tile(k)],
                                          start=k == 0, stop=k == FH // P - 1)
                        last.then_inc(s["y3_psum"], 1)

                    def turns(f, *args):
                        for b in lanes:
                            f(b, *args)

                    turns(to_columns, G0)
                    for k in range(GNN0_STEPS):
                        turns(g0_messages, k)
                        turns(g0_gates, k)
                    turns(g0_back)
                    turns(f0_logits)
                    turns(f0_hidden, 0)
                    turns(f0_bias)
                    for e in range(EXPERTS):
                        turns(f0_out, e)
                        if e + 1 < EXPERTS:
                            turns(f0_hidden, e + 1)
                    turns(g1_project)
                    for t in range(T + 2):
                        if t < T:
                            turns(g1_scores, t)
                        if t >= 2:
                            turns(g1_turn, t - 2)
                    turns(g1_out)
                    for t in range(T + 2):
                        if t < T:
                            turns(f1_logits, t)
                        if t >= 2:
                            turns(f1_turn, t - 2)
                    turns(f1_tokens)
                    turns(f1_project)
                    turns(f1_attend)
                    turns(f1_mix)
                    turns(f1_out)
                    turns(g2_project)
                    turns(g2_messages)
                    turns(f2_project)
                    turns(f2_gate)
                    turns(f2_cumulate)
                    turns(f2_turn)
                    for c in range(T):
                        turns(f2_rows, c)
                        turns(f2_chunk, c)
                    turns(f2_out)
                    for layer in range(2):
                        turns(g3_project, layer)
                        for n in range(T * AH + 3):
                            for b in lanes:
                                if n < T * AH:
                                    g3_scores(b, layer, n)
                                if 2 <= n < T * AH + 2:
                                    g3_turn(b, layer, n - 2)
                                if n >= 3 and (n - 3) % AH == AH - 1:
                                    g3_values(b, layer, (n - 3) // AH)
                    turns(g3_out)
                    turns(f3_router)
                    for k in range(FH // P):
                        turns(f3_hidden, k)
                        if k == 1:
                            turns(f3_rank)
                    turns(f3_out)

                @block.scalar
                def _(act):
                    own = Steps(act, s["a_step"])

                    def f(o, a, func, **k):
                        return act.activation(o, a, func, **k)

                    def columns_out(b, k):
                        act.wait_ge(s["xT_psum"], nth(k, b))
                        if k == F0:
                            f(XT[b][:, :], ps(b, 0), ACT.Identity, scale=W("f0_gamma"), bias=W("f0_beta")).then_inc(s["xT_ready"], 1)
                        else:
                            f(XT[b][:, :], ps(b, 0), ACT.Copy).then_inc(s["xT_ready"], 1)

                    def g0_messages(b, k):
                        act.wait_ge(s["m_psum"], nth(k, b))
                        f(cut(b, G0_M, N), ps(b, 1), ACT.Copy).then_inc(s["m_ready"], 1)

                    def g0_gates(b, k):
                        act.wait_ge(s["rz_psum"], nth(k, b))
                        f(cut(b, G0_R, N), ps(b, 2), ACT.Sigmoid, bias=M("g0_brz")[:, 0:1]).then_inc(s["r_ready"], 1)
                        f(cut(b, G0_Z, N), ps(b, 3), ACT.Sigmoid, bias=M("g0_brz")[:, 1:2]).then_inc(s["z_ready"], 1)
                        act.wait_ge(s["u_ready"], nth(k, b))
                        f(cut(b, G0_U, N), cut(b, G0_U, N), ACT.Tanh, bias=W("g0_bih")[:, 2:3]).then_inc(s["n_ready"], 1)

                    def f0_hidden(b, e):
                        act.wait_ge(s["hid_psum"], nth(e, b))
                        if e:
                            act.wait_ge(s["y_psum"], nth(e - 1, b))
                        for k in range(2):
                            last = f(cut(b, F0_HID + k * N, N), ps(b, k), ACT.Gelu, bias=W("f0_b1")[:, 2 * e + k:2 * e + k + 1])
                        last.then_inc(s["hid_ready"], 1)

                    def f0_tanh(b):
                        act.wait_ge(s["half_gap"], b + 1)
                        th = cut(b, F0_TH, T * EXPERTS)
                        f(th, th, ACT.Tanh).then_inc(s["gate_tanh"], 1)

                    def g1_project(b):
                        act.wait_ge(s["wh_psum"], b + 1)
                        f(cut(b, G1_WH, N), ps(b, 1), ACT.Copy).then_inc(s["wh_ready"], 1)

                    def g1_scores(b, t):
                        act.wait_ge(s["z1_psum"], nth(t, b))
                        if t == 0:
                            act.wait_ge(s["f_ready"], b + 1)
                        if t >= 2:
                            act.wait_ge(s["u1_ready"], nth(t - 2, b))
                        f(cut(b, G1_Z + t % 2 * N, N), ps(b, t % 2), ACT.Identity, bias=cut(b, G1_F + 2 * t, 1)).then_inc(s["z1_ready"], 1)

                    def g1_exp(b, t):
                        act.wait_ge(s["u1_ready"], nth(t, b))
                        if t >= 2:
                            act.wait_ge(s["p1T_psum"], nth(t - 2, b))
                        f(cut(b, G1_P + t % 2 * N, N), cut(b, G1_U + t % 2 * N, N), ACT.Exp, bias=cut(b, G1_MX + t, 1),
                          accum_out=cut(b, G1_SUM + t, 1)).then_inc(s["p1_ready"], 1)

                    def g1_turned(b, t):
                        act.wait_ge(s["p1T_psum"], nth(t, b))
                        pt = cut(b, G1_PT, T * N).rearrange("p (j n) -> p j n", j=T)
                        f(pt[:, :, tile(t)], ps(b, 2 + t % 2).rearrange("p (j n) -> p j n", j=T), ACT.Copy).then_inc(s["p1T_ready"], 1)

                    def g1_elu(b):
                        act.wait_ge(s["o1_neg"], b + 1)
                        f(cut(b, G1_NEG, N), cut(b, G1_NEG, N), ACT.Exp).then_inc(s["elu_exp"], 1)

                    def f1_exp(b, t):
                        act.wait_ge(s["sl_shifted"], nth(t, b))
                        sw = cut(b, F1_SW + t * N, N)
                        f(sw, sw, ACT.Exp).then_inc(s["sl_exp"], 1)

                    def f1_turned(b, t):
                        act.wait_ge(s["swT_psum"], nth(t, b))
                        swt = cut(b, F1_SWT, T * N).rearrange("p (k n) -> p k n", k=PAIRS)
                        f(swt[:, :, tile(t)], ps(b, 2 + t % 2).rearrange("p (k n) -> p k n", k=PAIRS), ACT.Copy).then_inc(s["swT_ready"], 1)

                    def f1_project(b):
                        act.wait_ge(s["sT_psum"], b + 1)
                        f(cut(b, F1_ST, N), ps(b, 2), ACT.Copy).then_inc(s["sT_ready"], 1)

                    def f1_attend(b):
                        act.wait_ge(s["qp_psum"], b + 1)
                        f(cut(b, F1_QP, N, SD), ps(b, 1, N, SD), ACT.Copy).then_inc(s["qp_ready"], 1)
                        act.wait_ge(s["tok_psum"], nth(1, b))
                        f(cut(b, F1_TV, N, SG), ps(b, 2, N, SG), ACT.Copy)
                        f(cut(b, F1_TV + N, N, SG), ps(b, 3, N, SG), ACT.Copy).then_inc(s["tv_ready"], 1)
                        act.wait_ge(s["sc_shifted"], b + 1)
                        e = cut(b, F1_E, PAIRS * SG)
                        f(e, e, ACT.Exp).then_inc(s["sc_exp"], 1)

                    def g2_project(b):
                        act.wait_ge(s["h2_psum"], b + 1)
                        f(XN[b][:, :, 0:D], ps(b, 1).rearrange("p (t d) -> p t d", t=T), ACT.Copy).then_inc(s["h2_ready"], 1)

                    def f2_project(b):
                        for k in range(3):
                            act.wait_ge(s["xbc_psum"], 3 * b + k + 1)
                            last = f(cut(b, F2_CIN + k * CW + PAD, N), ps(b, 1 + k), ACT.Copy)
                        last.then_inc(s["xbc_ready"], 1)

                    def f2_gate(b):
                        act.wait_ge(s["zg_psum"], b + 1)
                        for k in range(2):
                            last = f(cut(b, F2_Z + k * N, N), ps(b, 1 + k), ACT.Silu)
                        last.then_inc(s["zg_ready"], 1)

                    def f2_silu(b):
                        for k in range(3):
                            act.wait_ge(s["conv_ready"], 3 * b + k + 1)
                            xs = cut(b, F2_XS + k * N, N)
                            last = f(xs, xs, ACT.Silu, bias=W("f2_convb")[:, k:k + 1])
                        last.then_inc(s["silu_ready"], 1)

                    def f2_softplus(b):
                        act.wait_ge(s["dt_v"], b + 1)
                        f(cut(b, F2_S + 16, 16), cut(b, F2_S + 16, 16), ACT.Exp).then_inc(s["dt_e"], 1)
                        act.wait_ge(s["dt_u"], b + 1)
                        f(cut(b, F2_S + 3 * 16, 16), cut(b, F2_S + 2 * 16, 16), ACT.Ln).then_inc(s["dt_ln"], 1)

                    def f2_rows(b, c):
                        act.wait_ge(s["row_psum"], nth(c, b))
                        if c:
                            act.wait_ge(s["pv_ready"], nth(c - 1, b))
                        f(cut(b, F2_RE, N), ps(b, 1), ACT.Exp).then_inc(s["re_ready"], 1)
                        act.wait_ge(s["dd_ready"], nth(c, b))
                        f(cut(b, F2_E, N), cut(b, F2_DD, N), ACT.Exp).then_inc(s["e_ready"], 1)

                    def f2_square(b):
                        act.wait_ge(s["yg_ready"], b + 1)
                        f(cut(b, F2_SQ, 2 * N), cut(b, F2_YG, 2 * N), ACT.Square).then_inc(s["sq_ready"], 1)

                    def g3_project(b, layer):
                        act.wait_ge(s["qkv_psum"], nth(layer, b))
                        if layer == 0:
                            act.wait_ge(s["qz_zero"], b + 1)
                        for h in range(AH):
                            rows = slice(h * AD, (h + 1) * AD)
                            a = G3_QZ + h * N
                            last = f(SC[b][rows, a:a + N], PS[b][1][rows, :], ACT.Identity, bias=M(f"g3_bq{layer}")[rows, :])
                        last.then_inc(s["q_ready"], 1)

                    def g3_exp(b, layer, n):
                        k = layer * T * AH + n
                        act.wait_ge(s["att_max"], nth(k, b))
                        if k >= G3_RING:
                            act.wait_ge(s["pT_psum"], nth(k - G3_RING, b))
                        f(cut(b, G3_P + n % G3_RING * N, N), ps(b, n % 2), ACT.Exp, bias=cut(b, G3_MX + n, 1),
                          accum_out=cut(b, G3_SUM + n, 1)).then_inc(s["att_exp"], 1)

                    def g3_turned(b, layer, n):
                        k = layer * T * AH + n
                        act.wait_ge(s["pT_psum"], nth(k, b))
                        pt = cut(b, G3_PT, T * AH * P).rearrange("p (j h n) -> p j h n", j=T, h=AH)
                        f(pt[:, :, n % AH, :], ps(b, 2).rearrange("p (j n) -> p j n", j=T), ACT.Copy).then_inc(s["pT_odd"], 1)

                    def g3_gather(b, layer):
                        act.wait_ge(s["pv_psum"], nth(layer * T + T - 1, b))
                        f(cut(b, G3_H + layer * N, N), ps(b, 3), ACT.Copy).then_inc(s["h3_ready"], 1)

                    def f3_hidden(b, k):
                        act.wait_ge(s["hid3_psum"], nth(k, b))
                        f(cut(b, F3_HID + k * N, N), ps(b, k % 2), ACT.Gelu_apprx_tanh, bias=W("f3_b1")[:, k:k + 1]).then_inc(s["hid3_ready"], 1)

                    def turns(g, *args):
                        for b in lanes:
                            g(b, *args)

                    turns(columns_out, G0)
                    for k in range(GNN0_STEPS):
                        turns(g0_messages, k)
                        turns(g0_gates, k)
                    turns(columns_out, F0)
                    turns(f0_hidden, 0)
                    turns(f0_tanh)
                    for e in range(1, EXPERTS):
                        turns(f0_hidden, e)
                    turns(columns_out, G1)
                    turns(g1_project)
                    for t in range(T + 2):
                        if t < T:
                            turns(g1_scores, t)
                        if 1 <= t <= T:
                            turns(g1_exp, t - 1)
                        if t >= 2:
                            turns(g1_turned, t - 2)
                    turns(g1_elu)
                    turns(columns_out, F1)
                    for t in range(T + 1):
                        if t < T:
                            turns(f1_exp, t)
                        if t >= 1:
                            turns(f1_turned, t - 1)
                    turns(f1_project)
                    turns(f1_attend)
                    turns(columns_out, G2)
                    turns(g2_project)
                    turns(columns_out, F2)
                    turns(f2_project)
                    turns(f2_gate)
                    turns(f2_silu)
                    turns(f2_softplus)
                    for c in range(T):
                        turns(f2_rows, c)
                    turns(f2_square)
                    turns(columns_out, G3)
                    for layer in range(2):
                        turns(g3_project, layer)
                        for n in range(T * AH + 2):
                            for b in lanes:
                                if n < T * AH:
                                    g3_exp(b, layer, n)
                                if n >= 2 and n % 2:
                                    g3_turned(b, layer, n - 2)
                        turns(g3_gather, layer)
                    turns(columns_out, F3)
                    for k in range(FH // P):
                        turns(f3_hidden, k)

                @block.vector
                def _(v):
                    own = Steps(v, s["v_step"])

                    def tt(o, a, c, op):
                        return v.tensor_tensor(o, a, c, op)

                    def ts(o, a, s1, op0, s2=None, op1=ALU.bypass, **k):
                        return v.tensor_scalar(o, a, s1, s2, op0, op1, **k)

                    def stt(o, a, s1, c, op0, op1, **k):
                        return v.scalar_tensor_tensor(out=o, in0=a, scalar=s1, in1=c, op0=op0, op1=op1, **k)

                    def tiles(ap, n=T):
                        return ap.rearrange("p (t d) -> p t d", t=n)

                    def layernorm(b, n, src, column):
                        for t in range(T):
                            last = v.bn_stats(stats[b][:, t, :], src[:, t, 0:D])
                        own(last)
                        own.wait()
                        for t in range(T):
                            last = v.bn_aggr(mv[b][:, t, :], stats[b][:, t, :])
                        own(last)
                        own.wait()
                        ts(ve[b][:, :], mv[b][:, :, 1], EPS, ALU.add).then_inc(s[f"var_ready{b}"], 1)
                        v.wait_ge(s[f"rstd_ready{b}"], n + 1)
                        for t in range(T):
                            last = ts(XN[b][:, t, 0:D], src[:, t, 0:D], mv[b][:, t, 0:1], ALU.subtract, rstd[b][:, t:t + 1], ALU.mult)
                        if column is None:
                            own(last)
                        else:
                            last.then_inc(s["xn_ready"], 1)

                    def new_x(b, k, ins):
                        ins.then_inc(s["x_new"], 1)
                        v.wait_ge(s["x_new"], nth(k, b))

                    def g0_start(b):
                        v.wait_ge(s[f"x_loaded{b}"], 16)
                        layernorm(b, 0, X[b], G0)

                    def g0_masks(b):
                        v.wait_ge(s[f"adj_loaded{b}"], 16)
                        ts(AF[b][:, :, :], ADJ[b][:, :, :], 0, ALU.not_equal)
                        ts(NM[b][:, :, :], ADJ[b][:, :, :], 0, ALU.is_gt, 1.0, ALU.subtract).then_inc(s["masks_ready"], 1)

                    def g0_messages(b, k):
                        v.wait_ge(s["aggr_psum"], nth(k, b))
                        v.tensor_copy(cut(b, G0_AG, N), ps(b, 1)).then_inc(s["aggr_ready"], 1)

                    def g0_gates(b, k):
                        h, r, z, u = XT[b][:, :], cut(b, G0_R, N), cut(b, G0_Z, N), cut(b, G0_U, N)
                        v.wait_ge(s["r_ready"], nth(k, b))
                        v.wait_ge(s["n_psum"], nth(k, b))
                        own(stt(u, ps(b, 0), W("g0_bhh")[:, 2:3], r, ALU.add, ALU.mult))
                        own.wait()
                        tt(u, u, ps(b, 1), ALU.add).then_inc(s["u_ready"], 1)
                        v.wait_ge(s["n_ready"], nth(k, b))
                        own(tt(r, h, u, ALU.subtract))
                        own.wait()
                        own(tt(r, r, z, ALU.mult))
                        own.wait()
                        tt(h, u, r, ALU.add).then_inc(s["h_ready"], 1)

                    def g0_end(b):
                        v.wait_ge(s["h_back"], b + 1)
                        new_x(b, 0, tt(X[b][:, :, :], X[b][:, :, :], tiles(ps(b, 0)), ALU.add))

                    def f0_start(b):
                        layernorm(b, 1, X[b], None)
                        own.wait()
                        layernorm(b, 2, XN[b], F0)

                    def f0_gate(b):
                        te = T * EXPERTS
                        lg, sel, ls, th = cut(b, F0_LG, te), cut(b, F0_SEL, te), cut(b, F0_LS, te), cut(b, F0_TH, te)
                        gt, eq, rk, sm, gate = cut(b, F0_GT, 256), cut(b, F0_EQ, 256), cut(b, F0_RK, te), cut(b, F0_S, T), cut(b, F0_GATE, te)
                        full = [P, T, EXPERTS, EXPERTS]
                        v.wait_ge(s["logit_psum"], b + 1)
                        own(tt(tiles(lg), tiles(ps(b, 3, te)), spread(W("f0_br"), 1, [P, T, EXPERTS]), ALU.add))
                        own.wait()
                        rivals, mine = spread(tiles(lg), 2, full), spread(tiles(lg), 3, full)
                        g4, e4 = (a.rearrange("p (t e f) -> p t e f", t=T, e=EXPERTS) for a in (gt, eq))
                        tt(g4, rivals, mine, ALU.is_gt)
                        own(tt(e4, rivals, mine, ALU.is_equal))
                        own.wait()
                        before = spread(W("before"), 1, [P, T, EXPERTS * EXPERTS])
                        own(tt(tiles(eq), tiles(eq), before, ALU.mult))
                        own.wait()
                        own(tt(gt, gt, eq, ALU.add))
                        own.wait()
                        own(v.tensor_reduce(tiles(rk), g4, AX, ALU.add))
                        own.wait()
                        own(ts(sel, rk, 1.5, ALU.is_lt))
                        own.wait()
                        own(tt(ls, lg, sel, ALU.mult))
                        own.wait()
                        own(v.tensor_reduce(sm, tiles(ls), AX, ALU.add))
                        own.wait()
                        stt(tiles(th), spread(sm, 2, [P, T, EXPERTS]), -0.5, tiles(lg), ALU.mult, ALU.add).then_inc(s["half_gap"], 1)

                    def f0_gate_end(b):
                        te = T * EXPERTS
                        sel, th, gate = cut(b, F0_SEL, te), cut(b, F0_TH, te), cut(b, F0_GATE, te)
                        v.wait_ge(s["gate_tanh"], b + 1)
                        own(ts(th, th, 0.5, ALU.mult, 0.5, ALU.add))
                        own.wait()
                        tt(gate, th, sel, ALU.mult).then_inc(s["gate_ready"], 1)

                    def f0_bias(b):
                        v.wait_ge(s["gT_psum"], b + 1)
                        v.tensor_copy(cut(b, F0_GATET, N, EXPERTS), ps(b, 3, N, EXPERTS)).then_inc(s["gT_ready"], 1)
                        v.wait_ge(s["b2_psum"], b + 1)
                        tt(X[b][:, :, :], X[b][:, :, :], tiles(ps(b, 2)), ALU.add).then_inc(s["b2_added"], 1)

                    def f0_combine(b, e):
                        v.wait_ge(s["y_psum"], nth(e, b))
                        if e == 0:
                            v.wait_ge(s["gate_ready"], b + 1)
                            v.wait_ge(s["b2_added"], b + 1)
                        else:
                            v.wait_ge(s["combined"], nth(e - 1, b))
                        for t in range(T):
                            x = X[b][:, t, :]
                            last = stt(x, ps(b, 3 - e % 2, D, P, t * D), cut(b, F0_GATE + t * EXPERTS + e, 1), x, ALU.mult, ALU.add)
                        if e < EXPERTS - 1:
                            last.then_inc(s["combined"], 1)
                        else:
                            new_x(b, 1, last)

                    def g1_project(b):
                        v.wait_ge(s["wh_psum"], b + 1)
                        v.tensor_copy(cut(b, G1_F, 2 * T), ps(b, 2, 2 * T)).then_inc(s["f_ready"], 1)

                    def g1_scores(b, t):
                        z, u = cut(b, G1_Z + t % 2 * N, N), cut(b, G1_U + t % 2 * N, N)
                        v.wait_ge(s["z1_ready"], nth(t, b))
                        if t >= 2:
                            v.wait_ge(s["p1_ready"], nth(t - 2, b))
                        own(stt(u, z, 0.2, z, ALU.mult, ALU.max))
                        own.wait()
                        v.tensor_reduce(cut(b, G1_MX + t, 1), u, AX, ALU.max, negate=True).then_inc(s["u1_ready"], 1)

                    def g1_end(b):
                        ri = cut(b, G1_RI, T)
                        v.wait_ge(s["p1_ready"], nth(T - 1, b))
                        own(v.reciprocal(ri, cut(b, G1_SUM, T)))
                        own.wait()
                        v.wait_ge(s["o1_psum"], b + 1)
                        for t in range(T):
                            ts(cut(b, G1_POS + t * D, D), ps(b, 0, D, P, t * D), ri[:, t:t + 1], ALU.mult, 0.0, ALU.max)
                        for t in range(T):
                            last = ts(cut(b, G1_NEG + t * D, D), ps(b, 0, D, P, t * D), ri[:, t:t + 1], ALU.mult, 0.0, ALU.min)
                        last.then_inc(s["o1_neg"], 1)
                        v.wait_ge(s["o1_neg"], b + 1)
                        own(tt(X[b][:, :, :], X[b][:, :, :], tiles(cut(b, G1_POS, N)), ALU.add))
                        own.wait()
                        v.wait_ge(s["elu_exp"], b + 1)
                        new_x(b, 2, stt(X[b][:, :, :], tiles(cut(b, G1_NEG, N)), -1.0, X[b][:, :, :], ALU.add, ALU.add))

                    def heads(ap):
                        return ap.rearrange("p (h g) -> p h g", g=SG)

                    def f1_logits(b, t):
                        sw, mx = cut(b, F1_SW + t * N, N), cut(b, F1_MX + t * SH, SH)
                        v.wait_ge(s["sl_psum"], nth(t, b))
                        tt(sw, ps(b, t % 2), M("f1_bs"), ALU.add).then_inc(s["sl_biased"], 1)
                        v.wait_ge(s["sl_biased"], nth(t, b))
                        own(v.tensor_reduce(mx, heads(sw), AX, ALU.max))
                        own.wait()
                        tt(heads(sw), heads(sw), spread(mx, 2, [P, SH, SG]), ALU.subtract).then_inc(s["sl_shifted"], 1)

                    def f1_sums(b, t):
                        sw, sm, ri = cut(b, F1_SW + t * N, N), cut(b, F1_SUM + t * SH, SH), cut(b, F1_RI + t * SH, SH)
                        v.wait_ge(s["sl_exp"], nth(t, b))
                        own(v.tensor_reduce(sm, heads(sw), AX, ALU.add))
                        own.wait()
                        v.reciprocal(ri, sm).then_inc(s["sl_rsum"], 1)

                    def f1_tokens(b):
                        den, rd, rat = cut(b, F1_DEN, PAIRS), cut(b, F1_RD, PAIRS), cut(b, F1_RAT, PAIRS)
                        v.wait_ge(s["tok_psum"], nth(0, b))
                        for k in range(PAIRS):
                            last = ts(den[:, k:k + 1], ps(b, k // 2, 1, P, k % 2 * 256 + D), 1e-5, ALU.add)
                        own(last)
                        own.wait()
                        own(v.reciprocal(rd, den))
                        own.wait()
                        for k in range(PAIRS):
                            ts(cut(b, F1_SN + k * D, D), ps(b, k // 2, D, P, k % 2 * 256), rd[:, k:k + 1], ALU.mult)
                            last = ts(rat[:, k:k + 1], ps(b, k // 2, 1, P, k % 2 * 256 + D), rd[:, k:k + 1], ALU.mult)
                        own(last)
                        own.wait()
                        rm = cut(b, F1_RM, PAIRS * SH).rearrange("p (k h) -> p k h", h=SH)
                        tt(rm, W("own_head").rearrange("p (k h) -> p k h", h=SH), spread(rat, 2, [P, PAIRS, SH]), ALU.mult)\
                            .then_inc(s["sn_ready"], 1)

                    def f1_project(b):
                        v.wait_ge(s["ratio_psum"], b + 1)
                        v.tensor_copy(cut(b, F1_RR, N, SH), ps(b, 3, N, SH)).then_inc(s["ratio_ready"], 1)
                        v.wait_ge(s["tk_psum"], b + 1)
                        v.tensor_copy(cut(b, F1_TK, N, SD), ps(b, 0, N, SD)).then_inc(s["tk_ready"], 1)

                    def f1_attend(b):
                        mx, e = cut(b, F1_EMX, PAIRS), cut(b, F1_E, PAIRS * SG)
                        v.wait_ge(s["sc_psum"], b + 1)
                        own(v.tensor_reduce(mx, heads(ps(b, 0, PAIRS * SG)), AX, ALU.max))
                        own.wait()
                        tt(heads(e), heads(ps(b, 0, PAIRS * SG)), spread(mx, 2, [P, PAIRS, SG]), ALU.subtract).then_inc(s["sc_shifted"], 1)

                    def f1_mix(b):
                        e, es, er = cut(b, F1_E, PAIRS * SG), cut(b, F1_ES, PAIRS), cut(b, F1_ER, PAIRS)
                        v.wait_ge(s["sc_exp"], b + 1)
                        own(v.tensor_reduce(es, heads(e), AX, ALU.add))
                        own.wait()
                        own(v.reciprocal(er, es))
                        v.wait_ge(s["eT_psum"], b + 1)
                        v.tensor_copy(cut(b, F1_ET, N, SG), ps(b, 1, N, SG)).then_inc(s["eT_ready"], 1)
                        own.wait()
                        v.wait_ge(s["u_psum"], b + 1)
                        tt(tiles(cut(b, F1_U, N), PAIRS), tiles(ps(b, 0), PAIRS), spread(er, 2, [P, PAIRS, D]), ALU.mult).then_inc(s["us_ready"], 1)

                    def f1_end(b):
                        v.wait_ge(s["so_psum"], b + 1)
                        v.wait_ge(s["bout_added"], b + 1)
                        new_x(b, 3, tt(X[b][:, :, :], X[b][:, :, :], tiles(ps(b, 1)), ALU.add))

                    def g2_end(b):
                        up, o = cut(b, G2_UP, N), cut(b, G2_O, N)
                        rd, pos, c = cut(b, G2_RD, T), cut(b, G2_POS, T), cut(b, G2_C, T)
                        v.wait_ge(s["upd_psum"], b + 1)
                        own(tt(tiles(up), tiles(ps(b, 2)), spread(W("g2_bias"), 1, [P, T, D]), ALU.add))
                        v.wait_ge(s["msg_psum"], b + 1)
                        for j in range(T):
                            deg = ps(b, 3 * (j // 2), 1, P, j % 2 * 256 + D)
                            ts(rd[:, j:j + 1], deg, 1.0, ALU.max)
                            last = ts(pos[:, j:j + 1], deg, 0.0, ALU.is_gt)
                        own(last)
                        own.wait()
                        own(v.reciprocal(rd, rd))
                        own.wait()
                        own(tt(c, rd, pos, ALU.mult))
                        own.wait()
                        for j in range(T):
                            last = stt(o[:, tile(j)], ps(b, 3 * (j // 2), D, P, j % 2 * 256), c[:, j:j + 1], up[:, tile(j)], ALU.mult, ALU.add)
                        own(last)
                        own.wait()
                        new_x(b, 4, stt(X[b][:, :, :], tiles(o), 0.0, X[b][:, :, :], ALU.max, ALU.add))

                    def small(b, k):
                        return cut(b, F2_S + 16 * k, 16)

                    def f2_conv(b):
                        cin = cut(b, F2_CIN, 3 * CW).rearrange("p (k n) -> p k n", k=3)
                        v.memset(cin[:, :, 0:PAD], 0.0)
                        v.memset(cut(b, F2_PV, MI), 0.0)
                        v.wait_ge(s["dt_psum"], b + 1)
                        own(tt(tiles(small(b, 0)), tiles(ps(b, 0, 16)), spread(W("f2_dtb"), 1, [P, T, MH]), ALU.add))
                        own.wait()
                        stt(small(b, 1), small(b, 0), -1.0, small(b, 0), ALU.mult, ALU.min).then_inc(s["dt_v"], 1)
                        v.wait_ge(s["xbc_ready"], b + 1)
                        for tap in range(TAPS):
                            for k in range(3):
                                xs, w = cut(b, F2_XS + k * N, N), W("f2_convw")[:, k * TAPS + tap:k * TAPS + tap + 1]
                                if tap == 0:
                                    last = ts(xs, cin[:, k, tap:tap + N], w, ALU.mult)
                                else:
                                    last = stt(xs, cin[:, k, tap:tap + N], w, xs, ALU.mult, ALU.add)
                                if tap == TAPS - 1:
                                    last.then_inc(s["conv_ready"], 1)
                            if tap < TAPS - 1:
                                own(last)
                                own.wait()

                    def f2_decay(b):
                        vv, e, u, ln, d, z, q, dt, da = (small(b, k) for k in range(9))
                        v.wait_ge(s["dt_e"], b + 1)
                        ts(u, e, 1.0, ALU.add).then_inc(s["dt_u"], 1)
                        v.wait_ge(s["dt_u"], b + 1)
                        ts(d, u, -1.0, ALU.add, 1e-30, ALU.max)
                        own(stt(z, u, 1.0, e, ALU.is_equal, ALU.mult))
                        own.wait()
                        own(v.reciprocal(d, d))
                        own(stt(z, vv, 0.0, z, ALU.max, ALU.add))
                        own.wait()
                        own(tt(d, d, e, ALU.mult))
                        own.wait()
                        v.wait_ge(s["dt_ln"], b + 1)
                        own(tt(q, d, ln, ALU.mult))
                        own.wait()
                        own(tt(dt, q, z, ALU.add))
                        own.wait()
                        tt(tiles(da), tiles(dt), spread(M("f2_nega"), 1, [P, T, MH]), ALU.mult).then_inc(s["da_ready"], 1)

                    def f2_cumulate(b):
                        v.wait_ge(s["ac_psum"], b + 1)
                        v.tensor_copy(small(b, 9), ps(b, 0, 16)).then_inc(s["ac_ready"], 1)

                    def f2_turn(b):
                        dt = small(b, 7)
                        v.wait_ge(s["xs_T"], b + 1)
                        xd = cut(b, F2_XD, T * MI).rearrange("p (c h d) -> p c h d", c=T, h=MH)
                        for k in range(2):
                            mine = tiles(dt)[:, :, 2 * k:2 * k + 2]
                            tt(xd[:, :, 2 * k:2 * k + 2, :], ps(b, 1 + k).rearrange("p (c h d) -> p c h d", c=T, h=2),
                               spread(mine, 3, [P, T, 2, MD]), ALU.mult)
                        bb = cut(b, F2_BB, N).rearrange("p (c q n) -> p c q n", c=T, q=2)
                        b_rows = tiles(ps(b, 3))[:, :, 0:MS]
                        v.tensor_copy(bb, spread(b_rows, 2, [P, T, 2, MS])).then_inc(s["xd_ready"], 1)
                        v.wait_ge(s["gt_psum"], b + 1)
                        tt(tiles(cut(b, F2_GM, N)), tiles(ps(b, 0)), spread(W("tri"), 1, [P, T, P]), ALU.mult).then_inc(s["gm_ready"], 1)

                    def f2_rows(b, c):
                        v.wait_ge(s["re_ready"], nth(c, b))
                        if c:
                            v.wait_ge(s["e_ready"], nth(c - 1, b))
                        for h in range(MH):
                            a = F2_S + 9 * 16 + c * MH + h
                            last = ts(cut(b, F2_DD + h * P, P), ps(b, 1, P, P, h * P), SC[b][:, a:a + 1], ALU.subtract, 0.0, ALU.min)
                        last.then_inc(s["dd_ready"], 1)

                    def f2_chunk(b, c):
                        e = cut(b, F2_E, N)
                        e4 = tiles(e, MH)
                        v.wait_ge(s["e_ready"], nth(c, b))
                        v.wait_ge(s["re_ready"], nth(c, b))
                        if c == 0:
                            v.wait_ge(s[f"cc_ready{b}"], 32)
                            v.wait_ge(s["gm_ready"], b + 1)
                        else:
                            v.wait_ge(s["yt_psum"], nth(c - 1, b))
                        ce = tiles(cut(b, F2_CE, MI), 2)
                        re = tiles(cut(b, F2_RE, N), MH)
                        for half in range(2):
                            rows = slice(half * MS, (half + 1) * MS)
                            cc = SC[b][rows, F2_CC + c * P:F2_CC + (c + 1) * P]
                            tt(ce[rows, :, :], re[rows, half::2, :], spread(cc, 1, [MS, 2, P]), ALU.mult)
                        xd = cut(b, F2_XD + c * MI, MI).rearrange("p (h d) -> p h d", h=MH)
                        tt(cut(b, F2_XDD, MI).rearrange("p (h d) -> p h d", h=MH), xd, e4[:, :, P - 1:P].to_broadcast([P, MH, MD]), ALU.mult)
                        tt(tiles(cut(b, F2_MT, N), MH), e4, spread(cut(b, F2_GM + c * P, P), 1, [P, MH, P]), ALU.mult).then_inc(s["mt_ready"], 1)

                    def f2_state(b, c):
                        v.wait_ge(s["yt_psum"], nth(c, b))
                        for h in range(MH):
                            half = h % 2
                            rows = slice(half * MS, (half + 1) * MS)
                            at = F2_PV + h // 2 * P + half * MD
                            st = SC[b][rows, at:at + MD]
                            last = stt(st, st, SC[b][rows, F2_RE + h * P + P - 1:F2_RE + h * P + P],
                                       PS[b][0][rows, h // 2 * P + half * MD:h // 2 * P + half * MD + MD], ALU.mult, ALU.add)
                        last.then_inc(s["pv_ready"], 1)

                    def f2_finish(b):
                        v.wait_ge(s["pv_ready"], nth(T - 1, b))
                        for k in range(2):
                            last = stt(cut(b, F2_YG + k * N, N), cut(b, F2_XS + k * N, N), W("f2_d")[:, k:k + 1], ps(b, 2 + k), ALU.mult, ALU.add)
                        own(last)
                        own.wait()
                        tt(cut(b, F2_YG, 2 * N), cut(b, F2_YG, 2 * N), cut(b, F2_Z, 2 * N), ALU.mult).then_inc(s["yg_ready"], 1)

                    def f2_end(b):
                        v.wait_ge(s["ym_psum"], b + 1)
                        ts(small(b, 10)[:, 0:T], ps(b, 1, T), 1.0 / MI, ALU.mult, EPS, ALU.add).then_inc(s["ms_ready"], 1)
                        v.wait_ge(s["rs_ready"], b + 1)
                        v.wait_ge(s["blin_added"], b + 1)
                        for t in range(T):
                            x = X[b][:, t, :]
                            last = stt(x, ps(b, 0, D, P, t * D), small(b, 11)[:, t:t + 1], x, ALU.mult, ALU.add)
                        new_x(b, 5, last)

                    def g3_project(b, layer):
                        v.wait_ge(s["qkv_psum"], nth(layer, b))
                        ts(cut(b, G3_K, N), ps(b, 2), W(f"g3_bk{layer}"), ALU.add)
                        tt(tiles(cut(b, G3_V, N)), tiles(ps(b, 3)), spread(W(f"g3_bv{layer}"), 1, [P, T, D]), ALU.add).then_inc(s["kv_ready"], 1)

                    def g3_max(b, layer, n):
                        k = layer * T * AH + n
                        v.wait_ge(s["att_psum"], nth(k, b))
                        v.tensor_reduce(cut(b, G3_MX + n, 1), ps(b, n % 2), AX, ALU.max, negate=True).then_inc(s["att_max"], 1)

                    def g3_sum(b, layer, n):
                        k = layer * T * AH + n
                        v.wait_ge(s["att_exp"], nth(k, b))
                        v.reciprocal(cut(b, G3_RI + n, 1), cut(b, G3_SUM + n, 1)).then_inc(s["att_rsum"], 1)

                    def g3_turned(b, layer, n):
                        k = layer * T * AH + n
                        v.wait_ge(s["pT_psum"], nth(k, b))
                        if n % AH == 0 and n:
                            v.wait_ge(s["pv_psum"], nth(layer * T + n // AH - 1, b))
                        pt = cut(b, G3_PT, T * AH * P).rearrange("p (j h n) -> p j h n", j=T, h=AH)
                        v.tensor_copy(pt[:, :, n % AH, :], ps(b, 2).rearrange("p (j n) -> p j n", j=T)).then_inc(s["pT_even"], 1)

                    def g3_end(b):
                        o = cut(b, G3_O, N)
                        v.wait_ge(s["g3_psum"], b + 1)
                        own(tt(tiles(o), tiles(ps(b, 0)), spread(W("g3_bout"), 1, [P, T, D]), ALU.add))
                        own.wait()
                        new_x(b, 6, stt(X[b][:, :, :], tiles(o), 0.0, X[b][:, :, :], ALU.max, ALU.add))

                    def f3_router(b):
                        v.wait_ge(s["w3_psum"], b + 1)
                        ts(cut(b, F3_W, T), ps(b, 3, T), W("f3_br"), ALU.add).then_inc(s["w3_ready"], 1)

                    def f3_rank(b):
                        w, cnt, sc = cut(b, F3_W, T), cut(b, F3_CNT, 3 * T), cut(b, F3_SC, T)
                        v.wait_ge(s["w3_ready"], b + 1)
                        own(v.memset(cnt, 0.0))
                        own.wait()
                        v.wait_ge(s["row3_psum"], b + 1)
                        for t in range(T):
                            cmp = cut(b, F3_CMP + t * (N + P), N + P)
                            if t:
                                ts(cmp[:, 0:t * P], ps(b, 2, t * P), w[:, t:t + 1], ALU.is_ge, None, ALU.add, accum_out=cnt[:, 3 * t:3 * t + 1])
                            ts(cmp[:, t * P:N], ps(b, 2, N - t * P, P, t * P), w[:, t:t + 1], ALU.is_gt, None, ALU.add,
                               accum_out=cnt[:, 3 * t + 1:3 * t + 2])
                            last = stt(cmp[:, N:N + P], ps(b, 2, P, P, t * P), w[:, t:t + 1], W("lower"), ALU.is_equal, ALU.mult,
                                       accum_out=cnt[:, 3 * t + 2:3 * t + 3])
                        own(last)
                        own.wait()
                        own(v.tensor_reduce(sc, cnt.rearrange("p (t k) -> p t k", t=T), AX, ALU.add))
                        own.wait()
                        stt(sc, sc, KEPT - 0.5, w, ALU.is_lt, ALU.mult).then_inc(s["scale3_ready"], 1)

                    def f3_end(b):
                        y = cut(b, F3_Y, N)
                        v.wait_ge(s["y3_psum"], b + 1)
                        own(tt(tiles(y), tiles(ps(b, 3)), spread(W("f3_b2"), 1, [P, T, D]), ALU.add))
                        own.wait()
                        v.wait_ge(s["scale3_ready"], b + 1)
                        v.wait_ge(s["xn_added"], b + 1)
                        for t in range(T):
                            x = X[b][:, t, :]
                            last = stt(x, y[:, tile(t)], cut(b, F3_SC + t, 1), x, ALU.mult, ALU.add)
                        last.then_inc(s["x_new"], 1)

                    def turns(g, *args):
                        for b in lanes:
                            g(b, *args)

                    turns(g0_start)
                    turns(g0_masks)
                    for k in range(GNN0_STEPS):
                        turns(g0_messages, k)
                        turns(g0_gates, k)
                    for b in lanes:
                        g0_end(b)
                        f0_start(b)
                    turns(f0_gate)
                    turns(f0_gate_end)
                    turns(f0_bias)
                    for e in range(EXPERTS - 1):
                        turns(f0_combine, e)
                    for b in lanes:
                        f0_combine(b, EXPERTS - 1)
                        layernorm(b, 3, X[b], G1)
                    turns(g1_project)
                    for t in range(T):
                        turns(g1_scores, t)
                    for b in lanes:
                        g1_end(b)
                        layernorm(b, 4, X[b], F1)
                    for t in range(T + 1):
                        if t < T:
                            turns(f1_logits, t)
                        if t >= 1:
                            turns(f1_sums, t - 1)
                    turns(f1_tokens)
                    turns(f1_project)
                    turns(f1_attend)
                    turns(f1_mix)
                    for b in lanes:
                        f1_end(b)
                        layernorm(b, 5, X[b], G2)
                    for b in lanes:
                        g2_end(b)
                        layernorm(b, 6, X[b], F2)
                    turns(f2_conv)
                    turns(f2_decay)
                    turns(f2_cumulate)
                    turns(f2_turn)
                    for c in range(T):
                        turns(f2_rows, c)
                        turns(f2_chunk, c)
                        turns(f2_state, c)
                    turns(f2_finish)
                    for b in lanes:
                        f2_end(b)
                        layernorm(b, 7, X[b], G3)
                    for layer in range(2):
                        turns(g3_project, layer)
                        for n in range(T * AH + 2):
                            for b in lanes:
                                if n < T * AH:
                                    g3_max(b, layer, n)
                                if 1 <= n <= T * AH:
                                    g3_sum(b, layer, n - 1)
                                if n >= 2 and n % 2 == 0:
                                    g3_turned(b, layer, n - 2)
                    for b in lanes:
                        g3_end(b)
                        layernorm(b, 8, X[b], F3)
                    turns(f3_router)
                    turns(f3_rank)
                    turns(f3_end)

                @block.gpsimd
                def _(g):
                    own = Steps(g, s["g_step"])

                    def root(b, n):
                        g.wait_ge(s[f"var_ready{b}"], n + 1)
                        g.tensor_tensor(rstd[b][:, :], ve[b][:, :], minus_half[:, :], ALU.pow).then_inc(s[f"rstd_ready{b}"], 1)

                    def add_to_x(b, row, done):
                        g.tensor_tensor(X[b][:, :, :], X[b][:, :, :], spread(row, 1, [P, T, D]), ALU.add).then_inc(done, 1)

                    def f1_normalise(b, t):
                        sw = cut(b, F1_SW + t * N, N).rearrange("p (h g) -> p h g", g=SG)
                        g.wait_ge(s["sl_rsum"], nth(t, b))
                        g.tensor_tensor(sw, sw, spread(cut(b, F1_RI + t * SH, SH), 2, [P, SH, SG]), ALU.mult).then_inc(s["sw_ready"], 1)

                    def g2_adjacency(b):
                        g.wait_ge(s["aggr_psum"], nth(GNN0_STEPS - 1, b))
                        g.tensor_copy(AF[b][:, :, :], ADJ[b][:, :, :]).then_inc(s["adjf_ready"], 1)

                    def g3_normalise(b, layer, n):
                        k = layer * T * AH + n
                        p = cut(b, G3_P + n % G3_RING * N, N)
                        g.wait_ge(s["att_rsum"], nth(k, b))
                        g.tensor_scalar(p, p, cut(b, G3_RI + n, 1), 1.0, ALU.mult, ALU.mult).then_inc(s["att_p"], 1)

                    for b in lanes:
                        root(b, 0)
                    for b in lanes:
                        root(b, 1)
                        root(b, 2)
                    for b in lanes:
                        g2_adjacency(b)
                    for b in lanes:
                        root(b, 3)
                    for b in lanes:
                        root(b, 4)
                    for b in lanes:
                        g.wait_ge(s["xn_ready"], nth(F1, b))
                        add_to_x(b, W("f1_bout"), s["bout_added"])
                    for t in range(T):
                        for b in lanes:
                            f1_normalise(b, t)
                    for b in lanes:
                        root(b, 5)
                    for b in lanes:
                        root(b, 6)
                    for b in lanes:
                        g.wait_ge(s["xn_ready"], nth(F2, b))
                        add_to_x(b, W("f2_blin"), s["blin_added"])
                    for b in lanes:
                        g.wait_ge(s["ms_ready"], b + 1)
                        g.tensor_tensor(cut(b, F2_S + 11 * 16, T), cut(b, F2_S + 10 * 16, T), minus_half[:, :], ALU.pow).then_inc(s["rs_ready"], 1)
                        root(b, 7)
                    for b in lanes:
                        g.wait_ge(s["xn_ready"], nth(G3, b))
                        g.memset(cut(b, G3_QZ, AH * N), 0.0).then_inc(s["qz_zero"], 1)
                    for layer in range(2):
                        for n in range(T * AH):
                            for b in lanes:
                                g3_normalise(b, layer, n)
                    for b in lanes:
                        root(b, 8)
                    for b in lanes:
                        g.wait_ge(s["xn_ready"], nth(F3, b))
                        g.tensor_tensor(X[b][:, :, :], X[b][:, :, :], XN[b][:, :, 0:D], ALU.add).then_inc(s["xn_added"], 1)

            nc.gpsimd.sem_clear(range(first_sem, last_sem + 1))
            nc.all_engine_barrier()


def lay_out(inputs):
    def rows(a, n=P):
        return np.broadcast_to(np.asarray(a, np.float32).reshape(1, -1), (n, np.asarray(a).size))

    def cols(a):
        return np.asarray(a, np.float32).reshape(-1, P).T

    def k_tiles(a):
        a = np.asarray(a, np.float32)
        return a.reshape(-1, P, a.shape[-1]).transpose(1, 0, 2).reshape(P, -1)

    g = {k: np.asarray(v) for k, v in inputs.items()}
    index = np.arange(P)
    parts = {
        "ident": np.eye(P), "tri": index[:, None] <= index[None, :], "lower": index[:, None] > index[None, :],
        "ones": np.ones((P, 1)),
        "before": rows(np.arange(EXPERTS)[None, :] < np.arange(EXPERTS)[:, None]),
        "own_head": (2 * np.arange(PAIRS)[None, :, None] + (index // SG)[:, None, None]
                     == np.arange(SH)[None, None, :]).reshape(P, -1),
        "g0_w": g["L0_gnn_weight"].transpose(1, 0, 2).reshape(D, -1),
        "g0_wih": g["L0_gnn_w_ih"].T, "g0_whh": g["L0_gnn_w_hh"].T,
        "g0_bih": cols(g["L0_gnn_b_ih"]), "g0_bhh": cols(g["L0_gnn_b_hh"]),
        "f0_gamma": cols(g["L0_ffn_gamma"]), "f0_beta": cols(g["L0_ffn_beta"]),
        "f0_wr": g["L0_ffn_Wr"], "f0_br": rows(g["L0_ffn_br"]),
        "f0_w1": g["L0_ffn_W1"].transpose(1, 0, 2).reshape(D, -1), "f0_b1": cols(g["L0_ffn_b1"]),
        "f0_w2": k_tiles(g["L0_ffn_W2"].reshape(EXPERTS * EXPERT_H, D)), "f0_b2": g["L0_ffn_b2"],
        "g1_w": g["L1_gnn_W"], "g1_wT": g["L1_gnn_W"].T, "g1_a": cols(g["L1_gnn_a"]),
        "f1_wfx": g["L1_ffn_W_fx"], "f1_bfx": g["L1_ffn_b_fx"].reshape(SH, SD), "f1_bout": rows(g["L1_ffn_b_out"]),
        "f1_wxT": g["L1_ffn_W_x"].reshape(D, SH, SD).transpose(2, 1, 0).reshape(SD, -1),
        "f1_wslice": g["L1_ffn_W_slice"], "f1_bx": g["L1_ffn_b_x"].reshape(SH, SD).T, "f1_bslice": rows(g["L1_ffn_b_slice"]),
        "f1_temp": rows(g["L1_ffn_temperature"]),
        "f1_wqT": g["L1_ffn_W_q"].T, "f1_wkT": g["L1_ffn_W_k"].T, "f1_wvT": g["L1_ffn_W_v"].T,
        "f1_wout": g["L1_ffn_W_out"].reshape(SH, SD, D).transpose(1, 0, 2).reshape(SD, -1),
        "g2_wmsg": g["L2_gnn_W_msg"], "g2_wupd": g["L2_gnn_W_upd"], "g2_bias": rows(g["L2_gnn_bias"]),
        "f2_win": g["L2_ffn_W_in"],
        "f2_convw": g["L2_ffn_conv_w"].reshape(3, P, TAPS).transpose(1, 0, 2).reshape(P, -1), "f2_convb": cols(g["L2_ffn_conv_b"]),
        "f2_dtb": rows(g["L2_ffn_dt_bias"]), "f2_alog": rows(g["L2_ffn_A_log"]),
        "f2_d": cols(np.repeat(g["L2_ffn_D"], MD)), "f2_normw": cols(g["L2_ffn_norm_w"]),
        "f2_woutT": g["L2_ffn_W_out"].T, "f2_wlin": g["L2_ffn_W_lin"], "f2_blin": rows(g["L2_ffn_b_lin"]),
        "g3_wout": k_tiles(g["L3_gnn_Wout"]), "g3_bout": rows(g["L3_gnn_bout"]),
        "f3_wr": g["L3_ffn_wr"], "f3_br": rows(g["L3_ffn_br"]), "f3_w1": g["L3_ffn_w1"], "f3_b1": cols(g["L3_ffn_b1"]),
        "f3_w2": k_tiles(g["L3_ffn_w2"]), "f3_b2": rows(g["L3_ffn_b2"]),
    }
    for n in range(2):
        for q in "qkv":
            parts[f"g3_w{q}{n}"] = k_tiles(g[f"L3_gnn_W{q}{n}"])
        for q in "qk":
            parts[f"g3_b{q}{n}"] = cols(g[f"L3_gnn_b{q}{n}"])
        parts[f"g3_bv{n}"] = rows(g[f"L3_gnn_bv{n}"])
    packs = []
    for table in (WEIGHTS, RAW):
        at, width = columns_of(table)
        pack = np.zeros((P, width), np.float32)
        for name, n_rows, n_cols in table:
            pack[0:n_rows, at[name][0]:at[name][0] + n_cols] = parts[name]
        packs.append(pack)
    return packs


def kernel(**inputs):
    import concourse.bacc as bacc
    from concourse.bass_utils import run_bass_kernel_spmd

    weights, raw = lay_out(inputs)
    arrays = {
        "x": np.ascontiguousarray(inputs["x"]), "adj": np.ascontiguousarray(inputs["adj"]),
        "weights": weights, "raw": raw,
    }
    nc = bacc.Bacc("TRN2", target_bir_lowering=False, num_devices=1)
    aps = [nc.dram_tensor(k, a.shape, mybir.dt.from_np(a.dtype), kind="ExternalInput").ap() for k, a in arrays.items()]
    out = nc.dram_tensor("out", arrays["x"].shape, F32, kind="ExternalOutput").ap()
    build(nc, *aps, out)
    result = run_bass_kernel_spmd(nc, [arrays], core_ids=[0])
    return result.results[0]["out"]
```

```python
from contextlib import ExitStack

import concourse.bass as bass
import numpy as np
from concourse import mybir

F32 = mybir.dt.float32
BF16 = mybir.dt.bfloat16
I32 = mybir.dt.int32
ALU = mybir.AluOpType
ACT = mybir.ActivationFunctionType
AX = mybir.AxisListType.X

P = 128
LANES = 2
D = 128
N = 512
T = N // P
EPS = 1e-5
GNN0_STEPS = 3
EXPERTS, EXPERT_H = 8, 256
GATE_TURN = 4
SH, SG, SD = 8, 64, 64
PAIRS = SH // 2
MH, MD, MS = 4, 64, 64
MI = MH * MD
TAPS = 4
AH, AD = 4, 32
FH = 512
KEPT = N // 2 - 1
BIG = 2.0 ** 60
SCRATCH = 9216

WEIGHTS = [
    ("ident", P, P), ("tri", P, P), ("lower", P, P), ("ones", P, 1), ("before", P, 64), ("own_head", P, PAIRS * SH),
    ("g0_w", P, GNN0_STEPS * D), ("g0_wih", P, 3 * D), ("g0_whh", P, 3 * D), ("g0_bih", P, 3), ("g0_bhh", P, 3),
    ("f0_gamma", P, 1), ("f0_beta", P, 1), ("f0_wr", P, EXPERTS), ("f0_br", P, EXPERTS),
    ("f0_w1", P, EXPERTS * EXPERT_H), ("f0_b1", P, EXPERTS * 2), ("f0_w2", P, EXPERTS * 2 * D), ("f0_b2", EXPERTS, D),
    ("g1_w", P, D),
    ("f1_wfx", P, SH * SD), ("f1_bfx", SH, SD), ("f1_bout", P, D),
    ("g2_wmsg", P, D), ("g2_wupd", P, D), ("g2_bias", P, D),
    ("f2_win", P, 2 * MI + 2 * MS + MH), ("f2_convw", P, 3 * TAPS), ("f2_convb", P, 3), ("f2_dtb", P, MH),
    ("f2_d", P, 2), ("f2_blin", P, D),
    ("g3_wk0", P, D), ("g3_wv0", P, D), ("g3_wk1", P, 2 * D), ("g3_wv1", P, 2 * D),
    ("g3_bk0", P, 1), ("g3_bk1", P, 1), ("g3_bv0", P, D), ("g3_bv1", P, D), ("g3_wout", P, 3 * D), ("g3_bout", P, D),
    ("f3_wr", P, 1), ("f3_br", P, 1), ("f3_w1", P, FH), ("f3_b1", P, FH // P), ("f3_w2", P, FH), ("f3_b2", P, D),
]
RAW = [
    ("g1_wT", P, D), ("g1_a", P, 2),
    ("f1_wxT", SD, SH * D), ("f1_wslice", SD, SG), ("f1_bx", SD, SH), ("f1_bslice", P, SG), ("f1_temp", P, SH),
    ("f1_wqT", SD, SD), ("f1_wkT", SD, SD), ("f1_wvT", SD, SD), ("f1_wout", SD, SH * D),
    ("f2_woutT", P, MI), ("f2_wlin", P, D), ("f2_normw", P, 2), ("f2_alog", P, MH),
    ("g3_wq0", P, D), ("g3_wq1", P, 2 * D), ("g3_bq0", P, 1), ("g3_bq1", P, 1),
]
MADE = [
    ("g0_brz", 2), ("g1_wa", 2), ("g1_wa2", P), ("f1_ws", SH * SG), ("f1_bs", SH * SG), ("f1_wqk", SD),
    ("f1_wvo", SH * D), ("f2_wol", 2 * D), ("f2_nega", MH), ("g3_wq0", D), ("g3_wq1", 2 * D), ("g3_bq0", 1), ("g3_bq1", 1),
    ("f1_rtemp", SH),
]


def columns_of(table):
    at, out = 0, {}
    for entry in table:
        out[entry[0]] = (at, entry[-1])
        at += entry[-1]
    return out, at


class Steps:

    def __init__(self, eng, sem):
        self.eng, self.sem, self.n = eng, sem, 0

    def __call__(self, ins):
        self.n += 1
        ins.then_inc(self.sem, 1)

    def wait(self):
        self.eng.wait_ge(self.sem, self.n)


def nth(k, b):
    return LANES * k + b + 1


def build(nc, x, adj, weights, raw, out):
    graphs = x.shape[0]
    x_rows = x.rearrange("g (t p) d -> g p t d", p=P)
    adj_rows = adj.rearrange("g (t p) n -> g p t n", p=P)
    out_rows = out.rearrange("g (t p) d -> g p t d", p=P)
    w_at, w_cols = columns_of(WEIGHTS)
    raw_at, raw_cols = columns_of(RAW)
    made_at, made_cols = columns_of(MADE)
    assert raw_cols <= SCRATCH

    ctx = ExitStack()
    with ctx:
        def sb(name, shape, dt=F32):
            return ctx.enter_context(nc.sbuf_tensor(name, shape, dt))

        def sem(name):
            return ctx.enter_context(nc.semaphore(name))

        weights_sb = sb("weights_sb", [P, w_cols])
        made_sb = sb("made_sb", [P, made_cols])
        ident_big = sb("ident_big", [P, P], BF16)
        minus_half = sb("minus_half", [P, T])
        XIN = [sb(f"x_in{b}", [P, T, D]) for b in range(LANES)]
        X = [sb(f"x{b}", [P, T, D]) for b in range(LANES)]
        XN = [sb(f"xn{b}", [P, T, 132]) for b in range(LANES)]
        XT = [sb(f"xT{b}", [P, N]) for b in range(LANES)]
        ADJ = [sb(f"adj{b}", [P, T, N], I32) for b in range(LANES)]
        AF = [sb(f"adjf{b}", [P, T, N]) for b in range(LANES)]
        NM = [sb(f"nomask{b}", [P, T, N], BF16) for b in range(LANES)]
        stats = [sb(f"stats{b}", [P, T, 6]) for b in range(LANES)]
        mv = [sb(f"mv{b}", [P, T, 2]) for b in range(LANES)]
        ve = [sb(f"ve{b}", [P, T]) for b in range(LANES)]
        rstd = [sb(f"rstd{b}", [P, T]) for b in range(LANES)]
        SC = [sb(f"scratch{b}", [P, SCRATCH]) for b in range(LANES)]
        PS = [[ctx.enter_context(nc.psum_tensor(f"ps{b}_{i}", [P, 512], F32)) for i in range(4)] for b in range(LANES)]

        def W(name, rows=P):
            a, n = w_at[name]
            return weights_sb[0:rows, a:a + n]

        def R(name, rows=P):
            a, n = raw_at[name]
            return SC[0][0:rows, a:a + n]

        def M(name, rows=P):
            a, n = made_at[name]
            return made_sb[0:rows, a:a + n]

        def cut(b, at, n, rows=P):
            return SC[b][0:rows, at:at + n]

        def ps(b, i, n=512, rows=P, at=0):
            return PS[b][i][0:rows, at:at + n]

        def tile(t, n=P):
            return slice(t * n, (t + 1) * n)

        def spread(ap, axis, shape):
            return ap.unsqueeze(axis).to_broadcast(shape)

        ident = W("ident")

        G0_M, G0_AG, G0_R, G0_Z, G0_U = (512 * k for k in range(5))
        F0_HID, F0_LG, F0_GT, F0_EQ, F0_RK, F0_SEL, F0_LS, F0_S, F0_TH, F0_GATE, F0_GATET = (
            0, 1024, 1088, 1344, 1600, 1632, 1664, 1696, 1704, 1736, 1792)
        G1_WH, G1_F, G1_Z, G1_U, G1_P, G1_PT, G1_MX, G1_SUM, G1_RI, G1_POS, G1_NEG = (
            0, 512, 1024, 2048, 3072, 4096, 6144, 6148, 6152, 6160, 6672)
        F1_SW, F1_SWT, F1_MX, F1_SUM, F1_RI, F1_SN, F1_DEN, F1_RD, F1_RAT, F1_RM, F1_ST, F1_RR, F1_TK, F1_QP, F1_TV = (
            0, 2048, 4096, 4128, 4160, 4192, 4704, 4708, 4712, 4716, 4748, 5260, 5772, 6284, 6796)
        F1_E, F1_EMX, F1_ES, F1_ER, F1_ET, F1_U = 7820, 8076, 8080, 8084, 8088, 8600
        G2_UP, G2_DEG, G2_RD, G2_POS, G2_C, G2_O = 0, 512, 516, 520, 524, 528
        PAD = TAPS - 1
        CW = N + PAD + 1
        F2_CIN, F2_XS, F2_CC, F2_Z, F2_XD, F2_BB, F2_GM, F2_CE, F2_XDD, F2_S = (
            0, 2048, 3840, 4352, 5376, 6400, 6912, 7424, 8192, 8960)
        F2_E, F2_PV, F2_YG, F2_SQ = 0, 3072, 0, 5376
        G3_QZ, G3_K, G3_V, G3_P, G3_PT, G3_H, G3_MX, G3_SUM, G3_RI = 0, 2048, 2560, 3072, 5120, 7168, 8192, 8224, 8256
        G3_RING = 4
        G3_O = 3072
        F3_HID, F3_W, F3_CMP, F3_CNT, F3_SC, F3_Y = 0, 2048, 2056, 4616, 4640, 4650
        lanes = range(LANES)

        loaded, first_loaded = sem("weights_loaded"), sem("first_loaded")
        prep_pe, prep_dve, prep_act = sem("prep_pe"), sem("prep_dve"), sem("prep_act")
        with nc.Block() as block:
            @block.sync
            def _(sp):
                sp.dma_start(SC[0][:, 0:raw_cols], raw).then_inc(loaded, 16)
                sp.dma_start(weights_sb[:, :], weights).then_inc(loaded, 16)
                for b in lanes:
                    sp.dma_start(XIN[b][:, :, :], x_rows[b]).then_inc(first_loaded, 16)
                    sp.dma_start(ADJ[b][:, :, :], adj_rows[b]).then_inc(first_loaded, 16)
                sp.wait_ge(first_loaded, 32 * LANES)

            @block.tensor
            def _(pe):
                pe.wait_ge(loaded, 32)
                pe.matmul(ps(0, 0, 2), R("g1_wT"), R("g1_a"), start=True, stop=True)
                pe.matmul(ps(0, 0, SD, SD, 64), R("f1_wqT", SD), R("f1_wkT", SD), start=True, stop=True)
                for k in range(2):
                    pe.matmul(ps(0, 3, D, P, k * D), R("f2_woutT")[:, tile(k)], R("f2_wlin"), start=True, stop=True)
                for h in range(SH):
                    pe.matmul(ps(0, 1, SG, P, h * SG), R("f1_wxT", SD)[:, tile(h)], R("f1_wslice", SD), start=True, stop=True)
                    pe.matmul(ps(0, 2, SG, P, h * SG), R("f1_bx", SD)[:, h:h + 1].to_broadcast([SD, P]),
                              R("f1_wslice", SD), start=True, stop=True)
                    last = pe.matmul(ps(1, h // 4, D, SD, (h % 4) * D), R("f1_wvT", SD), R("f1_wout", SD)[:, tile(h)],
                                     start=True, stop=True)
                last.then_inc(prep_pe, 1)

            @block.vector
            def _(v):
                v.memset(minus_half[:, :], -0.5)
                for b in lanes:
                    v.memset(XN[b][:, :, D:132], 1.0)
                v.wait_ge(loaded, 32)
                v.tensor_scalar(ident_big[:, :], ident, BIG, None, ALU.mult)
                v.tensor_tensor(M("g0_brz"), W("g0_bih")[:, 0:2], W("g0_bhh")[:, 0:2], ALU.add)
                v.tensor_scalar(M("f1_rtemp"), R("f1_temp"), 0.1, 5.0, ALU.max, ALU.min).then_inc(prep_dve, 1)
                v.wait_ge(prep_dve, 1)
                v.reciprocal(M("f1_rtemp"), M("f1_rtemp")).then_inc(prep_dve, 1)
                for q in ("g3_wq0", "g3_wq1", "g3_bq0", "g3_bq1"):
                    v.tensor_scalar(M(q), R(q), AD ** -0.5, None, ALU.mult)
                v.wait_ge(prep_pe, 1)
                v.tensor_copy(M("g1_wa"), ps(0, 0, 2))
                v.tensor_copy(M("g1_wa2"), ps(0, 0, 1, P, 1).to_broadcast([P, P]))
                v.tensor_scalar(M("f1_wqk", SD), ps(0, 0, SD, SD, 64), SD ** -0.5, None, ALU.mult)
                for k in range(2):
                    v.tensor_scalar(M("f2_wol")[:, tile(k)], ps(0, 3, D, P, k * D), R("f2_normw")[:, k:k + 1], None, ALU.mult)
                    v.tensor_copy(M("f1_wvo", SD)[:, tile(k, 512)], ps(1, k, 512, SD))
                v.wait_ge(prep_dve, 2)
                rtemp = spread(M("f1_rtemp"), 2, [P, SH, SG])
                v.tensor_tensor(M("f1_ws").rearrange("p (h g) -> p h g", h=SH), ps(0, 1).rearrange("p (h g) -> p h g", h=SH),
                                rtemp, ALU.mult)
                bs = M("f1_bs").rearrange("p (h g) -> p h g", h=SH)
                v.tensor_tensor(bs, ps(0, 2).rearrange("p (h g) -> p h g", h=SH), spread(R("f1_bslice"), 1, [P, SH, SG]),
                                ALU.add).then_inc(prep_dve, 1)
                v.wait_ge(prep_dve, 3)
                v.tensor_tensor(bs, bs, rtemp, ALU.mult)
                v.wait_ge(prep_act, 1)
                v.tensor_scalar(M("f2_nega"), M("f2_nega"), -1.0, None, ALU.mult)

            @block.scalar
            def _(act):
                act.wait_ge(loaded, 32)
                act.activation(M("f2_nega"), R("f2_alog"), ACT.Exp).then_inc(prep_act, 1)

        names = [
            "next_loaded",
            "v_step", "g_step", "a_step",
            "x_new", "var_ready0", "var_ready1", "rstd_ready0", "rstd_ready1", "xn_ready", "xT_psum", "xT_ready", "masks_ready", "stored",
            "m_psum", "m_ready", "aggr_psum", "aggr_ready", "rz_psum", "n_psum", "r_ready", "z_ready", "u_ready", "n_ready",
            "h_ready", "h_back",
            "logit_psum", "half_gap", "gate_tanh", "gate_ready", "gT_psum", "gT_ready", "b2_psum", "b2_added", "hid_psum", "hid_ready", "y_psum", "combined",
            "wh_psum", "wh_ready", "f_ready", "z1_psum", "z1_ready", "u1_ready", "p1_ready", "p1T_psum", "p1T_ready",
            "o1_psum", "o1_neg", "elu_exp",
            "sl_psum", "sl_biased", "sl_shifted", "sl_exp", "sl_rsum", "sw_ready", "swT_psum", "swT_ready", "tok_psum",
            "sn_ready", "sT_psum", "sT_ready", "ratio_psum", "ratio_ready", "tk_psum", "tk_ready", "qp_psum", "qp_ready",
            "tv_ready", "sc_psum", "sc_shifted", "sc_exp", "sc_sum", "eT_psum", "eT_ready", "u_psum", "us_ready", "so_psum", "bout_added",
            "adjf_ready", "h2_psum", "h2_ready", "upd_psum", "msg_psum",
            "xbc_psum", "dt_psum", "dt_v", "dt_e", "dt_u", "dt_ln", "xbc_ready", "zg_psum", "zg_ready", "conv_ready", "silu_ready", "cc_ready0", "cc_ready1",
            "da_ready", "ac_psum", "ac_ready", "xs_T", "xd_ready", "gt_psum", "gm_ready", "row_psum", "dd_ready", "re_ready", "e_ready",
            "ce_ready", "xdd_ready", "mt_ready", "st_psum", "pv_ready", "yt_psum", "yg_ready", "sq_ready", "ym_psum", "ms_ready", "rs_ready", "blin_added",
            "qkv_psum", "q_ready", "kv_ready", "qz_zero", "att_psum", "att_max", "att_exp", "att_rsum", "att_p", "pT_psum", "pT_even", "pT_odd",
            "pv_psum", "h3_ready", "g3_psum",
            "w3_psum", "w3_ready", "row3_psum", "scale3_ready", "hid3_psum", "hid3_ready", "y3_psum", "xn_added",
        ]
        s = {name: sem(name) for name in names}
        first_sem, last_sem = s[names[0]].num, s[names[-1]].num
        assert last_sem - first_sem == len(names) - 1

        def weights_T(b, h):
            if h % 2:
                return AF[b][:, :, :].rearrange("p t n -> p (t n)")[:, h // 2 * T * 2 * P:(h // 2 + 1) * T * 2 * P]
            return cut(b, G3_PT + h // 2 * T * 2 * P, T * 2 * P)

        def turned(eng, b, layer, n):
            eng.wait_ge(s["pT_odd" if n % 2 else "pT_even"], nth((layer * T * AH + n) // 2, b))

        G0, F0, G1, F1, G2, F2, G3, F3 = range(8)
        LN_OF = {G0: 0, F0: 2, G1: 3, F1: 4, G2: 5, F2: 6, G3: 7, F3: 8}

        rounds = graphs // LANES
        with nc.Fori(0, rounds) as i:
            after = (i + 1) % rounds
            with nc.Block() as block:
                @block.sync
                def _(sp):
                    for b in lanes:
                        sp.wait_ge(s["x_new"], nth(0, b))
                        g = bass.ds(after * LANES + b, 1)
                        sp.dma_start(XIN[b][:, :, :], x_rows[g].rearrange("a p t d -> (a p) t d")).then_inc(s["next_loaded"], 16)
                    for b in lanes:
                        sp.wait_ge(s["adjf_ready"], b + 1)
                        g = bass.ds(after * LANES + b, 1)
                        sp.dma_start(ADJ[b][:, :, :], adj_rows[g].rearrange("a p t n -> (a p) t n")).then_inc(s["next_loaded"], 16)
                    for b in lanes:
                        c_rows = SC[b][MS:P, F2_XS + 2 * N:F2_XS + 3 * N]
                        sp.wait_ge(s["silu_ready"], 3 * b + 1)
                        sp.dma_start(cut(b, F2_CC, N, MS), c_rows).then_inc(s[f"cc_ready{b}"], 16)
                        sp.dma_start(SC[b][MS:P, F2_CC:F2_CC + N], c_rows).then_inc(s[f"cc_ready{b}"], 16)
                    for b in lanes:
                        g = bass.ds(i * LANES + b, 1)
                        sp.wait_ge(s["x_new"], nth(8 - 1, b))
                        sp.dma_start(out_rows[g].rearrange("a p t d -> (a p) t d"), X[b][:, :, :]).then_inc(s["stored"], 16)
                    sp.wait_ge(s["stored"], 16 * LANES)
                    sp.wait_ge(s["next_loaded"], 32 * LANES)

                @block.tensor
                def _(pe):
                    def mm(o, lhsT, rhs, start=True, stop=True, **k):
                        return pe.matmul(o, lhsT, rhs, start=start, stop=stop, **k)

                    def to_columns(b, k):
                        pe.wait_ge(s["xn_ready"], nth(k, b))
                        for t in range(T):
                            last = pe.transpose(ps(b, 0, P, P, t * P), XN[b][:, t, 0:D], ident)
                        last.then_inc(s["xT_psum"], 1)

                    def g0_messages(b, k):
                        if k == 0:
                            pe.wait_ge(s["xT_ready"], nth(G0, b))
                        else:
                            pe.wait_ge(s["h_ready"], nth(k - 1, b))
                        h = XT[b]
                        for t in range(T):
                            last = mm(ps(b, 1, D, P, t * D), h[:, tile(t)], W("g0_w")[:, tile(k)])
                        last.then_inc(s["m_psum"], 1)
                        for gate in range(2):
                            mm(ps(b, 2 + gate), W("g0_whh")[:, tile(gate)], h[:, :], stop=False)
                        pe.wait_ge(s["m_ready"], nth(k, b))
                        if k == 0:
                            pe.wait_ge(s["masks_ready"], b + 1)
                        for t in range(T):
                            last = mm(ps(b, 1), cut(b, G0_M, N)[:, tile(t)], AF[b][:, t, :], start=t == 0, stop=t == T - 1)
                        last.then_inc(s["aggr_psum"], 1)
                        mm(ps(b, 0), W("g0_whh")[:, tile(2)], h[:, :])

                    def g0_gates(b, k):
                        pe.wait_ge(s["aggr_ready"], nth(k, b))
                        ag = cut(b, G0_AG, N)
                        for gate in range(2):
                            last = mm(ps(b, 2 + gate), W("g0_wih")[:, tile(gate)], ag, start=False)
                        last.then_inc(s["rz_psum"], 1)
                        mm(ps(b, 1), W("g0_wih")[:, tile(2)], ag).then_inc(s["n_psum"], 1)

                    def g0_back(b):
                        pe.wait_ge(s["h_ready"], nth(GNN0_STEPS - 1, b))
                        for t in range(T):
                            last = pe.transpose(ps(b, 0, P, P, t * P), XT[b][:, tile(t)], ident)
                        last.then_inc(s["h_back"], 1)

                    def f0_logits(b):
                        to_columns(b, F0)
                        pe.wait_ge(s["xT_ready"], nth(F0, b))
                        for t in range(T):
                            last = mm(ps(b, 3, EXPERTS, P, t * EXPERTS), XT[b][:, tile(t)], W("f0_wr"))
                        last.then_inc(s["logit_psum"], 1)

                    def f0_gate_columns(b):
                        pe.wait_ge(s["gate_ready"], b + 1)
                        pe.wait_ge(s["combined"], nth(GATE_TURN - 2, b))
                        gate = cut(b, F0_GATE, T * EXPERTS)
                        for t in range(T):
                            last = pe.transpose(ps(b, 3, P, EXPERTS, t * P), gate[:, tile(t, EXPERTS)], ident)
                        last.then_inc(s["gT_psum"], 1)

                    def f0_bias(b):
                        pe.wait_ge(s["gT_ready"], b + 1)
                        pe.wait_ge(s["combined"], nth(GATE_TURN - 1, b))
                        for t in range(T):
                            last = mm(ps(b, 2, D, P, t * D), cut(b, F0_GATET, N, EXPERTS)[:, tile(t)], W("f0_b2", EXPERTS))
                        last.then_inc(s["b2_psum"], 1)

                    def f0_hidden(b, e):
                        if e:
                            pe.wait_ge(s["hid_ready"], nth(e - 1, b))
                        for k in range(2):
                            last = mm(ps(b, k), W("f0_w1")[:, tile(2 * e + k)], XT[b][:, :])
                        last.then_inc(s["hid_psum"], 1)

                    def f0_out(b, e):
                        pe.wait_ge(s["hid_ready"], nth(e, b))
                        if e == 0:
                            pe.wait_ge(s["half_gap"], b + 1)
                        elif e == GATE_TURN:
                            pe.wait_ge(s["gT_ready"], b + 1)
                        elif e == GATE_TURN + 1:
                            pe.wait_ge(s["b2_added"], b + 1)
                        elif e >= 2:
                            pe.wait_ge(s["combined"], nth(e - 2, b))
                        for t in range(T):
                            for k in range(2):
                                last = mm(ps(b, 3 - e % 2, D, P, t * D), cut(b, F0_HID + k * N, N)[:, tile(t)],
                                          W("f0_w2")[:, tile(2 * e + k)], start=k == 0, stop=k == 1)
                        last.then_inc(s["y_psum"], 1)

                    def g1_project(b):
                        to_columns(b, G1)
                        pe.wait_ge(s["xT_ready"], nth(G1, b))
                        for t in range(T):
                            mm(ps(b, 1, D, P, t * D), XT[b][:, tile(t)], W("g1_w"))
                            last = mm(ps(b, 2, 2, P, 2 * t), XT[b][:, tile(t)], M("g1_wa"))
                        last.then_inc(s["wh_psum"], 1)

                    def g1_scores(b, t):
                        if t == 0:
                            pe.wait_ge(s["wh_ready"], b + 1)
                            pe.wait_ge(s["f_ready"], b + 1)
                        if t >= 2:
                            pe.wait_ge(s["z1_ready"], nth(t - 2, b))
                        mm(ps(b, t % 2), M("g1_wa2"), XT[b][:, :], stop=False)
                        mm(ps(b, t % 2), ident_big[:, :], NM[b][:, t, :], start=False).then_inc(s["z1_psum"], 1)

                    def g1_turn(b, t):
                        pe.wait_ge(s["p1_ready"], nth(t, b))
                        if t >= 2:
                            pe.wait_ge(s["p1T_ready"], nth(t - 2, b))
                        for j in range(T):
                            last = pe.transpose(ps(b, 2 + t % 2, P, P, j * P), cut(b, G1_P + t % 2 * N, N)[:, tile(j)], ident)
                        last.then_inc(s["p1T_psum"], 1)

                    def g1_out(b):
                        pe.wait_ge(s["p1T_ready"], nth(T - 1, b))
                        for t in range(T):
                            for j in range(T):
                                last = mm(ps(b, 0, D, P, t * D), cut(b, G1_PT + j * N, N)[:, tile(t)],
                                          cut(b, G1_WH, N)[:, tile(j)], start=j == 0, stop=j == T - 1)
                        last.then_inc(s["o1_psum"], 1)

                    def f1_logits(b, t):
                        if t == 0:
                            to_columns(b, F1)
                            pe.wait_ge(s["xT_ready"], nth(F1, b))
                        if t >= 2:
                            pe.wait_ge(s["sl_biased"], nth(t - 2, b))
                        mm(ps(b, t % 2), XT[b][:, tile(t)], M("f1_ws")).then_inc(s["sl_psum"], 1)

                    def f1_turn(b, t):
                        pe.wait_ge(s["sw_ready"], nth(t, b))
                        if t >= 2:
                            pe.wait_ge(s["swT_ready"], nth(t - 2, b))
                        for k in range(PAIRS):
                            last = pe.transpose(ps(b, 2 + t % 2, P, P, k * P), cut(b, F1_SW + t * N, N)[:, tile(k)], ident)
                        last.then_inc(s["swT_psum"], 1)

                    def f1_tokens(b):
                        pe.wait_ge(s["sl_biased"], nth(T - 1, b))
                        for k in range(PAIRS):
                            for t in range(T):
                                last = mm(ps(b, k // 2, D + 1, P, k % 2 * 256), cut(b, F1_SW + t * N, N)[:, tile(k)],
                                          XN[b][:, t, 0:D + 1], start=t == 0, stop=t == T - 1)
                        last.then_inc(s["tok_psum"], 1)

                    def f1_project(b):
                        pe.wait_ge(s["sn_ready"], b + 1)
                        pe.wait_ge(s["swT_ready"], nth(T - 1, b))
                        for k in range(PAIRS):
                            last = pe.transpose(ps(b, 2, P, P, k * P), cut(b, F1_SN, N)[:, tile(k)], ident)
                        last.then_inc(s["sT_psum"], 1)
                        for k in range(PAIRS):
                            last = mm(ps(b, 3, P, SH, k * P), cut(b, F1_RM, PAIRS * SH)[:, tile(k, SH)], ident)
                        last.then_inc(s["ratio_psum"], 1)
                        pe.wait_ge(s["ratio_ready"], b + 1)
                        pe.wait_ge(s["sT_ready"], b + 1)
                        mm(ps(b, 0, N, SD), W("f1_bfx", SH), cut(b, F1_RR, N, SH), stop=False)
                        for h in range(SH):
                            last = mm(ps(b, 0, SG, SD, h * SG), W("f1_wfx")[:, tile(h, SD)], cut(b, F1_ST, N)[:, tile(h, SG)],
                                      start=False, stop=h == SH - 1)
                        last.then_inc(s["tk_psum"], 1)

                    def f1_attend(b):
                        pe.wait_ge(s["tk_ready"], b + 1)
                        tk = cut(b, F1_TK, N, SD)
                        mm(ps(b, 1, N, SD), M("f1_wqk", SD), tk).then_inc(s["qp_psum"], 1)
                        for h in range(SH):
                            last = mm(ps(b, 2 + h // 4, D, SD, h % 4 * D), tk[:, tile(h, SG)], M("f1_wvo", SD)[:, tile(h)])
                        last.then_inc(s["tok_psum"], 1)
                        pe.wait_ge(s["qp_ready"], b + 1)
                        for h in range(SH):
                            half = SG * (h % 2)
                            last = mm(PS[b][0][half:half + SG, h // 2 * SG:(h // 2 + 1) * SG], cut(b, F1_QP, N, SD)[:, tile(h, SG)],
                                      tk[:, tile(h, SG)], tile_position=(0, half))
                        last.then_inc(s["sc_psum"], 1)

                    def f1_mix(b):
                        pe.wait_ge(s["sc_exp"], b + 1)
                        for k in range(PAIRS):
                            last = pe.transpose(ps(b, 1, P, SG, k * P), cut(b, F1_E, PAIRS * SG)[:, tile(k, SG)], ident)
                        last.then_inc(s["eT_psum"], 1)
                        pe.wait_ge(s["eT_ready"], b + 1)
                        pe.wait_ge(s["tv_ready"], b + 1)
                        for h in range(SH):
                            half = SG * (h % 2)
                            last = mm(PS[b][0][half:half + SG, tile(h // 2)], cut(b, F1_ET, N, SG)[:, tile(h, SG)],
                                      cut(b, F1_TV, SH * D, SG)[:, tile(h)], tile_position=(0, half))
                        last.then_inc(s["u_psum"], 1)

                    def f1_out(b):
                        pe.wait_ge(s["us_ready"], b + 1)
                        for t in range(T):
                            for k in range(PAIRS):
                                last = mm(ps(b, 1, D, P, t * D), cut(b, F1_SWT + k * N, N)[:, tile(t)],
                                          cut(b, F1_U, N)[:, tile(k)], start=k == 0, stop=k == PAIRS - 1)
                        last.then_inc(s["so_psum"], 1)

                    def g2_project(b):
                        to_columns(b, G2)
                        pe.wait_ge(s["xT_ready"], nth(G2, b))
                        for t in range(T):
                            last = mm(ps(b, 1, D, P, t * D), XT[b][:, tile(t)], W("g2_wmsg"))
                        last.then_inc(s["h2_psum"], 1)
                        for t in range(T):
                            last = mm(ps(b, 2, D, P, t * D), XT[b][:, tile(t)], W("g2_wupd"))
                        last.then_inc(s["upd_psum"], 1)

                    def g2_messages(b):
                        pe.wait_ge(s["h2_ready"], b + 1)
                        pe.wait_ge(s["adjf_ready"], b + 1)
                        for j in range(T):
                            for t in range(T):
                                last = mm(ps(b, 3 * (j // 2), D + 1, P, j % 2 * 256), AF[b][:, t, tile(j)],
                                          XN[b][:, t, 0:D + 1], start=t == 0, stop=t == T - 1)
                        last.then_inc(s["msg_psum"], 1)

                    def f2_project(b):
                        to_columns(b, F2)
                        pe.wait_ge(s["xT_ready"], nth(F2, b))
                        for k in (2, 0, 1):
                            mm(ps(b, 1 + k), W("f2_win")[:, tile(2 + k)], XT[b][:, :]).then_inc(s["xbc_psum"], 1)
                        for t in range(T):
                            last = mm(ps(b, 0, MH, P, t * MH), XT[b][:, tile(t)], W("f2_win")[:, 2 * MI + 2 * MS:])
                        last.then_inc(s["dt_psum"], 1)

                    def f2_gate(b):
                        pe.wait_ge(s["xbc_ready"], b + 1)
                        for k in range(2):
                            last = mm(ps(b, 1 + k), W("f2_win")[:, tile(k)], XT[b][:, :])
                        last.then_inc(s["zg_psum"], 1)

                    def f2_cumulate(b):
                        pe.wait_ge(s["da_ready"], b + 1)
                        mm(ps(b, 0, T * MH), W("tri"), cut(b, F2_S + 8 * 16, T * MH)).then_inc(s["ac_psum"], 1)

                    def f2_turn(b):
                        pe.wait_ge(s["zg_ready"], b + 1)
                        for n, k in enumerate((2, 0, 1)):
                            pe.wait_ge(s["silu_ready"], 3 * b + n + 1)
                            for c in range(T):
                                last = pe.transpose(ps(b, 1 + k, P, P, c * P), cut(b, F2_XS + k * N, N)[:, tile(c)], ident)
                        last.then_inc(s["xs_T"], 1)
                        pe.wait_ge(s[f"cc_ready{b}"], 32)
                        pe.wait_ge(s["ac_ready"], b + 1)
                        for c in range(T):
                            last = mm(ps(b, 0, P, P, c * P), cut(b, F2_XS + 2 * N, N, MS)[:, tile(c)], cut(b, F2_CC, N, MS)[:, tile(c)])
                        last.then_inc(s["gt_psum"], 1)

                    def f2_rows(b):
                        pe.wait_ge(s["xd_ready"], b + 1)
                        for c in (1, 2, 3, 0):
                            if c == 0:
                                pe.wait_ge(s["gm_ready"], b + 1)
                            for h in range(MH):
                                a = F2_S + 9 * 16 + c * MH + h
                                last = pe.transpose(ps(b, c, P, P, h * P), SC[b][:, a:a + 1].to_broadcast([P, P]), ident)
                            last.then_inc(s["row_psum"], 1)

                    def f2_states(b):
                        pe.wait_ge(s["xdd_ready"], b + 1)
                        for c in range(T - 1):
                            for k in range(2):
                                last = mm(ps(b, (c + 1) // 2, P, P, (c + 1) % 2 * MI + k * P), cut(b, F2_BB, N)[:, tile(c)],
                                          cut(b, F2_XDD + c * MI, MI)[:, tile(k)])
                            last.then_inc(s["st_psum"], 1)

                    def f2_within(b):
                        for c in range(T):
                            if c % 2 == 0:
                                pe.wait_ge(s["mt_ready"], 2 * b + c // 2 + 1)
                            for k in range(2):
                                for q in range(2):
                                    h = c * MH + 2 * k + q
                                    mm(PS[b][2 + k][q * MD:(q + 1) * MD, tile(c)], cut(b, F2_XD, T * MI)[:, tile(h, MD)],
                                       cut(b, F2_E, T * N)[:, tile(h)], start=c == 0, stop=False, tile_position=(0, q * MD))

                    def f2_across(b):
                        pe.wait_ge(s["ce_ready"], b + 1)
                        for c in range(1, T):
                            pe.wait_ge(s["pv_ready"], (T - 1) * b + c)
                            for k in range(2):
                                last = mm(ps(b, 2 + k, P, P, c * P), cut(b, F2_PV + (c - 1) * MI, MI)[:, tile(k)],
                                          cut(b, F2_CE + (c - 1) * MI, MI)[:, tile(k)], start=False, stop=c == T - 1)
                        last.then_inc(s["yt_psum"], 1)

                    def f2_out(b):
                        pe.wait_ge(s["yg_ready"], b + 1)
                        for t in range(T):
                            for k in range(2):
                                last = mm(ps(b, 0, D, P, t * D), cut(b, F2_YG + k * N, N)[:, tile(t)], M("f2_wol")[:, tile(k)],
                                          start=k == 0, stop=k == 1)
                        pe.wait_ge(s["sq_ready"], b + 1)
                        for t in range(T):
                            for k in range(2):
                                last = mm(ps(b, 1, 1, P, t), cut(b, F2_SQ + k * N, N)[:, tile(t)], W("ones"), start=k == 0, stop=k == 1)
                        last.then_inc(s["ym_psum"], 1)

                    def g3_project(b, layer):
                        if layer == 0:
                            to_columns(b, G3)
                            pe.wait_ge(s["xT_ready"], nth(G3, b))
                            ins = [XT[b][:, :]]
                        else:
                            pe.wait_ge(s["h3_ready"], nth(0, b))
                            turned(pe, b, 0, T * AH - 1)
                            ins = [XT[b][:, :], cut(b, G3_H, N)]
                        wq, wk, wv = M(f"g3_wq{layer}"), W(f"g3_wk{layer}"), W(f"g3_wv{layer}")
                        for bank, w in ((1, wq), (2, wk)):
                            for n, a in enumerate(ins):
                                mm(ps(b, bank), w[:, tile(n)], a, start=n == 0, stop=n == layer)
                        for t in range(T):
                            for n, a in enumerate(ins):
                                last = mm(ps(b, 3, D, P, t * D), a[:, tile(t)], wv[:, tile(n)], start=n == 0, stop=n == layer)
                        last.then_inc(s["qkv_psum"], 1)

                    def g3_scores(b, layer, n):
                        q, h = divmod(n, AH)
                        k = layer * T * AH + n
                        if n == 0:
                            pe.wait_ge(s["q_ready"], nth(layer, b))
                            pe.wait_ge(s["kv_ready"], nth(layer, b))
                        if n >= 2:
                            pe.wait_ge(s["att_exp"], nth(k - 2, b))
                        mm(ps(b, n % 2), cut(b, G3_QZ + h * N, N)[:, tile(q)], cut(b, G3_K, N), stop=False)
                        mm(ps(b, n % 2), ident_big[:, :], NM[b][:, q, :], start=False).then_inc(s["att_psum"], 1)

                    def g3_turn(b, layer, n):
                        k = layer * T * AH + n
                        pe.wait_ge(s["att_p"], nth(k, b))
                        if n >= 1:
                            turned(pe, b, layer, n - 1)
                        for j in range(T):
                            last = pe.transpose(ps(b, 2, P, P, j * P), cut(b, G3_P + n % G3_RING * N, N)[:, tile(j)], ident)
                        last.then_inc(s["pT_psum"], 1)

                    def g3_values(b, layer, pair):
                        turned(pe, b, layer, AH * (2 * pair + 2) - 2)
                        turned(pe, b, layer, AH * (2 * pair + 2) - 1)
                        for j in range(T):
                            for h in range(AH):
                                last = mm(PS[b][3][h * AD:(h + 1) * AD, tile(pair, 2 * P)], cut(b, G3_V + j * D, D)[:, tile(h, AD)],
                                          weights_T(b, h)[:, tile(j, 2 * P)], start=j == 0, stop=j == T - 1, tile_position=(0, h * AD))
                        last.then_inc(s["pv_psum"], 1)

                    def g3_out(b):
                        pe.wait_ge(s["h3_ready"], nth(1, b))
                        ins = [XT[b][:, :], cut(b, G3_H, N), cut(b, G3_H + N, N)]
                        for t in range(T):
                            for n, a in enumerate(ins):
                                last = mm(ps(b, 0, D, P, t * D), a[:, tile(t)], W("g3_wout")[:, tile(n)], start=n == 0, stop=n == 2)
                        last.then_inc(s["g3_psum"], 1)

                    def f3_router(b):
                        to_columns(b, F3)
                        pe.wait_ge(s["xT_ready"], nth(F3, b))
                        for t in range(T):
                            last = mm(ps(b, 3, 1, P, t), XT[b][:, tile(t)], W("f3_wr"))
                        last.then_inc(s["w3_psum"], 1)

                    def f3_hidden(b, k):
                        if k >= 2:
                            pe.wait_ge(s["hid3_ready"], nth(k - 2, b))
                        mm(ps(b, k % 2), W("f3_w1")[:, tile(k)], XT[b][:, :]).then_inc(s["hid3_psum"], 1)

                    def f3_rank(b):
                        pe.wait_ge(s["w3_ready"], b + 1)
                        for t in range(T):
                            last = pe.transpose(ps(b, 2, P, P, t * P), cut(b, F3_W + t, 1).to_broadcast([P, P]), ident)
                        last.then_inc(s["row3_psum"], 1)

                    def f3_out(b):
                        pe.wait_ge(s["hid3_ready"], nth(3, b))
                        for t in range(T):
                            for k in range(FH // P):
                                last = mm(ps(b, 3, D, P, t * D), cut(b, F3_HID + k * N, N)[:, tile(t)], W("f3_w2")[:, tile(k)],
                                          start=k == 0, stop=k == FH // P - 1)
                        last.then_inc(s["y3_psum"], 1)

                    def turns(f, *args):
                        for b in lanes:
                            f(b, *args)

                    turns(to_columns, G0)
                    for k in range(GNN0_STEPS):
                        for b in lanes:
                            g0_messages(b, k)
                            if k == GNN0_STEPS - 1 and b:
                                g0_back(b - 1)
                            g0_gates(b, k)
                    f0_logits(0)
                    f0_hidden(0, 0)
                    g0_back(1)
                    f0_logits(1)
                    f0_hidden(1, 0)
                    for e in range(EXPERTS):
                        if e == GATE_TURN:
                            turns(f0_gate_columns)
                        turns(f0_out, e)
                        if e == GATE_TURN:
                            turns(f0_bias)
                        if e + 1 < EXPERTS:
                            turns(f0_hidden, e + 1)
                    turns(g1_project)
                    for t in range(T + 2):
                        if t < T:
                            turns(g1_scores, t)
                        if t >= 2:
                            turns(g1_turn, t - 2)
                    turns(g1_out)
                    for t in range(T + 2):
                        if t < T:
                            turns(f1_logits, t)
                        if t >= 2:
                            turns(f1_turn, t - 2)
                    turns(f1_tokens)
                    turns(f1_project)
                    turns(f1_attend)
                    turns(f1_mix)
                    turns(f1_out)
                    turns(g2_project)
                    turns(g2_messages)
                    for b in lanes:
                        f2_project(b)
                        f2_gate(b)
                    for b in lanes:
                        f2_cumulate(b)
                        f2_turn(b)
                        f2_rows(b)
                    for b in lanes:
                        f2_states(b)
                        f2_within(b)
                    turns(f2_across)
                    turns(f2_out)
                    for layer in range(2):
                        turns(g3_project, layer)
                        for n in range(T * AH + 3):
                            for b in lanes:
                                if n < T * AH:
                                    g3_scores(b, layer, n)
                                if n >= 3 and (n - 3) % (2 * AH) == 2 * AH - 1:
                                    g3_values(b, layer, (n - 3) // (2 * AH))
                                if 2 <= n < T * AH + 2:
                                    g3_turn(b, layer, n - 2)
                    turns(g3_out)
                    turns(f3_router)
                    for k in range(FH // P):
                        turns(f3_hidden, k)
                        if k == 1:
                            turns(f3_rank)
                    turns(f3_out)

                @block.scalar
                def _(act):
                    own = Steps(act, s["a_step"])

                    def f(o, a, func, **k):
                        return act.activation(o, a, func, **k)

                    def columns_out(b, k):
                        act.wait_ge(s["xT_psum"], nth(k, b))
                        if k == F0:
                            f(XT[b][:, :], ps(b, 0), ACT.Identity, scale=W("f0_gamma"), bias=W("f0_beta")).then_inc(s["xT_ready"], 1)
                        else:
                            f(XT[b][:, :], ps(b, 0), ACT.Copy).then_inc(s["xT_ready"], 1)

                    def g0_messages(b, k):
                        act.wait_ge(s["m_psum"], nth(k, b))
                        f(cut(b, G0_M, N), ps(b, 1), ACT.Copy).then_inc(s["m_ready"], 1)

                    def g0_gates(b, k):
                        act.wait_ge(s["rz_psum"], nth(k, b))
                        f(cut(b, G0_R, N), ps(b, 2), ACT.Sigmoid, bias=M("g0_brz")[:, 0:1]).then_inc(s["r_ready"], 1)
                        f(cut(b, G0_Z, N), ps(b, 3), ACT.Sigmoid, bias=M("g0_brz")[:, 1:2]).then_inc(s["z_ready"], 1)
                        act.wait_ge(s["u_ready"], nth(k, b))
                        f(cut(b, G0_U, N), cut(b, G0_U, N), ACT.Tanh, bias=W("g0_bih")[:, 2:3]).then_inc(s["n_ready"], 1)

                    def f0_hidden(b, e):
                        act.wait_ge(s["hid_psum"], nth(e, b))
                        if e:
                            act.wait_ge(s["y_psum"], nth(e - 1, b))
                        for k in range(2):
                            last = f(cut(b, F0_HID + k * N, N), ps(b, k), ACT.Gelu, bias=W("f0_b1")[:, 2 * e + k:2 * e + k + 1])
                        last.then_inc(s["hid_ready"], 1)

                    def f0_tanh(b):
                        act.wait_ge(s["half_gap"], b + 1)
                        th = cut(b, F0_TH, T * EXPERTS)
                        f(th, th, ACT.Tanh).then_inc(s["gate_tanh"], 1)

                    def g1_project(b):
                        act.wait_ge(s["wh_psum"], b + 1)
                        f(cut(b, G1_WH, N), ps(b, 1), ACT.Copy).then_inc(s["wh_ready"], 1)

                    def g1_scores(b, t):
                        act.wait_ge(s["z1_psum"], nth(t, b))
                        if t == 0:
                            act.wait_ge(s["f_ready"], b + 1)
                        if t >= 2:
                            act.wait_ge(s["u1_ready"], nth(t - 2, b))
                        f(cut(b, G1_Z + t % 2 * N, N), ps(b, t % 2), ACT.Identity, bias=cut(b, G1_F + 2 * t, 1)).then_inc(s["z1_ready"], 1)

                    def g1_exp(b, t):
                        act.wait_ge(s["u1_ready"], nth(t, b))
                        if t >= 2:
                            act.wait_ge(s["p1T_psum"], nth(t - 2, b))
                        f(cut(b, G1_P + t % 2 * N, N), cut(b, G1_U + t % 2 * N, N), ACT.Exp, bias=cut(b, G1_MX + t, 1),
                          accum_out=cut(b, G1_SUM + t, 1)).then_inc(s["p1_ready"], 1)

                    def g1_turned(b, t):
                        act.wait_ge(s["p1T_psum"], nth(t, b))
                        pt = cut(b, G1_PT, T * N).rearrange("p (j n) -> p j n", j=T)
                        f(pt[:, :, tile(t)], ps(b, 2 + t % 2).rearrange("p (j n) -> p j n", j=T), ACT.Copy).then_inc(s["p1T_ready"], 1)

                    def g1_elu(b):
                        act.wait_ge(s["o1_neg"], b + 1)
                        f(cut(b, G1_NEG, N), cut(b, G1_NEG, N), ACT.Exp).then_inc(s["elu_exp"], 1)

                    def f1_exp(b, t):
                        act.wait_ge(s["sl_shifted"], nth(t, b))
                        sw = cut(b, F1_SW + t * N, N)
                        f(sw, sw, ACT.Exp).then_inc(s["sl_exp"], 1)

                    def f1_turned(b, t):
                        act.wait_ge(s["swT_psum"], nth(t, b))
                        swt = cut(b, F1_SWT, T * N).rearrange("p (k n) -> p k n", k=PAIRS)
                        f(swt[:, :, tile(t)], ps(b, 2 + t % 2).rearrange("p (k n) -> p k n", k=PAIRS), ACT.Copy).then_inc(s["swT_ready"], 1)

                    def f1_project(b):
                        act.wait_ge(s["sT_psum"], b + 1)
                        f(cut(b, F1_ST, N), ps(b, 2), ACT.Copy).then_inc(s["sT_ready"], 1)

                    def f1_attend(b):
                        act.wait_ge(s["qp_psum"], b + 1)
                        f(cut(b, F1_QP, N, SD), ps(b, 1, N, SD), ACT.Copy).then_inc(s["qp_ready"], 1)
                        act.wait_ge(s["tok_psum"], nth(1, b))
                        f(cut(b, F1_TV, N, SG), ps(b, 2, N, SG), ACT.Copy)
                        f(cut(b, F1_TV + N, N, SG), ps(b, 3, N, SG), ACT.Copy).then_inc(s["tv_ready"], 1)
                        act.wait_ge(s["sc_shifted"], b + 1)
                        e = cut(b, F1_E, PAIRS * SG)
                        f(e, e, ACT.Exp).then_inc(s["sc_exp"], 1)

                    def g2_project(b):
                        act.wait_ge(s["h2_psum"], b + 1)
                        f(XN[b][:, :, 0:D], ps(b, 1).rearrange("p (t d) -> p t d", t=T), ACT.Copy).then_inc(s["h2_ready"], 1)

                    def f2_project(b):
                        for n, k in enumerate((2, 0, 1)):
                            act.wait_ge(s["xbc_psum"], 3 * b + n + 1)
                            f(cut(b, F2_CIN + k * CW + PAD, N), ps(b, 1 + k), ACT.Copy)
                            tap = k * TAPS + TAPS - 1
                            last = f(cut(b, F2_XS + k * N, N), ps(b, 1 + k), ACT.Identity, scale=W("f2_convw")[:, tap:tap + 1])
                        last.then_inc(s["xbc_ready"], 1)

                    def f2_gate(b):
                        act.wait_ge(s["zg_psum"], b + 1)
                        for k in range(2):
                            last = f(cut(b, F2_Z + k * N, N), ps(b, 1 + k), ACT.Silu)
                        last.then_inc(s["zg_ready"], 1)

                    def f2_silu(b):
                        for n, k in enumerate((2, 0, 1)):
                            act.wait_ge(s["conv_ready"], 3 * b + n + 1)
                            xs = cut(b, F2_XS + k * N, N)
                            f(xs, xs, ACT.Silu, bias=W("f2_convb")[:, k:k + 1]).then_inc(s["silu_ready"], 1)

                    def f2_softplus(b):
                        act.wait_ge(s["dt_v"], b + 1)
                        f(cut(b, F2_S + 16, 16), cut(b, F2_S + 16, 16), ACT.Exp).then_inc(s["dt_e"], 1)

                    def f2_log(b):
                        act.wait_ge(s["dt_u"], b + 1)
                        f(cut(b, F2_S + 3 * 16, 16), cut(b, F2_S + 2 * 16, 16), ACT.Ln).then_inc(s["dt_ln"], 1)

                    def f2_rows(b):
                        for n, c in enumerate((1, 2, 3, 0)):
                            act.wait_ge(s["row_psum"], T * b + n + 1)
                            f(AF[b][:, c, :], ps(b, c), ACT.Exp).then_inc(s["re_ready"], 1)

                    def f2_decays(b):
                        act.wait_ge(s["dd_ready"], T * b + T)
                        for q in range(2):
                            e = cut(b, F2_E + 2 * q * N, 2 * N)
                            f(e, e, ACT.Exp).then_inc(s["e_ready"], 1)

                    def f2_square(b):
                        act.wait_ge(s["yg_ready"], b + 1)
                        f(cut(b, F2_SQ, 2 * N), cut(b, F2_YG, 2 * N), ACT.Square).then_inc(s["sq_ready"], 1)

                    def g3_project(b, layer):
                        act.wait_ge(s["qkv_psum"], nth(layer, b))
                        if layer == 0:
                            act.wait_ge(s["qz_zero"], b + 1)
                        for h in range(AH):
                            rows = slice(h * AD, (h + 1) * AD)
                            a = G3_QZ + h * N
                            last = f(SC[b][rows, a:a + N], PS[b][1][rows, :], ACT.Identity, bias=M(f"g3_bq{layer}")[rows, :])
                        last.then_inc(s["q_ready"], 1)

                    def g3_exp(b, layer, n):
                        k = layer * T * AH + n
                        act.wait_ge(s["att_max"], nth(k, b))
                        if k >= G3_RING:
                            act.wait_ge(s["pT_psum"], nth(k - G3_RING, b))
                        f(cut(b, G3_P + n % G3_RING * N, N), ps(b, n % 2), ACT.Exp, bias=cut(b, G3_MX + n, 1),
                          accum_out=cut(b, G3_SUM + n, 1)).then_inc(s["att_exp"], 1)

                    def g3_turned(b, layer, n):
                        k = layer * T * AH + n
                        act.wait_ge(s["pT_psum"], nth(k, b))
                        if n == 2 * AH + 1:
                            act.wait_ge(s["pv_psum"], nth(2 * layer, b))
                        pt = weights_T(b, n % AH).rearrange("p (j n) -> p j n", j=T)
                        f(pt[:, :, tile(n // AH % 2)], ps(b, 2).rearrange("p (j n) -> p j n", j=T), ACT.Copy).then_inc(s["pT_odd"], 1)

                    def g3_gather(b, layer):
                        act.wait_ge(s["pv_psum"], nth(2 * layer + 1, b))
                        f(cut(b, G3_H + layer * N, N), ps(b, 3), ACT.Copy).then_inc(s["h3_ready"], 1)

                    def f3_hidden(b, k):
                        act.wait_ge(s["hid3_psum"], nth(k, b))
                        f(cut(b, F3_HID + k * N, N), ps(b, k % 2), ACT.Gelu_apprx_tanh, bias=W("f3_b1")[:, k:k + 1]).then_inc(s["hid3_ready"], 1)

                    def turns(g, *args):
                        for b in lanes:
                            g(b, *args)

                    turns(columns_out, G0)
                    for k in range(GNN0_STEPS):
                        for b in lanes:
                            g0_messages(b, k)
                            g0_gates(b, k)
                    for b in lanes:
                        columns_out(b, F0)
                        f0_hidden(b, 0)
                        f0_tanh(b)
                    for e in range(1, EXPERTS):
                        turns(f0_hidden, e)
                    turns(columns_out, G1)
                    turns(g1_project)
                    for t in range(T + 2):
                        if t < T:
                            turns(g1_scores, t)
                        if 1 <= t <= T:
                            turns(g1_exp, t - 1)
                        if t >= 2:
                            turns(g1_turned, t - 2)
                    turns(g1_elu)
                    turns(columns_out, F1)
                    for t in range(T + 1):
                        if t < T:
                            turns(f1_exp, t)
                        if t >= 1:
                            turns(f1_turned, t - 1)
                    turns(f1_project)
                    turns(f1_attend)
                    turns(columns_out, G2)
                    turns(g2_project)
                    for b in lanes:
                        columns_out(b, F2)
                        f2_project(b)
                        f2_softplus(b)
                        f2_gate(b)
                    f2_silu(0)
                    f2_log(0)
                    f2_silu(1)
                    f2_log(1)
                    f2_rows(0)
                    f2_decays(0)
                    f2_rows(1)
                    f2_decays(1)
                    turns(f2_square)
                    turns(columns_out, G3)
                    for layer in range(2):
                        turns(g3_project, layer)
                        for n in range(T * AH + 2):
                            for b in lanes:
                                if n < T * AH:
                                    g3_exp(b, layer, n)
                                if n >= 2 and n % 2:
                                    g3_turned(b, layer, n - 2)
                        turns(g3_gather, layer)
                    turns(columns_out, F3)
                    for k in range(FH // P):
                        turns(f3_hidden, k)

                @block.vector
                def _(v):
                    own = Steps(v, s["v_step"])

                    def tt(o, a, c, op):
                        return v.tensor_tensor(o, a, c, op)

                    def ts(o, a, s1, op0, s2=None, op1=ALU.bypass, **k):
                        return v.tensor_scalar(o, a, s1, s2, op0, op1, **k)

                    def stt(o, a, s1, c, op0, op1, **k):
                        return v.scalar_tensor_tensor(out=o, in0=a, scalar=s1, in1=c, op0=op0, op1=op1, **k)

                    def tiles(ap, n=T):
                        return ap.rearrange("p (t d) -> p t d", t=n)

                    def layernorm(b, n, src, column):
                        for t in range(T):
                            last = v.bn_stats(stats[b][:, t, :], src[:, t, 0:D])
                        own(last)
                        own.wait()
                        for t in range(T):
                            last = v.bn_aggr(mv[b][:, t, :], stats[b][:, t, :])
                        own(last)
                        own.wait()
                        ts(ve[b][:, :], mv[b][:, :, 1], EPS, ALU.add).then_inc(s[f"var_ready{b}"], 1)
                        v.wait_ge(s[f"rstd_ready{b}"], n + 1)
                        for t in range(T):
                            last = ts(XN[b][:, t, 0:D], src[:, t, 0:D], mv[b][:, t, 0:1], ALU.subtract, rstd[b][:, t:t + 1], ALU.mult)
                        if column is None:
                            own(last)
                        else:
                            last.then_inc(s["xn_ready"], 1)

                    def new_x(b, k, ins):
                        ins.then_inc(s["x_new"], 1)
                        v.wait_ge(s["x_new"], nth(k, b))

                    def g0_start(b):
                        layernorm(b, 0, XIN[b], G0)

                    def g0_masks(b):
                        ts(AF[b][:, :, :], ADJ[b][:, :, :], 0, ALU.not_equal)
                        ts(NM[b][:, :, :], ADJ[b][:, :, :], 0, ALU.is_gt, 1.0, ALU.subtract).then_inc(s["masks_ready"], 1)

                    def g0_messages(b, k):
                        v.wait_ge(s["aggr_psum"], nth(k, b))
                        v.tensor_copy(cut(b, G0_AG, N), ps(b, 1)).then_inc(s["aggr_ready"], 1)

                    def g0_gates(b, k):
                        h, r, z, u = XT[b][:, :], cut(b, G0_R, N), cut(b, G0_Z, N), cut(b, G0_U, N)
                        v.wait_ge(s["r_ready"], nth(k, b))
                        v.wait_ge(s["n_psum"], nth(k, b))
                        own(stt(u, ps(b, 0), W("g0_bhh")[:, 2:3], r, ALU.add, ALU.mult))
                        own.wait()
                        tt(u, u, ps(b, 1), ALU.add).then_inc(s["u_ready"], 1)
                        v.wait_ge(s["n_ready"], nth(k, b))
                        own(tt(r, h, u, ALU.subtract))
                        own.wait()
                        own(tt(r, r, z, ALU.mult))
                        own.wait()
                        tt(h, u, r, ALU.add).then_inc(s["h_ready"], 1)

                    def g0_end(b):
                        v.wait_ge(s["h_back"], b + 1)
                        new_x(b, 0, tt(X[b][:, :, :], XIN[b][:, :, :], tiles(ps(b, 0)), ALU.add))

                    def f0_start(b):
                        layernorm(b, 1, X[b], None)
                        own.wait()
                        layernorm(b, 2, XN[b], F0)

                    def f0_gate(b):
                        te = T * EXPERTS
                        lg, sel, ls, th = cut(b, F0_LG, te), cut(b, F0_SEL, te), cut(b, F0_LS, te), cut(b, F0_TH, te)
                        gt, eq, rk, sm, gate = cut(b, F0_GT, 256), cut(b, F0_EQ, 256), cut(b, F0_RK, te), cut(b, F0_S, T), cut(b, F0_GATE, te)
                        full = [P, T, EXPERTS, EXPERTS]
                        v.wait_ge(s["logit_psum"], b + 1)
                        own(tt(tiles(lg), tiles(ps(b, 3, te)), spread(W("f0_br"), 1, [P, T, EXPERTS]), ALU.add))
                        own.wait()
                        rivals, mine = spread(tiles(lg), 2, full), spread(tiles(lg), 3, full)
                        g4, e4 = (a.rearrange("p (t e f) -> p t e f", t=T, e=EXPERTS) for a in (gt, eq))
                        tt(g4, rivals, mine, ALU.is_gt)
                        own(tt(e4, rivals, mine, ALU.is_equal))
                        own.wait()
                        before = spread(W("before"), 1, [P, T, EXPERTS * EXPERTS])
                        own(tt(tiles(eq), tiles(eq), before, ALU.mult))
                        own.wait()
                        own(tt(gt, gt, eq, ALU.add))
                        own.wait()
                        own(v.tensor_reduce(tiles(rk), g4, AX, ALU.add))
                        own.wait()
                        own(ts(sel, rk, 1.5, ALU.is_lt))
                        own.wait()
                        own(tt(ls, lg, sel, ALU.mult))
                        own.wait()
                        own(v.tensor_reduce(sm, tiles(ls), AX, ALU.add))
                        own.wait()
                        stt(tiles(th), spread(sm, 2, [P, T, EXPERTS]), -0.5, tiles(lg), ALU.mult, ALU.add).then_inc(s["half_gap"], 1)

                    def f0_gate_end(b):
                        te = T * EXPERTS
                        sel, th, gate = cut(b, F0_SEL, te), cut(b, F0_TH, te), cut(b, F0_GATE, te)
                        v.wait_ge(s["gate_tanh"], b + 1)
                        own(ts(th, th, 0.5, ALU.mult, 0.5, ALU.add))
                        own.wait()
                        tt(gate, th, sel, ALU.mult).then_inc(s["gate_ready"], 1)

                    def f0_gate_columns(b):
                        v.wait_ge(s["gT_psum"], b + 1)
                        v.tensor_copy(cut(b, F0_GATET, N, EXPERTS), ps(b, 3, N, EXPERTS)).then_inc(s["gT_ready"], 1)

                    def f0_bias(b):
                        v.wait_ge(s["combined"], nth(GATE_TURN, b))
                        v.wait_ge(s["b2_psum"], b + 1)
                        tt(X[b][:, :, :], X[b][:, :, :], tiles(ps(b, 2)), ALU.add).then_inc(s["b2_added"], 1)

                    def f0_combine(b, e):
                        v.wait_ge(s["y_psum"], nth(e, b))
                        if e == 0:
                            v.wait_ge(s["gate_ready"], b + 1)
                        elif e == GATE_TURN + 1:
                            v.wait_ge(s["b2_added"], b + 1)
                        else:
                            v.wait_ge(s["combined"], nth(e - 1, b))
                        for t in range(T):
                            x = X[b][:, t, :]
                            last = stt(x, ps(b, 3 - e % 2, D, P, t * D), cut(b, F0_GATE + t * EXPERTS + e, 1), x, ALU.mult, ALU.add)
                        if e < EXPERTS - 1:
                            last.then_inc(s["combined"], 1)
                        else:
                            new_x(b, 1, last)

                    def g1_project(b):
                        v.wait_ge(s["wh_psum"], b + 1)
                        v.tensor_copy(cut(b, G1_F, 2 * T), ps(b, 2, 2 * T)).then_inc(s["f_ready"], 1)

                    def g1_scores(b, t):
                        z, u = cut(b, G1_Z + t % 2 * N, N), cut(b, G1_U + t % 2 * N, N)
                        v.wait_ge(s["z1_ready"], nth(t, b))
                        if t >= 2:
                            v.wait_ge(s["p1_ready"], nth(t - 2, b))
                        own(stt(u, z, 0.2, z, ALU.mult, ALU.max))
                        own.wait()
                        v.tensor_reduce(cut(b, G1_MX + t, 1), u, AX, ALU.max, negate=True).then_inc(s["u1_ready"], 1)

                    def g1_end(b):
                        ri = cut(b, G1_RI, T)
                        v.wait_ge(s["p1_ready"], nth(T - 1, b))
                        own(v.reciprocal(ri, cut(b, G1_SUM, T)))
                        own.wait()
                        v.wait_ge(s["o1_psum"], b + 1)
                        for t in range(T):
                            ts(cut(b, G1_POS + t * D, D), ps(b, 0, D, P, t * D), ri[:, t:t + 1], ALU.mult, 0.0, ALU.max)
                        for t in range(T):
                            last = ts(cut(b, G1_NEG + t * D, D), ps(b, 0, D, P, t * D), ri[:, t:t + 1], ALU.mult, 0.0, ALU.min)
                        last.then_inc(s["o1_neg"], 1)
                        v.wait_ge(s["o1_neg"], b + 1)
                        own(tt(X[b][:, :, :], X[b][:, :, :], tiles(cut(b, G1_POS, N)), ALU.add))
                        own.wait()
                        v.wait_ge(s["elu_exp"], b + 1)
                        new_x(b, 2, stt(X[b][:, :, :], tiles(cut(b, G1_NEG, N)), -1.0, X[b][:, :, :], ALU.add, ALU.add))

                    def heads(ap):
                        return ap.rearrange("p (h g) -> p h g", g=SG)

                    def f1_logits(b, t):
                        sw, mx = cut(b, F1_SW + t * N, N), cut(b, F1_MX + t * SH, SH)
                        v.wait_ge(s["sl_psum"], nth(t, b))
                        tt(sw, ps(b, t % 2), M("f1_bs"), ALU.add).then_inc(s["sl_biased"], 1)
                        v.wait_ge(s["sl_biased"], nth(t, b))
                        own(v.tensor_reduce(mx, heads(sw), AX, ALU.max))
                        own.wait()
                        tt(heads(sw), heads(sw), spread(mx, 2, [P, SH, SG]), ALU.subtract).then_inc(s["sl_shifted"], 1)

                    def f1_sums(b, t):
                        sw, sm, ri = cut(b, F1_SW + t * N, N), cut(b, F1_SUM + t * SH, SH), cut(b, F1_RI + t * SH, SH)
                        v.wait_ge(s["sl_exp"], nth(t, b))
                        own(v.tensor_reduce(sm, heads(sw), AX, ALU.add))
                        own.wait()
                        v.reciprocal(ri, sm).then_inc(s["sl_rsum"], 1)

                    def f1_tokens(b):
                        den, rd, rat = cut(b, F1_DEN, PAIRS), cut(b, F1_RD, PAIRS), cut(b, F1_RAT, PAIRS)
                        v.wait_ge(s["tok_psum"], nth(0, b))
                        for k in range(PAIRS):
                            last = ts(den[:, k:k + 1], ps(b, k // 2, 1, P, k % 2 * 256 + D), 1e-5, ALU.add)
                        own(last)
                        own.wait()
                        own(v.reciprocal(rd, den))
                        own.wait()
                        for k in range(PAIRS):
                            ts(cut(b, F1_SN + k * D, D), ps(b, k // 2, D, P, k % 2 * 256), rd[:, k:k + 1], ALU.mult)
                            last = ts(rat[:, k:k + 1], ps(b, k // 2, 1, P, k % 2 * 256 + D), rd[:, k:k + 1], ALU.mult)
                        own(last)
                        own.wait()
                        rm = cut(b, F1_RM, PAIRS * SH).rearrange("p (k h) -> p k h", h=SH)
                        tt(rm, W("own_head").rearrange("p (k h) -> p k h", h=SH), spread(rat, 2, [P, PAIRS, SH]), ALU.mult)\
                            .then_inc(s["sn_ready"], 1)

                    def f1_project(b):
                        v.wait_ge(s["ratio_psum"], b + 1)
                        v.tensor_copy(cut(b, F1_RR, N, SH), ps(b, 3, N, SH)).then_inc(s["ratio_ready"], 1)
                        v.wait_ge(s["tk_psum"], b + 1)
                        v.tensor_copy(cut(b, F1_TK, N, SD), ps(b, 0, N, SD)).then_inc(s["tk_ready"], 1)

                    def f1_attend(b):
                        mx, e = cut(b, F1_EMX, PAIRS), cut(b, F1_E, PAIRS * SG)
                        v.wait_ge(s["sc_psum"], b + 1)
                        own(v.tensor_reduce(mx, heads(ps(b, 0, PAIRS * SG)), AX, ALU.max))
                        own.wait()
                        tt(heads(e), heads(ps(b, 0, PAIRS * SG)), spread(mx, 2, [P, PAIRS, SG]), ALU.subtract).then_inc(s["sc_shifted"], 1)

                    def f1_mix(b):
                        e, es, er = cut(b, F1_E, PAIRS * SG), cut(b, F1_ES, PAIRS), cut(b, F1_ER, PAIRS)
                        v.wait_ge(s["sc_exp"], b + 1)
                        own(v.tensor_reduce(es, heads(e), AX, ALU.add))
                        own.wait()
                        own(v.reciprocal(er, es))
                        v.wait_ge(s["eT_psum"], b + 1)
                        v.tensor_copy(cut(b, F1_ET, N, SG), ps(b, 1, N, SG)).then_inc(s["eT_ready"], 1)
                        own.wait()
                        v.wait_ge(s["u_psum"], b + 1)
                        tt(tiles(cut(b, F1_U, N), PAIRS), tiles(ps(b, 0), PAIRS), spread(er, 2, [P, PAIRS, D]), ALU.mult).then_inc(s["us_ready"], 1)

                    def f1_end(b):
                        v.wait_ge(s["so_psum"], b + 1)
                        v.wait_ge(s["bout_added"], b + 1)
                        new_x(b, 3, tt(X[b][:, :, :], X[b][:, :, :], tiles(ps(b, 1)), ALU.add))

                    def g2_end(b):
                        up, o = cut(b, G2_UP, N), cut(b, G2_O, N)
                        rd, pos, c = cut(b, G2_RD, T), cut(b, G2_POS, T), cut(b, G2_C, T)
                        v.wait_ge(s["upd_psum"], b + 1)
                        own(tt(tiles(up), tiles(ps(b, 2)), spread(W("g2_bias"), 1, [P, T, D]), ALU.add))
                        v.wait_ge(s["msg_psum"], b + 1)
                        for j in range(T):
                            deg = ps(b, 3 * (j // 2), 1, P, j % 2 * 256 + D)
                            ts(rd[:, j:j + 1], deg, 1.0, ALU.max)
                            last = ts(pos[:, j:j + 1], deg, 0.0, ALU.is_gt)
                        own(last)
                        own.wait()
                        own(v.reciprocal(rd, rd))
                        own.wait()
                        own(tt(c, rd, pos, ALU.mult))
                        own.wait()
                        for j in range(T):
                            last = stt(o[:, tile(j)], ps(b, 3 * (j // 2), D, P, j % 2 * 256), c[:, j:j + 1], up[:, tile(j)], ALU.mult, ALU.add)
                        own(last)
                        own.wait()
                        new_x(b, 4, stt(X[b][:, :, :], tiles(o), 0.0, X[b][:, :, :], ALU.max, ALU.add))

                    def small(b, k):
                        return cut(b, F2_S + 16 * k, 16)

                    def f2_conv(b):
                        cin = cut(b, F2_CIN, 3 * CW).rearrange("p (k n) -> p k n", k=3)
                        v.memset(cin[:, :, 0:PAD], 0.0)
                        v.wait_ge(s["dt_psum"], b + 1)
                        own(tt(tiles(small(b, 0)), tiles(ps(b, 0, 16)), spread(W("f2_dtb"), 1, [P, T, MH]), ALU.add))
                        own.wait()
                        stt(small(b, 1), small(b, 0), -1.0, small(b, 0), ALU.mult, ALU.min).then_inc(s["dt_v"], 1)
                        v.wait_ge(s["xbc_ready"], b + 1)
                        for tap in range(PAD):
                            for k in (2, 0, 1):
                                xs, w = cut(b, F2_XS + k * N, N), W("f2_convw")[:, k * TAPS + tap:k * TAPS + tap + 1]
                                last = stt(xs, cin[:, k, tap:tap + N], w, xs, ALU.mult, ALU.add)
                                if tap == PAD - 1:
                                    last.then_inc(s["conv_ready"], 1)
                            if tap < PAD - 1:
                                own(last)
                                own.wait()

                    def f2_softplus(b):
                        v.wait_ge(s["dt_e"], b + 1)
                        ts(small(b, 2), small(b, 1), 1.0, ALU.add).then_inc(s["dt_u"], 1)

                    def f2_decay(b):
                        vv, e, u, ln, d, z, q, dt, da = (small(b, k) for k in range(9))
                        v.wait_ge(s["dt_u"], b + 1)
                        ts(d, u, -1.0, ALU.add, 1e-30, ALU.max)
                        own(stt(z, u, 1.0, e, ALU.is_equal, ALU.mult))
                        own.wait()
                        own(v.reciprocal(d, d))
                        own(stt(z, vv, 0.0, z, ALU.max, ALU.add))
                        own.wait()
                        own(tt(d, d, e, ALU.mult))
                        own.wait()
                        v.wait_ge(s["dt_ln"], b + 1)
                        own(tt(q, d, ln, ALU.mult))
                        own.wait()
                        own(tt(dt, q, z, ALU.add))
                        own.wait()
                        tt(tiles(da), tiles(dt), spread(M("f2_nega"), 1, [P, T, MH]), ALU.mult).then_inc(s["da_ready"], 1)

                    def f2_cumulate(b):
                        v.wait_ge(s["ac_psum"], b + 1)
                        v.tensor_copy(small(b, 9), ps(b, 0, 16)).then_inc(s["ac_ready"], 1)

                    def f2_turn(b):
                        dt = small(b, 7)
                        v.wait_ge(s["xs_T"], b + 1)
                        xd = cut(b, F2_XD, T * MI).rearrange("p (c h d) -> p c h d", c=T, h=MH)
                        for k in range(2):
                            mine = tiles(dt)[:, :, 2 * k:2 * k + 2]
                            tt(xd[:, :, 2 * k:2 * k + 2, :], ps(b, 1 + k).rearrange("p (c h d) -> p c h d", c=T, h=2),
                               spread(mine, 3, [P, T, 2, MD]), ALU.mult)
                        bb = cut(b, F2_BB, N).rearrange("p (c q n) -> p c q n", c=T, q=2)
                        b_rows = tiles(ps(b, 3))[:, :, 0:MS]
                        v.tensor_copy(bb, spread(b_rows, 2, [P, T, 2, MS])).then_inc(s["xd_ready"], 1)
                        v.wait_ge(s["gt_psum"], b + 1)
                        tt(tiles(cut(b, F2_GM, N)), tiles(ps(b, 0)), spread(W("tri"), 1, [P, T, P]), ALU.mult).then_inc(s["gm_ready"], 1)

                    def f2_rows(b):
                        for n, c in enumerate((1, 2, 3, 0)):
                            v.wait_ge(s["re_ready"], T * b + n + 1)
                            for h in range(MH):
                                a = F2_S + 9 * 16 + c * MH + h
                                last = ts(cut(b, F2_E + (c * MH + h) * P, P), ps(b, c, P, P, h * P), SC[b][:, a:a + 1], ALU.subtract, 0.0, ALU.min)
                            last.then_inc(s["dd_ready"], 1)
                        own(v.memset(cut(b, F2_PV, (T - 1) * MI), 0.0))

                    def f2_weigh(b):
                        e = cut(b, F2_E, T * N)
                        v.wait_ge(s["e_ready"], 2 * b + 2)
                        n = (T - 1) * MH
                        xd, xdd = (cut(b, at, n * MD).rearrange("p (h d) -> p h d", d=MD) for at in (F2_XD, F2_XDD))
                        to_end = e.rearrange("p (h n) -> p h n", n=P)[:, 0:n, P - 1:P]
                        tt(xdd, xd, to_end.to_broadcast([P, n, MD]), ALU.mult).then_inc(s["xdd_ready"], 1)
                        v.wait_ge(s["xdd_ready"], b + 1)
                        for q in range(2):
                            e4 = cut(b, F2_E + 2 * q * N, 2 * N).rearrange("p (c h n) -> p c h n", c=2, h=MH)
                            gm = cut(b, F2_GM + 2 * q * P, 2 * P).rearrange("p (c n) -> p c n", c=2)
                            tt(e4, e4, spread(gm, 2, [P, 2, MH, P]), ALU.mult).then_inc(s["mt_ready"], 1)

                    def f2_state(b):
                        own.wait()
                        for c in range(T - 1):
                            v.wait_ge(s["st_psum"], (T - 1) * b + (T - 1 if c else 1))
                            if c:
                                v.wait_ge(s["pv_ready"], (T - 1) * b + c)
                            for half in range(2):
                                rows = slice(half * MS, (half + 1) * MS)
                                for k in range(2):
                                    at = F2_PV + c * MI + k * P + half * MD
                                    st = SC[b][rows, at:at + MD]
                                    at_psum = (c + 1) % 2 * MI + k * P + half * MD
                                    more = PS[b][(c + 1) // 2][rows, at_psum:at_psum + MD]
                                    if c == 0:
                                        last = v.tensor_copy(st, more)
                                    else:
                                        h = 2 * k + half
                                        last = stt(st, SC[b][rows, at - MI:at - MI + MD], AF[b][rows, c, h * P + P - 1:h * P + P], more, ALU.mult, ALU.add)
                            last.then_inc(s["pv_ready"], 1)

                    def f2_finish(b):
                        v.wait_ge(s["yt_psum"], b + 1)
                        for k in range(2):
                            last = stt(cut(b, F2_YG + k * N, N), cut(b, F2_XS + k * N, N), W("f2_d")[:, k:k + 1], ps(b, 2 + k), ALU.mult, ALU.add)
                        own(last)
                        own.wait()
                        tt(cut(b, F2_YG, 2 * N), cut(b, F2_YG, 2 * N), cut(b, F2_Z, 2 * N), ALU.mult).then_inc(s["yg_ready"], 1)

                    def f2_end(b):
                        v.wait_ge(s["ym_psum"], b + 1)
                        ts(small(b, 10)[:, 0:T], ps(b, 1, T), 1.0 / MI, ALU.mult, EPS, ALU.add).then_inc(s["ms_ready"], 1)
                        v.wait_ge(s["rs_ready"], b + 1)
                        v.wait_ge(s["blin_added"], b + 1)
                        for t in range(T):
                            x = X[b][:, t, :]
                            last = stt(x, ps(b, 0, D, P, t * D), small(b, 11)[:, t:t + 1], x, ALU.mult, ALU.add)
                        new_x(b, 5, last)

                    def g3_project(b, layer):
                        v.wait_ge(s["qkv_psum"], nth(layer, b))
                        ts(cut(b, G3_K, N), ps(b, 2), W(f"g3_bk{layer}"), ALU.add)
                        tt(tiles(cut(b, G3_V, N)), tiles(ps(b, 3)), spread(W(f"g3_bv{layer}"), 1, [P, T, D]), ALU.add).then_inc(s["kv_ready"], 1)

                    def g3_max(b, layer, n):
                        k = layer * T * AH + n
                        v.wait_ge(s["att_psum"], nth(k, b))
                        v.tensor_reduce(cut(b, G3_MX + n, 1), ps(b, n % 2), AX, ALU.max, negate=True).then_inc(s["att_max"], 1)

                    def g3_sum(b, layer, n):
                        k = layer * T * AH + n
                        v.wait_ge(s["att_exp"], nth(k, b))
                        v.reciprocal(cut(b, G3_RI + n, 1), cut(b, G3_SUM + n, 1)).then_inc(s["att_rsum"], 1)

                    def g3_turned(b, layer, n):
                        k = layer * T * AH + n
                        v.wait_ge(s["pT_psum"], nth(k, b))
                        if n == 2 * AH:
                            v.wait_ge(s["pv_psum"], nth(2 * layer, b))
                        pt = weights_T(b, n % AH).rearrange("p (j n) -> p j n", j=T)
                        v.tensor_copy(pt[:, :, tile(n // AH % 2)], ps(b, 2).rearrange("p (j n) -> p j n", j=T)).then_inc(s["pT_even"], 1)

                    def g3_end(b):
                        o = cut(b, G3_O, N)
                        v.wait_ge(s["g3_psum"], b + 1)
                        own(tt(tiles(o), tiles(ps(b, 0)), spread(W("g3_bout"), 1, [P, T, D]), ALU.add))
                        own.wait()
                        new_x(b, 6, stt(X[b][:, :, :], tiles(o), 0.0, X[b][:, :, :], ALU.max, ALU.add))

                    def f3_router(b):
                        v.wait_ge(s["w3_psum"], b + 1)
                        ts(cut(b, F3_W, T), ps(b, 3, T), W("f3_br"), ALU.add).then_inc(s["w3_ready"], 1)

                    def f3_rank(b):
                        w, cnt, sc = cut(b, F3_W, T), cut(b, F3_CNT, 3 * T), cut(b, F3_SC, T)
                        v.wait_ge(s["w3_ready"], b + 1)
                        own(v.memset(cnt, 0.0))
                        own.wait()
                        v.wait_ge(s["row3_psum"], b + 1)
                        for t in range(T):
                            cmp = cut(b, F3_CMP + t * (N + P), N + P)
                            if t:
                                ts(cmp[:, 0:t * P], ps(b, 2, t * P), w[:, t:t + 1], ALU.is_ge, None, ALU.add, accum_out=cnt[:, 3 * t:3 * t + 1])
                            ts(cmp[:, t * P:N], ps(b, 2, N - t * P, P, t * P), w[:, t:t + 1], ALU.is_gt, None, ALU.add,
                               accum_out=cnt[:, 3 * t + 1:3 * t + 2])
                            last = stt(cmp[:, N:N + P], ps(b, 2, P, P, t * P), w[:, t:t + 1], W("lower"), ALU.is_equal, ALU.mult,
                                       accum_out=cnt[:, 3 * t + 2:3 * t + 3])
                        own(last)
                        own.wait()
                        own(v.tensor_reduce(sc, cnt.rearrange("p (t k) -> p t k", t=T), AX, ALU.add))
                        own.wait()
                        stt(sc, sc, KEPT - 0.5, w, ALU.is_lt, ALU.mult).then_inc(s["scale3_ready"], 1)

                    def f3_end(b):
                        y = cut(b, F3_Y, N)
                        v.wait_ge(s["y3_psum"], b + 1)
                        own(tt(tiles(y), tiles(ps(b, 3)), spread(W("f3_b2"), 1, [P, T, D]), ALU.add))
                        own.wait()
                        v.wait_ge(s["scale3_ready"], b + 1)
                        v.wait_ge(s["xn_added"], b + 1)
                        for t in range(T):
                            x = X[b][:, t, :]
                            last = stt(x, y[:, tile(t)], cut(b, F3_SC + t, 1), x, ALU.mult, ALU.add)
                        last.then_inc(s["x_new"], 1)

                    def turns(g, *args):
                        for b in lanes:
                            g(b, *args)

                    turns(g0_start)
                    turns(g0_masks)
                    for k in range(GNN0_STEPS):
                        for b in lanes:
                            g0_messages(b, k)
                            if k == GNN0_STEPS - 1 and b:
                                g0_end(b - 1)
                                f0_start(b - 1)
                            g0_gates(b, k)
                    f0_gate(0)
                    g0_end(1)
                    f0_start(1)
                    f0_gate_end(0)
                    f0_gate(1)
                    f0_gate_end(1)
                    for e in range(EXPERTS - 1):
                        if e == GATE_TURN:
                            turns(f0_gate_columns)
                        turns(f0_combine, e)
                        if e == GATE_TURN:
                            turns(f0_bias)
                    for b in lanes:
                        f0_combine(b, EXPERTS - 1)
                        layernorm(b, 3, X[b], G1)
                    turns(g1_project)
                    for t in range(T):
                        turns(g1_scores, t)
                    for b in lanes:
                        g1_end(b)
                        layernorm(b, 4, X[b], F1)
                    for t in range(T + 1):
                        if t < T:
                            turns(f1_logits, t)
                        if t >= 1:
                            turns(f1_sums, t - 1)
                    turns(f1_tokens)
                    turns(f1_project)
                    turns(f1_attend)
                    turns(f1_mix)
                    for b in lanes:
                        f1_end(b)
                        layernorm(b, 5, X[b], G2)
                    for b in lanes:
                        g2_end(b)
                        layernorm(b, 6, X[b], F2)
                    for b in lanes:
                        f2_conv(b)
                        f2_softplus(b)
                    turns(f2_decay)
                    f2_cumulate(0)
                    f2_turn(0)
                    f2_cumulate(1)
                    f2_turn(1)
                    f2_rows(0)
                    f2_weigh(0)
                    f2_rows(1)
                    f2_state(0)
                    f2_weigh(1)
                    f2_state(1)
                    turns(f2_finish)
                    for b in lanes:
                        f2_end(b)
                        layernorm(b, 7, X[b], G3)
                    for layer in range(2):
                        turns(g3_project, layer)
                        for n in range(T * AH + 2):
                            for b in lanes:
                                if n < T * AH:
                                    g3_max(b, layer, n)
                                if 1 <= n <= T * AH:
                                    g3_sum(b, layer, n - 1)
                                if n >= 2 and n % 2 == 0:
                                    g3_turned(b, layer, n - 2)
                    for b in lanes:
                        g3_end(b)
                        layernorm(b, 8, X[b], F3)
                    turns(f3_router)
                    turns(f3_rank)
                    turns(f3_end)

                @block.gpsimd
                def _(g):
                    own = Steps(g, s["g_step"])

                    def root(b, n):
                        g.wait_ge(s[f"var_ready{b}"], n + 1)
                        g.tensor_tensor(rstd[b][:, :], ve[b][:, :], minus_half[:, :], ALU.pow).then_inc(s[f"rstd_ready{b}"], 1)

                    def add_to_x(b, row, done):
                        g.tensor_tensor(X[b][:, :, :], X[b][:, :, :], spread(row, 1, [P, T, D]), ALU.add).then_inc(done, 1)

                    def f1_normalise(b, t):
                        sw = cut(b, F1_SW + t * N, N).rearrange("p (h g) -> p h g", g=SG)
                        g.wait_ge(s["sl_rsum"], nth(t, b))
                        g.tensor_tensor(sw, sw, spread(cut(b, F1_RI + t * SH, SH), 2, [P, SH, SG]), ALU.mult).then_inc(s["sw_ready"], 1)

                    def g2_adjacency(b):
                        g.wait_ge(s["aggr_psum"], nth(GNN0_STEPS - 1, b))
                        g.tensor_copy(AF[b][:, :, :], ADJ[b][:, :, :]).then_inc(s["adjf_ready"], 1)

                    def f2_reading(b):
                        g.wait_ge(s["re_ready"], T * b + T)
                        g.wait_ge(s[f"cc_ready{b}"], 32)
                        if b == 0:
                            g.wait_ge(s["blin_added"], LANES)
                        else:
                            g.wait_ge(s["ce_ready"], b)
                        re = AF[b][:, :, :].rearrange("p c (h n) -> p c h n", h=MH)
                        for half in range(2):
                            rows = slice(half * MS, (half + 1) * MS)
                            cc = SC[b][rows, F2_CC + P:F2_CC + T * P].rearrange("p (c n) -> p c n", c=T - 1)
                            ce = SC[b][rows, F2_CE:F2_CE + (T - 1) * MI].rearrange("p (c k n) -> p c k n", c=T - 1, k=2)
                            own_half = g.tensor_tensor(ce, re[rows, 1:T, half::2, :], spread(cc, 2, [MS, T - 1, 2, P]), ALU.mult)
                            if half == 0:
                                own(own_half)
                                own.wait()
                            else:
                                own_half.then_inc(s["ce_ready"], 1)

                    def g3_normalise(b, layer, n):
                        k = layer * T * AH + n
                        p = cut(b, G3_P + n % G3_RING * N, N)
                        g.wait_ge(s["att_rsum"], nth(k, b))
                        g.tensor_scalar(p, p, cut(b, G3_RI + n, 1), 1.0, ALU.mult, ALU.mult).then_inc(s["att_p"], 1)

                    for b in lanes:
                        root(b, 0)
                    for b in lanes:
                        root(b, 1)
                        root(b, 2)
                    for b in lanes:
                        g2_adjacency(b)
                    for b in lanes:
                        root(b, 3)
                    for b in lanes:
                        root(b, 4)
                    for b in lanes:
                        g.wait_ge(s["xn_ready"], nth(F1, b))
                        add_to_x(b, W("f1_bout"), s["bout_added"])
                    for t in range(T):
                        for b in lanes:
                            f1_normalise(b, t)
                    for b in lanes:
                        root(b, 5)
                    for b in lanes:
                        root(b, 6)
                    for b in lanes:
                        g.wait_ge(s["xn_ready"], nth(F2, b))
                        add_to_x(b, W("f2_blin"), s["blin_added"])
                    for b in lanes:
                        f2_reading(b)
                    g.wait_ge(s["ce_ready"], LANES)
                    for b in lanes:
                        g.wait_ge(s["ms_ready"], b + 1)
                        g.tensor_tensor(cut(b, F2_S + 11 * 16, T), cut(b, F2_S + 10 * 16, T), minus_half[:, :], ALU.pow).then_inc(s["rs_ready"], 1)
                        root(b, 7)
                    for b in lanes:
                        g.wait_ge(s["xn_ready"], nth(G3, b))
                        g.memset(cut(b, G3_QZ, AH * N), 0.0).then_inc(s["qz_zero"], 1)
                    for layer in range(2):
                        for n in range(T * AH):
                            for b in lanes:
                                g3_normalise(b, layer, n)
                    for b in lanes:
                        root(b, 8)
                    for b in lanes:
                        g.wait_ge(s["xn_ready"], nth(F3, b))
                        g.tensor_tensor(X[b][:, :, :], X[b][:, :, :], XN[b][:, :, 0:D], ALU.add).then_inc(s["xn_added"], 1)

            nc.gpsimd.sem_clear(range(first_sem, last_sem + 1))
            nc.all_engine_barrier()


def lay_out(inputs):
    def rows(a, n=P):
        return np.broadcast_to(np.asarray(a, np.float32).reshape(1, -1), (n, np.asarray(a).size))

    def cols(a):
        return np.asarray(a, np.float32).reshape(-1, P).T

    def k_tiles(a):
        a = np.asarray(a, np.float32)
        return a.reshape(-1, P, a.shape[-1]).transpose(1, 0, 2).reshape(P, -1)

    g = {k: np.asarray(v) for k, v in inputs.items()}
    index = np.arange(P)
    parts = {
        "ident": np.eye(P), "tri": index[:, None] <= index[None, :], "lower": index[:, None] > index[None, :],
        "ones": np.ones((P, 1)),
        "before": rows(np.arange(EXPERTS)[None, :] < np.arange(EXPERTS)[:, None]),
        "own_head": (2 * np.arange(PAIRS)[None, :, None] + (index // SG)[:, None, None]
                     == np.arange(SH)[None, None, :]).reshape(P, -1),
        "g0_w": g["L0_gnn_weight"].transpose(1, 0, 2).reshape(D, -1),
        "g0_wih": g["L0_gnn_w_ih"].T, "g0_whh": g["L0_gnn_w_hh"].T,
        "g0_bih": cols(g["L0_gnn_b_ih"]), "g0_bhh": cols(g["L0_gnn_b_hh"]),
        "f0_gamma": cols(g["L0_ffn_gamma"]), "f0_beta": cols(g["L0_ffn_beta"]),
        "f0_wr": g["L0_ffn_Wr"], "f0_br": rows(g["L0_ffn_br"]),
        "f0_w1": g["L0_ffn_W1"].transpose(1, 0, 2).reshape(D, -1), "f0_b1": cols(g["L0_ffn_b1"]),
        "f0_w2": k_tiles(g["L0_ffn_W2"].reshape(EXPERTS * EXPERT_H, D)), "f0_b2": g["L0_ffn_b2"],
        "g1_w": g["L1_gnn_W"], "g1_wT": g["L1_gnn_W"].T, "g1_a": cols(g["L1_gnn_a"]),
        "f1_wfx": g["L1_ffn_W_fx"], "f1_bfx": g["L1_ffn_b_fx"].reshape(SH, SD), "f1_bout": rows(g["L1_ffn_b_out"]),
        "f1_wxT": g["L1_ffn_W_x"].reshape(D, SH, SD).transpose(2, 1, 0).reshape(SD, -1),
        "f1_wslice": g["L1_ffn_W_slice"], "f1_bx": g["L1_ffn_b_x"].reshape(SH, SD).T, "f1_bslice": rows(g["L1_ffn_b_slice"]),
        "f1_temp": rows(g["L1_ffn_temperature"]),
        "f1_wqT": g["L1_ffn_W_q"].T, "f1_wkT": g["L1_ffn_W_k"].T, "f1_wvT": g["L1_ffn_W_v"].T,
        "f1_wout": g["L1_ffn_W_out"].reshape(SH, SD, D).transpose(1, 0, 2).reshape(SD, -1),
        "g2_wmsg": g["L2_gnn_W_msg"], "g2_wupd": g["L2_gnn_W_upd"], "g2_bias": rows(g["L2_gnn_bias"]),
        "f2_win": g["L2_ffn_W_in"],
        "f2_convw": g["L2_ffn_conv_w"].reshape(3, P, TAPS).transpose(1, 0, 2).reshape(P, -1), "f2_convb": cols(g["L2_ffn_conv_b"]),
        "f2_dtb": rows(g["L2_ffn_dt_bias"]), "f2_alog": rows(g["L2_ffn_A_log"]),
        "f2_d": cols(np.repeat(g["L2_ffn_D"], MD)), "f2_normw": cols(g["L2_ffn_norm_w"]),
        "f2_woutT": g["L2_ffn_W_out"].T, "f2_wlin": g["L2_ffn_W_lin"], "f2_blin": rows(g["L2_ffn_b_lin"]),
        "g3_wout": k_tiles(g["L3_gnn_Wout"]), "g3_bout": rows(g["L3_gnn_bout"]),
        "f3_wr": g["L3_ffn_wr"], "f3_br": rows(g["L3_ffn_br"]), "f3_w1": g["L3_ffn_w1"], "f3_b1": cols(g["L3_ffn_b1"]),
        "f3_w2": k_tiles(g["L3_ffn_w2"]), "f3_b2": rows(g["L3_ffn_b2"]),
    }
    for n in range(2):
        for q in "qkv":
            parts[f"g3_w{q}{n}"] = k_tiles(g[f"L3_gnn_W{q}{n}"])
        for q in "qk":
            parts[f"g3_b{q}{n}"] = cols(g[f"L3_gnn_b{q}{n}"])
        parts[f"g3_bv{n}"] = rows(g[f"L3_gnn_bv{n}"])
    packs = []
    for table in (WEIGHTS, RAW):
        at, width = columns_of(table)
        pack = np.zeros((P, width), np.float32)
        for name, n_rows, n_cols in table:
            pack[0:n_rows, at[name][0]:at[name][0] + n_cols] = parts[name]
        packs.append(pack)
    return packs


def kernel(**inputs):
    import concourse.bacc as bacc
    from concourse.bass_utils import run_bass_kernel_spmd

    weights, raw = lay_out(inputs)
    arrays = {
        "x": np.ascontiguousarray(inputs["x"]), "adj": np.ascontiguousarray(inputs["adj"]),
        "weights": weights, "raw": raw,
    }
    nc = bacc.Bacc("TRN2", target_bir_lowering=False, num_devices=1)
    aps = [nc.dram_tensor(k, a.shape, mybir.dt.from_np(a.dtype), kind="ExternalInput").ap() for k, a in arrays.items()]
    out = nc.dram_tensor("out", arrays["x"].shape, F32, kind="ExternalOutput").ap()
    build(nc, *aps, out)
    result = run_bass_kernel_spmd(nc, [arrays], core_ids=[0])
    return result.results[0]["out"]
```

```python
from contextlib import ExitStack

import concourse.bass as bass
import numpy as np
from concourse import mybir

F32 = mybir.dt.float32
BF16 = mybir.dt.bfloat16
I32 = mybir.dt.int32
ALU = mybir.AluOpType
ACT = mybir.ActivationFunctionType
AX = mybir.AxisListType.X

P = 128
LANES = 2
D = 128
N = 512
T = N // P
EPS = 1e-5
GNN0_STEPS = 3
EXPERTS, EXPERT_H = 8, 256
F0_LAG, G1_LAG, MID_LAG = 1, 2, 0
MID_STEPS = T + 18
MID_LAGS = [MID_LAG] * MID_STEPS
GATE_TURN = 4
SH, SG, SD = 8, 64, 64
PAIRS = SH // 2
MH, MD, MS = 4, 64, 64
MI = MH * MD
TAPS = 4
AH, AD = 4, 32
FH = 512
KEPT = N // 2 - 1
BIG = 2.0 ** 60
SCRATCH = 9216

WEIGHTS = [
    ("ident", P, P), ("tri", P, P), ("lower", P, P), ("ones", P, P), ("before", P, 64), ("own_head", P, PAIRS * SH),
    ("g0_whh", P, 3 * D), ("g0_bih", P, 3), ("g0_bhh", P, 3),
    ("f0_gamma", P, 1), ("f0_beta", P, 1), ("f0_wr", P, P), ("f0_br", P, EXPERTS),
    ("f0_w1", P, EXPERTS * EXPERT_H), ("f0_b1", P, EXPERTS * 2), ("f0_w2", P, EXPERTS * 2 * D), ("f0_b2", EXPERTS, D),
    ("g1_w", P, D),
    ("f1_wfx", P, SH * SD), ("f1_bfx", SH, SD), ("f1_bout", P, D),
    ("g2_wmsg", P, D), ("g2_wupd", P, D), ("g2_bias", P, D),
    ("f2_win", P, 2 * MI + 2 * MS + MH), ("f2_convw", P, 3 * TAPS), ("f2_convb", P, 3), ("f2_dtb", P, MH),
    ("f2_d", P, 2), ("f2_blin", P, D),
    ("g3_wk0", P, D), ("g3_wv0", P, D), ("g3_wk1", P, 2 * D), ("g3_wv1", P, 2 * D),
    ("g3_bk0", P, 1), ("g3_bk1", P, 1), ("g3_bv0", P, D), ("g3_bv1", P, D), ("g3_wout", P, 3 * D), ("g3_bout", P, D),
    ("f3_wr", P, P), ("f3_br", P, 1), ("f3_w1", P, FH), ("f3_b1", P, FH // P), ("f3_w2", P, FH), ("f3_b2", P, D),
]
RAW = [
    ("g0_wT", P, GNN0_STEPS * D), ("g0_wih", P, 3 * D),
    ("g1_wT", P, D), ("g1_a", P, 2),
    ("f1_wxT", SD, SH * D), ("f1_wslice", SD, SG), ("f1_bx", SD, SH), ("f1_bslice", P, SG), ("f1_temp", P, SH),
    ("f1_wqT", SD, SD), ("f1_wkT", SD, SD), ("f1_wvT", SD, SD), ("f1_wout", SD, SH * D),
    ("f2_woutT", P, MI), ("f2_wlin", P, D), ("f2_normw", P, 2), ("f2_alog", P, MH),
    ("g3_wq0", P, D), ("g3_wq1", P, 2 * D), ("g3_bq0", P, 1), ("g3_bq1", P, 1),
]
MADE = [
    ("g0_wgi", GNN0_STEPS * 3 * D), ("g0_brz", 2), ("g1_wa1", P), ("g1_wa2", P), ("f1_ws", SH * SG), ("f1_wqk", SD),
    ("f1_wvo", SH * D), ("f2_wol", 2 * D), ("f2_nega", MH), ("g3_wq0", D), ("g3_wq1", 2 * D), ("g3_bq0", 1), ("g3_bq1", 1),
    ("f1_rtemp", SH),
]


def columns_of(table):
    at, out = 0, {}
    for entry in table:
        out[entry[0]] = (at, entry[-1])
        at += entry[-1]
    return out, at


class Steps:

    def __init__(self, eng, sem):
        self.eng, self.sem, self.n = eng, sem, 0

    def __call__(self, ins):
        self.n += 1
        ins.then_inc(self.sem, 1)

    def wait(self):
        self.eng.wait_ge(self.sem, self.n)


def nth(k, b, steps=None, lag=0):
    if b == 0:
        return k + 1 + max(0, k - lag)
    return k + 1 + (k + 1 if lag == 0 else min(steps, k + lag + 1))


def expert(e, b):
    return nth(e, b, EXPERTS, F0_LAG)


def mixed(e, b):
    return nth(e, b, EXPERTS - 1, F0_LAG)


def g1_tile(t, b):
    return nth(t, b, T, G1_LAG)


def f1_tile(t, b):
    return nth(t, b, T, MID_LAG)


def in_turn(steps, lags):
    order, behind = [], 0
    for i in range(steps):
        order.append((0, i))
        while behind <= i - lags[i]:
            order.append((1, behind))
            behind += 1
    return order + [(1, i) for i in range(behind, steps)]


def build(nc, x, adj, weights, raw, out):
    graphs = x.shape[0]
    x_rows = x.rearrange("g (t p) d -> g p t d", p=P)
    adj_rows = adj.rearrange("g (t p) n -> g p t n", p=P)
    out_rows = out.rearrange("g (t p) d -> g p t d", p=P)
    w_at, w_cols = columns_of(WEIGHTS)
    raw_at, raw_cols = columns_of(RAW)
    made_at, made_cols = columns_of(MADE)
    assert raw_cols <= SCRATCH

    ctx = ExitStack()
    with ctx:
        def sb(name, shape, dt=F32):
            return ctx.enter_context(nc.sbuf_tensor(name, shape, dt))

        def sem(name):
            return ctx.enter_context(nc.semaphore(name))

        weights_sb = sb("weights_sb", [P, w_cols])
        made_sb = sb("made_sb", [P, made_cols])
        ident_big = sb("ident_big", [P, P], BF16)
        ones_bf = sb("ones_bf", [P, P], BF16)
        bias_parts = sb("bias_parts", [P, SH * SG], BF16)
        part_bf = sb("part_bf", [P, SH * SG], BF16)
        minus_half = sb("minus_half", [P, T])
        XIN = [sb(f"x_in{b}", [P, T, D]) for b in range(LANES)]
        XLN = [sb(f"x_in_ln{b}", [P, T, D]) for b in range(LANES)]
        X = [sb(f"x{b}", [P, T, D]) for b in range(LANES)]
        XN = [sb(f"xn{b}", [P, T, 132]) for b in range(LANES)]
        XT = [sb(f"xT{b}", [P, N]) for b in range(LANES)]
        ADJ = [sb(f"adj{b}", [P, T, N], I32) for b in range(LANES)]
        AF = [sb(f"adjf{b}", [P, T, N]) for b in range(LANES)]
        NM = [sb(f"nomask{b}", [P, T, N], BF16) for b in range(LANES)]
        stats = [sb(f"stats{b}", [P, T, 6]) for b in range(LANES)]
        mv = [sb(f"mv{b}", [P, T, 2]) for b in range(LANES)]
        ve = [sb(f"ve{b}", [P, T]) for b in range(LANES)]
        rstd = [sb(f"rstd{b}", [P, T]) for b in range(LANES)]
        SC = [sb(f"scratch{b}", [P, SCRATCH]) for b in range(LANES)]
        PS = [[ctx.enter_context(nc.psum_tensor(f"ps{b}_{i}", [P, 512], F32)) for i in range(4)] for b in range(LANES)]

        def W(name, rows=P):
            a, n = w_at[name]
            return weights_sb[0:rows, a:a + n]

        def R(name, rows=P):
            a, n = raw_at[name]
            return SC[0][0:rows, a:a + n]

        def M(name, rows=P):
            a, n = made_at[name]
            return made_sb[0:rows, a:a + n]

        def cut(b, at, n, rows=P):
            return SC[b][0:rows, at:at + n]

        def ps(b, i, n=512, rows=P, at=0):
            return PS[b][i][0:rows, at:at + n]

        def tile(t, n=P):
            return slice(t * n, (t + 1) * n)

        def first_column(ap):
            return ap.rearrange("p (t n) -> p t n", n=P)[:, :, 0]

        def spread(ap, axis, shape):
            return ap.unsqueeze(axis).to_broadcast(shape)

        ident = W("ident")

        G0_M, G0_AG, G0_R, G0_Z, G0_U = (512 * k for k in range(5))
        F0_HID, F0_LG, F0_GT, F0_EQ, F0_RK, F0_SEL, F0_LS, F0_S, F0_TH, F0_GATE, F0_GATET = (
            0, 1024, 1088, 1344, 1600, 1632, 1664, 1696, 1704, 1736, 1792)
        G1_WH, G1_F, G1_Z, G1_U, G1_P, G1_PT, G1_MX, G1_SUM, G1_RI, G1_POS, G1_NEG = (
            0, 512, 1024, 2048, 3072, 4096, 6144, 6148, 6152, 6160, 6672)
        F1_SW, F1_SWT, F1_MX, F1_SUM, F1_RI, F1_SN, F1_DEN, F1_RD, F1_RAT, F1_RM, F1_ST, F1_RR, F1_TK, F1_QP, F1_TV = (
            0, 2048, 4096, 4128, 4160, 4192, 4704, 4708, 4712, 4716, 4748, 5260, 5772, 6284, 6796)
        F1_E, F1_EMX, F1_ES, F1_ER, F1_ET, F1_U = 7820, 8076, 8080, 8084, 8088, 8600
        G2_UP, G2_DEG, G2_RD, G2_POS, G2_C, G2_O = 0, 512, 516, 520, 524, 528
        PAD = TAPS - 1
        CW = N + PAD + 1
        F2_CIN, F2_XS, F2_CC, F2_Z, F2_XD, F2_BB, F2_GM, F2_CE, F2_XDD, F2_S = (
            0, 2048, 3840, 4352, 5376, 6400, 6912, 7424, 8192, 8960)
        F2_E, F2_PV, F2_YG, F2_SQ = 0, 3072, 0, 5376
        G3_QZ, G3_K, G3_V, G3_P, G3_PT, G3_H, G3_MX, G3_SUM, G3_RI = 0, 2048, 2560, 3072, 5120, 7168, 8192, 8224, 8256
        G3_RING = 4
        G3_O = 3072
        F3_HID, F3_W, F3_CMP, F3_CNT, F3_SC, F3_Y = 0, 2048, 2056, 4616, 4640, 4650
        lanes = range(LANES)
        mid_order = in_turn(MID_STEPS, MID_LAGS)

        loaded, first_loaded, first_x_loaded = sem("weights_loaded"), sem("first_loaded"), sem("first_x_loaded")
        prep_pe, prep_dve, prep_act = sem("prep_pe"), sem("prep_dve"), sem("prep_act")
        x_step, x_root = sem("first_x_step"), sem("first_x_root")
        with nc.Block() as block:
            @block.sync
            def _(sp):
                for b in lanes:
                    sp.dma_start(XIN[b][:, :, :], x_rows[b]).then_inc(first_x_loaded, 16)
                sp.dma_start(SC[0][:, 0:raw_cols], raw).then_inc(loaded, 16)
                sp.dma_start(weights_sb[:, :], weights).then_inc(loaded, 16)
                for b in lanes:
                    sp.dma_start(ADJ[b][:, :, :], adj_rows[b]).then_inc(first_loaded, 16)
                sp.wait_ge(first_loaded, 16 * LANES)

            @block.tensor
            def _(pe):
                pe.wait_ge(loaded, 32)
                for k, bank in enumerate((ps(1, 2, 3 * D), ps(1, 3, 3 * D), ps(0, 0, 3 * D, P, D))):
                    pe.matmul(bank, R("g0_wT")[:, tile(k)], R("g0_wih"), start=True, stop=True)
                pe.matmul(ps(0, 0, 2), R("g1_wT"), R("g1_a"), start=True, stop=True)
                pe.matmul(ps(0, 0, SD, SD, 64), R("f1_wqT", SD), R("f1_wkT", SD), start=True, stop=True)
                for k in range(2):
                    pe.matmul(ps(0, 3, D, P, k * D), R("f2_woutT")[:, tile(k)], R("f2_wlin"), start=True, stop=True)
                for h in range(SH):
                    pe.matmul(ps(0, 1, SG, P, h * SG), R("f1_wxT", SD)[:, tile(h)], R("f1_wslice", SD), start=True, stop=True)
                    pe.matmul(ps(0, 2, SG, P, h * SG), R("f1_bx", SD)[:, h:h + 1].to_broadcast([SD, P]),
                              R("f1_wslice", SD), start=True, stop=True)
                    last = pe.matmul(ps(1, h // 4, D, SD, (h % 4) * D), R("f1_wvT", SD), R("f1_wout", SD)[:, tile(h)],
                                     start=True, stop=True)
                last.then_inc(prep_pe, 1)

            @block.vector
            def _(v):
                v.memset(minus_half[:, :], -0.5)
                v.wait_ge(first_x_loaded, 16 * LANES)
                for b in lanes:
                    for t in range(T):
                        last = v.bn_stats(stats[b][:, t, :], XIN[b][:, t, :])
                last.then_inc(x_step, 1)
                v.wait_ge(x_step, 1)
                for b in lanes:
                    for t in range(T):
                        last = v.bn_aggr(mv[b][:, t, :], stats[b][:, t, :])
                last.then_inc(x_step, 1)
                v.wait_ge(x_step, 2)
                for b in lanes:
                    last = v.tensor_scalar(ve[b][:, :], mv[b][:, :, 1], EPS, None, ALU.add)
                last.then_inc(x_step, 1)
                v.wait_ge(x_root, LANES)
                for b in lanes:
                    for t in range(T):
                        v.tensor_scalar(XLN[b][:, t, :], XIN[b][:, t, :], mv[b][:, t, 0:1], rstd[b][:, t:t + 1], ALU.subtract, ALU.mult)
                for b in lanes:
                    v.memset(XN[b][:, :, D:132], 1.0)
                v.wait_ge(loaded, 32)
                v.tensor_scalar(ident_big[:, :], ident, BIG, None, ALU.mult)
                v.tensor_tensor(M("g0_brz"), W("g0_bih")[:, 0:2], W("g0_bhh")[:, 0:2], ALU.add)
                v.tensor_scalar(M("f1_rtemp"), R("f1_temp"), 0.1, 5.0, ALU.max, ALU.min).then_inc(prep_dve, 1)
                v.wait_ge(prep_dve, 1)
                v.reciprocal(M("f1_rtemp"), M("f1_rtemp")).then_inc(prep_dve, 1)
                for q in ("g3_wq0", "g3_wq1", "g3_bq0", "g3_bq1"):
                    v.tensor_scalar(M(q), R(q), AD ** -0.5, None, ALU.mult)
                v.wait_ge(prep_pe, 1)
                for k, bank in enumerate((ps(1, 2, 3 * D), ps(1, 3, 3 * D), ps(0, 0, 3 * D, P, D))):
                    v.tensor_copy(M("g0_wgi")[:, tile(k, 3 * D)], bank)
                v.tensor_copy(M("g1_wa1"), ps(0, 0, 1).to_broadcast([P, P]))
                v.tensor_copy(M("g1_wa2"), ps(0, 0, 1, P, 1).to_broadcast([P, P]))
                v.tensor_scalar(M("f1_wqk", SD), ps(0, 0, SD, SD, 64), SD ** -0.5, None, ALU.mult)
                for k in range(2):
                    v.tensor_scalar(M("f2_wol")[:, tile(k)], ps(0, 3, D, P, k * D), R("f2_normw")[:, k:k + 1], None, ALU.mult)
                    v.tensor_copy(M("f1_wvo", SD)[:, tile(k, 512)], ps(1, k, 512, SD))
                v.wait_ge(prep_dve, 2)
                rtemp = spread(M("f1_rtemp"), 2, [P, SH, SG])
                v.tensor_tensor(M("f1_ws").rearrange("p (h g) -> p h g", h=SH), ps(0, 1).rearrange("p (h g) -> p h g", h=SH),
                                rtemp, ALU.mult)
                bias = cut(1, 0, SH * SG)
                bs = bias.rearrange("p (h g) -> p h g", h=SH)
                v.tensor_tensor(bs, ps(0, 2).rearrange("p (h g) -> p h g", h=SH), spread(R("f1_bslice"), 1, [P, SH, SG]),
                                ALU.add).then_inc(prep_dve, 1)
                v.wait_ge(prep_dve, 3)
                v.tensor_tensor(bs, bs, rtemp, ALU.mult).then_inc(prep_dve, 1)
                v.wait_ge(prep_dve, 4)
                v.memset(ones_bf[:, :], 1.0)
                v.memset(bias_parts[:, :], 0.0)
                for k in range(3):
                    v.tensor_copy(part_bf[:, :], bias).then_inc(prep_dve, 1)
                    v.wait_ge(prep_dve, 5 + 2 * k)
                    v.scalar_tensor_tensor(out=bias_parts[:, :], in0=part_bf[:, :], scalar=ident[:, k:k + 1], in1=bias_parts[:, :],
                                           op0=ALU.mult, op1=ALU.add)
                    v.tensor_tensor(bias, bias, part_bf[:, :], ALU.subtract).then_inc(prep_dve, 1)
                    v.wait_ge(prep_dve, 6 + 2 * k)
                v.wait_ge(prep_act, 1)
                v.tensor_scalar(M("f2_nega"), M("f2_nega"), -1.0, None, ALU.mult)

            @block.gpsimd
            def _(g):
                g.wait_ge(x_step, 3)
                for b in lanes:
                    g.tensor_tensor(rstd[b][:, :], ve[b][:, :], minus_half[:, :], ALU.pow).then_inc(x_root, 1)

            @block.scalar
            def _(act):
                act.wait_ge(loaded, 32)
                act.activation(M("f2_nega"), R("f2_alog"), ACT.Exp).then_inc(prep_act, 1)

        names = [
            "next_loaded", "next_x_loaded",
            "v_step",
            "x_new0", "x_new1", "var_ready0", "var_ready1", "rstd_ready0", "rstd_ready1", "xn_ready0", "xn_ready1", "xT_psum0", "xT_psum1", "xT_ready0", "xT_ready1", "masks_ready", "stored",
            "rows_psum", "rows_ready", "aggr_psum", "aggr_ready", "rz_psum", "n_psum", "r_ready", "u_ready", "n_ready",
            "h_ready", "h_back",
            "logit_psum", "half_gap", "gate_tanh", "gate_ready", "gT_psum", "gT_ready", "b2_psum", "b2_added", "hid_psum", "hid_ready", "y_psum", "combined",
            "wh_psum", "wh_ready", "f_ready", "z1_psum", "z1_ready", "u1_ready", "p1_ready", "p1T_psum", "p1T_ready",
            "o1_psum", "o1_neg", "elu_exp",
            "sl_psum", "sl_shifted", "sl_exp", "sl_rsum", "sw_ready", "swT_psum", "swT_ready", "tok_psum",
            "sn_ready", "sT_psum", "sT_ready", "ratio_psum", "ratio_ready", "tk_psum", "tk_ready", "qp_psum", "qp_ready",
            "tv_psum", "tv_ready", "sc_psum", "sc_shifted", "sc_exp", "eT_psum", "eT_ready", "u_psum", "us_ready", "so_psum", "bout_added",
            "adjf_ready", "h2_psum", "h2_ready", "upd_psum", "msg_psum",
            "xbc_psum", "dt_psum", "dt_v", "dt_e", "dt_u", "dt_ln", "xbc_ready", "zg_psum", "zg_ready", "conv_ready", "silu_ready", "cc_ready0", "cc_ready1",
            "da_ready", "ac_psum", "ac_ready", "xs_T", "xd_ready", "gt_psum", "gm_ready", "row_psum", "dd_ready", "re_ready", "e_ready",
            "ce_ready", "xdd_ready", "mt_ready", "st_psum", "pv_zero", "pv_ready", "yt_psum", "yg_ready", "sq_ready", "ym_psum", "ms_ready", "rs_ready", "blin_added",
            "qkv_psum", "q_ready", "kv_ready", "qz_zero", "att_psum", "att_max", "att_exp", "att_rsum", "att_p", "pT_psum", "pT_even", "pT_odd",
            "pv_psum", "h3_ready", "g3_psum",
            "w3_psum", "w3_ready", "row3_psum", "scale3_ready", "hid3_psum", "hid3_ready", "y3_psum", "xn_added",
        ]
        s = {name: sem(name) for name in names}
        first_sem, last_sem = s[names[0]].num, s[names[-1]].num
        assert last_sem - first_sem == len(names) - 1

        def weights_T(b, h):
            if h % 2:
                return AF[b][:, :, :].rearrange("p t n -> p (t n)")[:, h // 2 * T * 2 * P:(h // 2 + 1) * T * 2 * P]
            return cut(b, G3_PT + h // 2 * T * 2 * P, T * 2 * P)

        def turned(eng, b, layer, n):
            eng.wait_ge(s["pT_odd" if n % 2 else "pT_even"], nth((layer * T * AH + n) // 2, b))

        G0, F0, G1, F1, G2, F2, G3, F3 = range(8)
        NEXT = "next"
        LN_COUNT = {F0: 1, NEXT: 2, G1: 3, F1: 4, G2: 5, F2: 6, G3: 7, F3: 8}

        rounds = graphs // LANES
        with nc.Fori(0, rounds) as i:
            after = (i + 1) % rounds
            with nc.Block() as block:
                @block.sync
                def _(sp):
                    for b in lanes:
                        sp.wait_ge(s[f"x_new{b}"], 1)
                        g = bass.ds(after * LANES + b, 1)
                        sp.dma_start(XIN[b][:, :, :], x_rows[g].rearrange("a p t d -> (a p) t d")).then_inc(s["next_x_loaded"], 16)
                    for b in lanes:
                        sp.wait_ge(s["adjf_ready"], b + 1)
                        g = bass.ds(after * LANES + b, 1)
                        sp.dma_start(ADJ[b][:, :, :], adj_rows[g].rearrange("a p t n -> (a p) t n")).then_inc(s["next_loaded"], 16)
                    for b in lanes:
                        c_rows = SC[b][MS:P, F2_XS + 2 * N:F2_XS + 3 * N]
                        sp.wait_ge(s["silu_ready"], 3 * b + 1)
                        sp.dma_start(cut(b, F2_CC, N, MS), c_rows).then_inc(s[f"cc_ready{b}"], 16)
                        sp.dma_start(SC[b][MS:P, F2_CC:F2_CC + N], c_rows).then_inc(s[f"cc_ready{b}"], 16)
                    for b in lanes:
                        g = bass.ds(i * LANES + b, 1)
                        sp.wait_ge(s[f"x_new{b}"], 8)
                        sp.dma_start(out_rows[g].rearrange("a p t d -> (a p) t d"), X[b][:, :, :]).then_inc(s["stored"], 16)
                    sp.wait_ge(s["stored"], 16 * LANES)
                    sp.wait_ge(s["next_loaded"], 16 * LANES)

                @block.tensor
                def _(pe):
                    def mm(o, lhsT, rhs, start=True, stop=True, **k):
                        return pe.matmul(o, lhsT, rhs, start=start, stop=stop, **k)

                    def to_columns(b, k):
                        if k != G0:
                            pe.wait_ge(s[f"xn_ready{b}"], k)
                        rows = XLN[b] if k == G0 else XN[b]
                        for t in range(T):
                            last = pe.transpose(ps(b, 0, P, P, t * P), rows[:, t, 0:D], ident)
                        last.then_inc(s[f"xT_psum{b}"], 1)

                    def g0_messages(b, k):
                        h = XT[b]
                        if k == 0:
                            pe.wait_ge(s[f"xT_ready{b}"], G0 + 1)
                            rows = [XLN[b][:, t, :] for t in range(T)]
                        else:
                            pe.wait_ge(s["h_ready"], nth(k - 1, b))
                            rows = [cut(b, G0_M, N)[:, tile(t)] for t in range(T)]
                            for t in range(T):
                                last = pe.transpose(ps(b, 1, P, P, t * P), h[:, tile(t)], ident)
                            last.then_inc(s["rows_psum"], 1)
                        for gate in range(2):
                            mm(ps(b, 2 + gate), W("g0_whh")[:, tile(gate)], h[:, :], stop=False)
                        if k == 0:
                            pe.wait_ge(s["masks_ready"], b + 1)
                        else:
                            pe.wait_ge(s["rows_ready"], nth(k - 1, b))
                        for t in range(T):
                            last = mm(ps(b, 1), rows[t], AF[b][:, t, :], start=t == 0, stop=t == T - 1)
                        last.then_inc(s["aggr_psum"], 1)
                        mm(ps(b, 0), W("g0_whh")[:, tile(2)], h[:, :])

                    def g0_gates(b, k):
                        pe.wait_ge(s["aggr_ready"], nth(k, b))
                        ag = cut(b, G0_AG, N)
                        wgi = M("g0_wgi")[:, tile(k, 3 * D)]
                        for gate in range(2):
                            last = mm(ps(b, 2 + gate), wgi[:, tile(gate)], ag, start=False)
                        last.then_inc(s["rz_psum"], 1)
                        mm(ps(b, 1), wgi[:, tile(2)], ag).then_inc(s["n_psum"], 1)

                    def g0_back(b):
                        pe.wait_ge(s["h_ready"], nth(GNN0_STEPS - 1, b))
                        for t in range(T):
                            last = pe.transpose(ps(b, 0, P, P, t * P), XT[b][:, tile(t)], ident)
                        last.then_inc(s["h_back"], 1)

                    def f0_logits(b):
                        to_columns(b, F0)
                        pe.wait_ge(s[f"xT_ready{b}"], F0 + 1)
                        for t in range(T):
                            last = mm(ps(b, 3, P, P, t * P), XT[b][:, tile(t)], W("f0_wr"))
                        last.then_inc(s["logit_psum"], 1)

                    def f0_gate_columns(b):
                        pe.wait_ge(s["gate_ready"], b + 1)
                        pe.wait_ge(s["combined"], mixed(GATE_TURN - 2, b))
                        gate = cut(b, F0_GATE, T * EXPERTS)
                        for t in range(T):
                            last = pe.transpose(ps(b, 3, P, EXPERTS, t * P), gate[:, tile(t, EXPERTS)], ident)
                        last.then_inc(s["gT_psum"], 1)

                    def f0_bias(b):
                        pe.wait_ge(s["gT_ready"], b + 1)
                        pe.wait_ge(s["combined"], mixed(GATE_TURN - 1, b))
                        for t in range(T):
                            last = mm(ps(b, 2, D, P, t * D), cut(b, F0_GATET, N, EXPERTS)[:, tile(t)], W("f0_b2", EXPERTS))
                        last.then_inc(s["b2_psum"], 1)

                    def f0_hidden(b, e):
                        if e:
                            pe.wait_ge(s["hid_ready"], expert(e - 1, b))
                        for k in range(2):
                            last = mm(ps(b, k), W("f0_w1")[:, tile(2 * e + k)], XT[b][:, :])
                        last.then_inc(s["hid_psum"], 1)

                    def f0_out(b, e):
                        pe.wait_ge(s["hid_ready"], expert(e, b))
                        if e == 0:
                            pe.wait_ge(s["half_gap"], b + 1)
                        elif e == GATE_TURN:
                            pe.wait_ge(s["gT_ready"], b + 1)
                        elif e == GATE_TURN + 1:
                            pe.wait_ge(s["b2_added"], b + 1)
                        elif e >= 2:
                            pe.wait_ge(s["combined"], mixed(e - 2, b))
                        for t in range(T):
                            for k in range(2):
                                last = mm(ps(b, 3 - e % 2, D, P, t * D), cut(b, F0_HID + k * N, N)[:, tile(t)],
                                          W("f0_w2")[:, tile(2 * e + k)], start=k == 0, stop=k == 1)
                        last.then_inc(s["y_psum"], 1)

                    def g1_project(b):
                        to_columns(b, G1)
                        pe.wait_ge(s[f"xT_ready{b}"], G1 + 1)
                        for t in range(T):
                            mm(ps(b, 1, D, P, t * D), XT[b][:, tile(t)], W("g1_w"))
                            last = mm(ps(b, 2, P, P, t * P), XT[b][:, tile(t)], M("g1_wa1"))
                        last.then_inc(s["wh_psum"], 1)

                    def g1_scores(b, t):
                        if t == 0:
                            pe.wait_ge(s["wh_ready"], b + 1)
                            pe.wait_ge(s["f_ready"], b + 1)
                        if t >= 2:
                            pe.wait_ge(s["z1_ready"], g1_tile(t - 2, b))
                        mm(ps(b, t % 2), M("g1_wa2"), XT[b][:, :], stop=False)
                        mm(ps(b, t % 2), ident_big[:, :], NM[b][:, t, :], start=False).then_inc(s["z1_psum"], 1)

                    def g1_turn(b, t):
                        pe.wait_ge(s["p1_ready"], g1_tile(t, b))
                        if t >= 2:
                            pe.wait_ge(s["p1T_ready"], g1_tile(t - 2, b))
                        for j in range(T):
                            last = pe.transpose(ps(b, 2 + t % 2, P, P, j * P), cut(b, G1_P + t % 2 * N, N)[:, tile(j)], ident)
                        last.then_inc(s["p1T_psum"], 1)

                    def g1_out(b):
                        pe.wait_ge(s["p1T_ready"], g1_tile(T - 1, b))
                        for t in range(T):
                            for j in range(T):
                                last = mm(ps(b, 0, D, P, t * D), cut(b, G1_PT + j * N, N)[:, tile(t)],
                                          cut(b, G1_WH, N)[:, tile(j)], start=j == 0, stop=j == T - 1)
                        last.then_inc(s["o1_psum"], 1)

                    def f1_logits(b, t):
                        if t == 0:
                            to_columns(b, F1)
                            pe.wait_ge(s[f"xT_ready{b}"], F1 + 1)
                        if t >= 2:
                            pe.wait_ge(s["sl_shifted"], f1_tile(t - 2, b))
                        mm(ps(b, t % 2), XT[b][:, tile(t)], M("f1_ws"), stop=False)
                        mm(ps(b, t % 2), ones_bf[:, :], bias_parts[:, :], start=False).then_inc(s["sl_psum"], 1)

                    def f1_turn(b, t):
                        pe.wait_ge(s["sw_ready"], f1_tile(t, b))
                        if t >= 2:
                            pe.wait_ge(s["swT_ready"], f1_tile(t - 2, b))
                        for k in range(PAIRS):
                            last = pe.transpose(ps(b, 2 + t % 2, P, P, k * P), cut(b, F1_SW + t * N, N)[:, tile(k)], ident)
                        last.then_inc(s["swT_psum"], 1)

                    def f1_tokens(b):
                        pe.wait_ge(s["sl_shifted"], f1_tile(T - 1, b))
                        for k in range(PAIRS):
                            for t in range(T):
                                last = mm(ps(b, k // 2, D + 1, P, k % 2 * 256), cut(b, F1_SW + t * N, N)[:, tile(k)],
                                          XN[b][:, t, 0:D + 1], start=t == 0, stop=t == T - 1)
                        last.then_inc(s["tok_psum"], 1)

                    def f1_project(b):
                        pe.wait_ge(s["sn_ready"], b + 1)
                        pe.wait_ge(s["swT_ready"], f1_tile(T - 1, b))
                        for k in range(PAIRS):
                            last = pe.transpose(ps(b, 2, P, P, k * P), cut(b, F1_SN, N)[:, tile(k)], ident)
                        last.then_inc(s["sT_psum"], 1)
                        for k in range(PAIRS):
                            last = mm(ps(b, 3, P, SH, k * P), cut(b, F1_RM, PAIRS * SH)[:, tile(k, SH)], ident)
                        last.then_inc(s["ratio_psum"], 1)
                        pe.wait_ge(s["ratio_ready"], b + 1)
                        pe.wait_ge(s["sT_ready"], b + 1)
                        mm(ps(b, 0, N, SD), W("f1_bfx", SH), cut(b, F1_RR, N, SH), stop=False)
                        for h in range(SH):
                            last = mm(ps(b, 0, SG, SD, h * SG), W("f1_wfx")[:, tile(h, SD)], cut(b, F1_ST, N)[:, tile(h, SG)],
                                      start=False, stop=h == SH - 1)
                        last.then_inc(s["tk_psum"], 1)

                    def f1_attend(b):
                        pe.wait_ge(s["tk_ready"], b + 1)
                        tk = cut(b, F1_TK, N, SD)
                        mm(ps(b, 1, N, SD), M("f1_wqk", SD), tk).then_inc(s["qp_psum"], 1)
                        for h in range(SH):
                            last = mm(ps(b, 2 + h // 4, D, SD, h % 4 * D), tk[:, tile(h, SG)], M("f1_wvo", SD)[:, tile(h)])
                        last.then_inc(s["tv_psum"], 1)
                        pe.wait_ge(s["qp_ready"], b + 1)
                        for h in range(SH):
                            half = SG * (h % 2)
                            last = mm(PS[b][0][half:half + SG, h // 2 * SG:(h // 2 + 1) * SG], cut(b, F1_QP, N, SD)[:, tile(h, SG)],
                                      tk[:, tile(h, SG)], tile_position=(0, half))
                        last.then_inc(s["sc_psum"], 1)

                    def f1_mix(b):
                        pe.wait_ge(s["sc_exp"], b + 1)
                        for k in range(PAIRS):
                            last = pe.transpose(ps(b, 1, P, SG, k * P), cut(b, F1_E, PAIRS * SG)[:, tile(k, SG)], ident)
                        last.then_inc(s["eT_psum"], 1)
                        pe.wait_ge(s["eT_ready"], b + 1)
                        pe.wait_ge(s["tv_ready"], b + 1)
                        for h in range(SH):
                            half = SG * (h % 2)
                            last = mm(PS[b][0][half:half + SG, tile(h // 2)], cut(b, F1_ET, N, SG)[:, tile(h, SG)],
                                      cut(b, F1_TV, SH * D, SG)[:, tile(h)], tile_position=(0, half))
                        last.then_inc(s["u_psum"], 1)

                    def f1_out(b):
                        pe.wait_ge(s["us_ready"], b + 1)
                        for t in range(T):
                            for k in range(PAIRS):
                                last = mm(ps(b, 1, D, P, t * D), cut(b, F1_SWT + k * N, N)[:, tile(t)],
                                          cut(b, F1_U, N)[:, tile(k)], start=k == 0, stop=k == PAIRS - 1)
                        last.then_inc(s["so_psum"], 1)

                    def g2_project(b):
                        to_columns(b, G2)
                        pe.wait_ge(s[f"xT_ready{b}"], G2 + 1)
                        for t in range(T):
                            last = mm(ps(b, 1, D, P, t * D), XT[b][:, tile(t)], W("g2_wmsg"))
                        last.then_inc(s["h2_psum"], 1)
                        for t in range(T):
                            last = mm(ps(b, 2, D, P, t * D), XT[b][:, tile(t)], W("g2_wupd"))
                        last.then_inc(s["upd_psum"], 1)

                    def g2_messages(b):
                        pe.wait_ge(s["h2_ready"], b + 1)
                        pe.wait_ge(s["adjf_ready"], b + 1)
                        for j in range(T):
                            for t in range(T):
                                last = mm(ps(b, 3 * (j // 2), D + 1, P, j % 2 * 256), AF[b][:, t, tile(j)],
                                          XN[b][:, t, 0:D + 1], start=t == 0, stop=t == T - 1)
                        last.then_inc(s["msg_psum"], 1)

                    def f2_project(b):
                        to_columns(b, F2)
                        pe.wait_ge(s[f"xT_ready{b}"], F2 + 1)
                        for k in (2, 0, 1):
                            mm(ps(b, 1 + k), W("f2_win")[:, tile(2 + k)], XT[b][:, :]).then_inc(s["xbc_psum"], 1)
                        for t in range(T):
                            last = mm(ps(b, 0, P, P, t * P), XT[b][:, tile(t)], W("f2_win")[:, 2 * MI + 2 * MS + MH - P:])
                        last.then_inc(s["dt_psum"], 1)

                    def f2_gate(b):
                        pe.wait_ge(s["xbc_ready"], b + 1)
                        for k in range(2):
                            last = mm(ps(b, 1 + k), W("f2_win")[:, tile(k)], XT[b][:, :])
                        last.then_inc(s["zg_psum"], 1)

                    def f2_cumulate(b):
                        pe.wait_ge(s["da_ready"], b + 1)
                        mm(ps(b, 0, T * MH), W("tri"), cut(b, F2_S + 8 * 16, T * MH)).then_inc(s["ac_psum"], 1)

                    def f2_turn(b):
                        pe.wait_ge(s["zg_ready"], b + 1)
                        for n, k in enumerate((2, 0, 1)):
                            pe.wait_ge(s["silu_ready"], 3 * b + n + 1)
                            for c in range(T):
                                last = pe.transpose(ps(b, 1 + k, P, P, c * P), cut(b, F2_XS + k * N, N)[:, tile(c)], ident)
                        last.then_inc(s["xs_T"], 1)

                    def f2_products(b):
                        pe.wait_ge(s[f"cc_ready{b}"], 32)
                        pe.wait_ge(s["ac_ready"], b + 1)
                        for c in range(T):
                            last = mm(ps(b, 0, P, P, c * P), cut(b, F2_XS + 2 * N, N, MS)[:, tile(c)], cut(b, F2_CC, N, MS)[:, tile(c)])
                        last.then_inc(s["gt_psum"], 1)

                    def f2_rows(b):
                        pe.wait_ge(s["xd_ready"], b + 1)
                        for c in (1, 2, 3, 0):
                            if c == 0:
                                pe.wait_ge(s["gm_ready"], b + 1)
                            for h in range(MH):
                                a = F2_S + 9 * 16 + c * MH + h
                                last = pe.transpose(ps(b, c, P, P, h * P), SC[b][:, a:a + 1].to_broadcast([P, P]), ident)
                            last.then_inc(s["row_psum"], 1)

                    def f2_states(b):
                        pe.wait_ge(s["xdd_ready"], b + 1)
                        for c in range(T - 1):
                            for k in range(2):
                                last = mm(ps(b, (c + 1) // 2, P, P, (c + 1) % 2 * MI + k * P), cut(b, F2_BB, N)[:, tile(c)],
                                          cut(b, F2_XDD + c * MI, MI)[:, tile(k)])
                            last.then_inc(s["st_psum"], 1)

                    def f2_within(b):
                        for c in range(T):
                            if c % 2 == 0:
                                pe.wait_ge(s["mt_ready"], 2 * b + c // 2 + 1)
                            for k in range(2):
                                for q in range(2):
                                    h = c * MH + 2 * k + q
                                    mm(PS[b][2 + k][q * MD:(q + 1) * MD, tile(c)], cut(b, F2_XD, T * MI)[:, tile(h, MD)],
                                       cut(b, F2_E, T * N)[:, tile(h)], start=c == 0, stop=False, tile_position=(0, q * MD))

                    def f2_across(b):
                        pe.wait_ge(s["ce_ready"], 2 * b + 2)
                        for c in range(1, T):
                            pe.wait_ge(s["pv_ready"], (T - 1) * b + c)
                            for k in range(2):
                                last = mm(ps(b, 2 + k, P, P, c * P), cut(b, F2_PV + (c - 1) * MI, MI)[:, tile(k)],
                                          cut(b, F2_CE + (c - 1) * MI, MI)[:, tile(k)], start=False, stop=c == T - 1)
                        last.then_inc(s["yt_psum"], 1)

                    def f2_out(b):
                        pe.wait_ge(s["yg_ready"], b + 1)
                        for t in range(T):
                            for k in range(2):
                                last = mm(ps(b, 0, D, P, t * D), cut(b, F2_YG + k * N, N)[:, tile(t)], M("f2_wol")[:, tile(k)],
                                          start=k == 0, stop=k == 1)
                        pe.wait_ge(s["sq_ready"], b + 1)
                        for t in range(T):
                            for k in range(2):
                                last = mm(ps(b, 1, P, P, t * P), cut(b, F2_SQ + k * N, N)[:, tile(t)], W("ones"), start=k == 0, stop=k == 1)
                        last.then_inc(s["ym_psum"], 1)

                    def g3_project(b, layer):
                        if layer == 0:
                            to_columns(b, G3)
                            pe.wait_ge(s[f"xT_ready{b}"], G3 + 1)
                            ins = [XT[b][:, :]]
                        else:
                            pe.wait_ge(s["h3_ready"], nth(0, b))
                            turned(pe, b, 0, T * AH - 1)
                            ins = [XT[b][:, :], cut(b, G3_H, N)]
                        wq, wk, wv = M(f"g3_wq{layer}"), W(f"g3_wk{layer}"), W(f"g3_wv{layer}")
                        for bank, w in ((1, wq), (2, wk)):
                            for n, a in enumerate(ins):
                                mm(ps(b, bank), w[:, tile(n)], a, start=n == 0, stop=n == layer)
                        for t in range(T):
                            for n, a in enumerate(ins):
                                last = mm(ps(b, 3, D, P, t * D), a[:, tile(t)], wv[:, tile(n)], start=n == 0, stop=n == layer)
                        last.then_inc(s["qkv_psum"], 1)

                    def g3_scores(b, layer, n):
                        q, h = divmod(n, AH)
                        k = layer * T * AH + n
                        if n == 0:
                            pe.wait_ge(s["q_ready"], nth(layer, b))
                            pe.wait_ge(s["kv_ready"], nth(layer, b))
                        if n >= 2:
                            pe.wait_ge(s["att_exp"], nth(k - 2, b))
                        mm(ps(b, n % 2), cut(b, G3_QZ + h * N, N)[:, tile(q)], cut(b, G3_K, N), stop=False)
                        mm(ps(b, n % 2), ident_big[:, :], NM[b][:, q, :], start=False).then_inc(s["att_psum"], 1)

                    def g3_turn(b, layer, n):
                        k = layer * T * AH + n
                        pe.wait_ge(s["att_p"], nth(k, b))
                        if n >= 1:
                            turned(pe, b, layer, n - 1)
                        for j in range(T):
                            last = pe.transpose(ps(b, 2, P, P, j * P), cut(b, G3_P + n % G3_RING * N, N)[:, tile(j)], ident)
                        last.then_inc(s["pT_psum"], 1)

                    def g3_values(b, layer, pair):
                        turned(pe, b, layer, AH * (2 * pair + 2) - 2)
                        turned(pe, b, layer, AH * (2 * pair + 2) - 1)
                        for j in range(T):
                            for h in range(AH):
                                last = mm(PS[b][3][h * AD:(h + 1) * AD, tile(pair, 2 * P)], cut(b, G3_V + j * D, D)[:, tile(h, AD)],
                                          weights_T(b, h)[:, tile(j, 2 * P)], start=j == 0, stop=j == T - 1, tile_position=(0, h * AD))
                        last.then_inc(s["pv_psum"], 1)

                    def g3_out(b):
                        pe.wait_ge(s["h3_ready"], nth(1, b))
                        ins = [XT[b][:, :], cut(b, G3_H, N), cut(b, G3_H + N, N)]
                        for t in range(T):
                            for n, a in enumerate(ins):
                                last = mm(ps(b, 0, D, P, t * D), a[:, tile(t)], W("g3_wout")[:, tile(n)], start=n == 0, stop=n == 2)
                        last.then_inc(s["g3_psum"], 1)

                    def f3_router(b):
                        to_columns(b, F3)
                        pe.wait_ge(s[f"xT_ready{b}"], F3 + 1)
                        for t in range(T):
                            last = mm(ps(b, 3, P, P, t * P), XT[b][:, tile(t)], W("f3_wr"))
                        last.then_inc(s["w3_psum"], 1)

                    def f3_hidden(b, k):
                        if k >= 2:
                            pe.wait_ge(s["hid3_ready"], nth(k - 2, b))
                        mm(ps(b, k % 2), W("f3_w1")[:, tile(k)], XT[b][:, :]).then_inc(s["hid3_psum"], 1)

                    def f3_rank(b):
                        pe.wait_ge(s["w3_ready"], b + 1)
                        for t in range(T):
                            last = pe.transpose(ps(b, 2, P, P, t * P), cut(b, F3_W + t, 1).to_broadcast([P, P]), ident)
                        last.then_inc(s["row3_psum"], 1)

                    def f3_out(b):
                        pe.wait_ge(s["hid3_ready"], nth(3, b))
                        for t in range(T):
                            for k in range(FH // P):
                                last = mm(ps(b, 3, D, P, t * D), cut(b, F3_HID + k * N, N)[:, tile(t)], W("f3_w2")[:, tile(k)],
                                          start=k == 0, stop=k == FH // P - 1)
                        last.then_inc(s["y3_psum"], 1)

                    def turns(f, *args):
                        for b in lanes:
                            f(b, *args)

                    turns(to_columns, G0)
                    for k in range(GNN0_STEPS):
                        for b in lanes:
                            g0_messages(b, k)
                            if k == GNN0_STEPS - 1 and b:
                                g0_back(b - 1)
                            g0_gates(b, k)
                    def f0_expert(b, e):
                        if e == GATE_TURN:
                            f0_gate_columns(b)
                        f0_out(b, e)
                        if e == GATE_TURN:
                            f0_bias(b)
                        if e + 1 < EXPERTS:
                            f0_hidden(b, e + 1)

                    f0_logits(0)
                    f0_hidden(0, 0)
                    g0_back(1)
                    for e in range(EXPERTS + F0_LAG - 1):
                        if e < EXPERTS:
                            f0_expert(0, e)
                        if e == F0_LAG - 1:
                            f0_logits(1)
                            f0_hidden(1, 0)
                        if e >= F0_LAG:
                            f0_expert(1, e - F0_LAG)
                    g1_project(0)
                    f0_expert(1, EXPERTS - 1)
                    def g1_step(b, t):
                        if t < T:
                            g1_scores(b, t)
                        if t >= 2:
                            g1_turn(b, t - 2)

                    for t in range(T + 2 + G1_LAG):
                        if t < T + 2:
                            g1_step(0, t)
                        if t == G1_LAG - 1:
                            g1_project(1)
                        if t >= G1_LAG:
                            g1_step(1, t - G1_LAG)
                    def mid_step(b, i):
                        if i == 0:
                            g1_out(b)
                        if 1 <= i < T + 1:
                            f1_logits(b, i - 1)
                        if 3 <= i < T + 3:
                            f1_turn(b, i - 3)
                        if i == T + 3:
                            f1_tokens(b)
                        if i == T + 4:
                            f1_project(b)
                        if i == T + 5:
                            f1_attend(b)
                        if i == T + 6:
                            f1_mix(b)
                        if i == T + 7:
                            f1_out(b)
                        if i == T + 8:
                            g2_project(b)
                        if i == T + 9:
                            g2_messages(b)
                        if i == T + 10:
                            f2_project(b)
                        if i == T + 11:
                            f2_gate(b)
                        if i == T + 12:
                            f2_turn(b)
                        if i == T + 13:
                            f2_cumulate(b)
                            f2_products(b)
                            f2_rows(b)
                        if i == T + 14:
                            f2_states(b)
                            f2_within(b)
                        if i == T + 15:
                            f2_across(b)
                        if i == T + 16:
                            f2_out(b)
                        if i == T + 17:
                            g3_project(b, 0)

                    for b, i in mid_order:
                        mid_step(b, i)
                    for layer in range(2):
                        if layer:
                            turns(g3_project, layer)
                        for n in range(T * AH + 3):
                            for b in lanes:
                                if n < T * AH:
                                    g3_scores(b, layer, n)
                                if n >= 3 and (n - 3) % (2 * AH) == 2 * AH - 1:
                                    g3_values(b, layer, (n - 3) // (2 * AH))
                                if 2 <= n < T * AH + 2:
                                    g3_turn(b, layer, n - 2)
                    turns(g3_out)
                    turns(f3_router)
                    for k in range(FH // P):
                        turns(f3_hidden, k)
                        if k == 1:
                            turns(f3_rank)
                    turns(f3_out)

                @block.scalar
                def _(act):
                    def f(o, a, func, **k):
                        return act.activation(o, a, func, **k)

                    def columns_out(b, k):
                        act.wait_ge(s[f"xT_psum{b}"], k + 1)
                        if k == F0:
                            f(XT[b][:, :], ps(b, 0), ACT.Identity, scale=W("f0_gamma"), bias=W("f0_beta")).then_inc(s[f"xT_ready{b}"], 1)
                        else:
                            f(XT[b][:, :], ps(b, 0), ACT.Copy).then_inc(s[f"xT_ready{b}"], 1)

                    def g0_messages(b, k):
                        if k:
                            act.wait_ge(s["rows_psum"], nth(k - 1, b))
                            f(cut(b, G0_M, N), ps(b, 1), ACT.Copy).then_inc(s["rows_ready"], 1)

                    def g0_gates(b, k):
                        act.wait_ge(s["rz_psum"], nth(k, b))
                        f(cut(b, G0_R, N), ps(b, 2), ACT.Sigmoid, bias=M("g0_brz")[:, 0:1]).then_inc(s["r_ready"], 1)
                        f(cut(b, G0_Z, N), ps(b, 3), ACT.Sigmoid, bias=M("g0_brz")[:, 1:2])

                    def g0_candidate(b, k):
                        act.wait_ge(s["u_ready"], nth(k, b))
                        f(cut(b, G0_U, N), cut(b, G0_U, N), ACT.Tanh, bias=W("g0_bih")[:, 2:3]).then_inc(s["n_ready"], 1)

                    def f0_hidden(b, e):
                        act.wait_ge(s["hid_psum"], expert(e, b))
                        if e:
                            act.wait_ge(s["y_psum"], expert(e - 1, b))
                        for k in range(2):
                            last = f(cut(b, F0_HID + k * N, N), ps(b, k), ACT.Gelu, bias=W("f0_b1")[:, 2 * e + k:2 * e + k + 1])
                        last.then_inc(s["hid_ready"], 1)

                    def f0_tanh(b):
                        act.wait_ge(s["half_gap"], b + 1)
                        th = cut(b, F0_TH, T * EXPERTS)
                        f(th, th, ACT.Tanh).then_inc(s["gate_tanh"], 1)

                    def g1_project(b):
                        act.wait_ge(s["wh_psum"], b + 1)
                        f(cut(b, G1_WH, N), ps(b, 1), ACT.Copy).then_inc(s["wh_ready"], 1)

                    def g1_scores(b, t):
                        act.wait_ge(s["z1_psum"], g1_tile(t, b))
                        if t == 0:
                            act.wait_ge(s["f_ready"], b + 1)
                        if t >= 2:
                            act.wait_ge(s["u1_ready"], g1_tile(t - 2, b))
                        f(cut(b, G1_Z + t % 2 * N, N), ps(b, t % 2), ACT.Identity, bias=cut(b, G1_F + t, 1)).then_inc(s["z1_ready"], 1)

                    def g1_exp(b, t):
                        act.wait_ge(s["u1_ready"], g1_tile(t, b))
                        if t >= 2:
                            act.wait_ge(s["p1T_psum"], g1_tile(t - 2, b))
                        f(cut(b, G1_P + t % 2 * N, N), cut(b, G1_U + t % 2 * N, N), ACT.Exp, bias=cut(b, G1_MX + t, 1),
                          accum_out=cut(b, G1_SUM + t, 1)).then_inc(s["p1_ready"], 1)

                    def g1_turned(b, t):
                        act.wait_ge(s["p1T_psum"], g1_tile(t, b))
                        pt = cut(b, G1_PT, T * N).rearrange("p (j n) -> p j n", j=T)
                        f(pt[:, :, tile(t)], ps(b, 2 + t % 2).rearrange("p (j n) -> p j n", j=T), ACT.Copy).then_inc(s["p1T_ready"], 1)

                    def g1_elu(b):
                        act.wait_ge(s["o1_neg"], b + 1)
                        f(cut(b, G1_NEG, N), cut(b, G1_NEG, N), ACT.Exp).then_inc(s["elu_exp"], 1)

                    def f1_exp(b, t):
                        act.wait_ge(s["sl_shifted"], f1_tile(t, b))
                        sw = cut(b, F1_SW + t * N, N)
                        f(sw, sw, ACT.Exp).then_inc(s["sl_exp"], 1)

                    def f1_turned(b, t):
                        act.wait_ge(s["swT_psum"], f1_tile(t, b))
                        swt = cut(b, F1_SWT, T * N).rearrange("p (k n) -> p k n", k=PAIRS)
                        f(swt[:, :, tile(t)], ps(b, 2 + t % 2).rearrange("p (k n) -> p k n", k=PAIRS), ACT.Copy).then_inc(s["swT_ready"], 1)

                    def f1_project(b):
                        act.wait_ge(s["sT_psum"], b + 1)
                        f(cut(b, F1_ST, N), ps(b, 2), ACT.Copy).then_inc(s["sT_ready"], 1)

                    def f1_attend(b):
                        act.wait_ge(s["qp_psum"], b + 1)
                        f(cut(b, F1_QP, N, SD), ps(b, 1, N, SD), ACT.Copy).then_inc(s["qp_ready"], 1)
                        act.wait_ge(s["tv_psum"], b + 1)
                        f(cut(b, F1_TV, N, SG), ps(b, 2, N, SG), ACT.Copy)
                        f(cut(b, F1_TV + N, N, SG), ps(b, 3, N, SG), ACT.Copy).then_inc(s["tv_ready"], 1)
                        act.wait_ge(s["sc_shifted"], b + 1)
                        e = cut(b, F1_E, PAIRS * SG)
                        f(e, e, ACT.Exp).then_inc(s["sc_exp"], 1)

                    def g2_project(b):
                        act.wait_ge(s["h2_psum"], b + 1)
                        f(XN[b][:, :, 0:D], ps(b, 1).rearrange("p (t d) -> p t d", t=T), ACT.Copy).then_inc(s["h2_ready"], 1)

                    def f2_project(b):
                        for n, k in enumerate((2, 0, 1)):
                            act.wait_ge(s["xbc_psum"], 3 * b + n + 1)
                            f(cut(b, F2_CIN + k * CW + PAD, N), ps(b, 1 + k), ACT.Copy)
                            tap = k * TAPS + TAPS - 1
                            last = f(cut(b, F2_XS + k * N, N), ps(b, 1 + k), ACT.Identity, scale=W("f2_convw")[:, tap:tap + 1])
                        last.then_inc(s["xbc_ready"], 1)

                    def f2_gate(b):
                        act.wait_ge(s["zg_psum"], b + 1)
                        for k in range(2):
                            last = f(cut(b, F2_Z + k * N, N), ps(b, 1 + k), ACT.Silu)
                        last.then_inc(s["zg_ready"], 1)

                    def f2_silu(b):
                        for n, k in enumerate((2, 0, 1)):
                            act.wait_ge(s["conv_ready"], 3 * b + n + 1)
                            xs = cut(b, F2_XS + k * N, N)
                            f(xs, xs, ACT.Silu, bias=W("f2_convb")[:, k:k + 1]).then_inc(s["silu_ready"], 1)

                    def f2_softplus(b):
                        act.wait_ge(s["dt_v"], b + 1)
                        f(cut(b, F2_S + 16, 16), cut(b, F2_S + 16, 16), ACT.Exp).then_inc(s["dt_e"], 1)

                    def f2_log(b):
                        act.wait_ge(s["dt_u"], b + 1)
                        f(cut(b, F2_S + 3 * 16, 16), cut(b, F2_S + 2 * 16, 16), ACT.Ln).then_inc(s["dt_ln"], 1)

                    def f2_rows(b):
                        for n, c in enumerate((1, 2, 3, 0)):
                            act.wait_ge(s["row_psum"], T * b + n + 1)
                            f(AF[b][:, c, :], ps(b, c), ACT.Exp).then_inc(s["re_ready"], 1)

                    def f2_decays(b):
                        act.wait_ge(s["dd_ready"], T * b + T)
                        for q in range(2):
                            e = cut(b, F2_E + 2 * q * N, 2 * N)
                            f(e, e, ACT.Exp).then_inc(s["e_ready"], 1)

                    def f2_square(b):
                        act.wait_ge(s["yg_ready"], b + 1)
                        f(cut(b, F2_SQ, 2 * N), cut(b, F2_YG, 2 * N), ACT.Square).then_inc(s["sq_ready"], 1)

                    def g3_project(b, layer):
                        act.wait_ge(s["qkv_psum"], nth(layer, b))
                        if layer == 0:
                            act.wait_ge(s["qz_zero"], b + 1)
                        for h in range(AH):
                            rows = slice(h * AD, (h + 1) * AD)
                            a = G3_QZ + h * N
                            last = f(SC[b][rows, a:a + N], PS[b][1][rows, :], ACT.Identity, bias=M(f"g3_bq{layer}")[rows, :])
                        last.then_inc(s["q_ready"], 1)

                    def g3_exp(b, layer, n):
                        k = layer * T * AH + n
                        act.wait_ge(s["att_max"], nth(k, b))
                        if k >= G3_RING:
                            act.wait_ge(s["pT_psum"], nth(k - G3_RING, b))
                        f(cut(b, G3_P + n % G3_RING * N, N), ps(b, n % 2), ACT.Exp, bias=cut(b, G3_MX + n, 1),
                          accum_out=cut(b, G3_SUM + n, 1)).then_inc(s["att_exp"], 1)

                    def g3_turned(b, layer, n):
                        k = layer * T * AH + n
                        act.wait_ge(s["pT_psum"], nth(k, b))
                        if n == 2 * AH + 1:
                            act.wait_ge(s["pv_psum"], nth(2 * layer, b))
                        pt = weights_T(b, n % AH).rearrange("p (j n) -> p j n", j=T)
                        f(pt[:, :, tile(n // AH % 2)], ps(b, 2).rearrange("p (j n) -> p j n", j=T), ACT.Copy).then_inc(s["pT_odd"], 1)

                    def g3_gather(b, layer):
                        act.wait_ge(s["pv_psum"], nth(2 * layer + 1, b))
                        f(cut(b, G3_H + layer * N, N), ps(b, 3), ACT.Copy).then_inc(s["h3_ready"], 1)

                    def f3_hidden(b, k):
                        act.wait_ge(s["hid3_psum"], nth(k, b))
                        f(cut(b, F3_HID + k * N, N), ps(b, k % 2), ACT.Gelu_apprx_tanh, bias=W("f3_b1")[:, k:k + 1]).then_inc(s["hid3_ready"], 1)

                    def turns(g, *args):
                        for b in lanes:
                            g(b, *args)

                    turns(columns_out, G0)
                    for k in range(GNN0_STEPS):
                        for b in lanes:
                            g0_messages(b, k)
                            if b:
                                g0_candidate(0, k)
                            elif k:
                                g0_candidate(1, k - 1)
                            g0_gates(b, k)
                    g0_candidate(1, GNN0_STEPS - 1)
                    columns_out(0, F0)
                    f0_hidden(0, 0)
                    f0_tanh(0)
                    for e in range(EXPERTS + F0_LAG - 1):
                        if e + 1 < EXPERTS:
                            f0_hidden(0, e + 1)
                        if e == F0_LAG - 1:
                            columns_out(1, F0)
                            f0_hidden(1, 0)
                            f0_tanh(1)
                        if e >= F0_LAG:
                            f0_hidden(1, e - F0_LAG + 1)
                    def g1_step(b, t):
                        if t < T:
                            g1_scores(b, t)
                        if 1 <= t <= T:
                            g1_exp(b, t - 1)
                        if t >= 2:
                            g1_turned(b, t - 2)

                    columns_out(0, G1)
                    g1_project(0)
                    for t in range(T + 2 + G1_LAG):
                        if t < T + 2:
                            g1_step(0, t)
                        if t == G1_LAG - 1:
                            columns_out(1, G1)
                            g1_project(1)
                        if t >= G1_LAG:
                            g1_step(1, t - G1_LAG)
                    def mid_step(b, i):
                        if i == 0:
                            g1_elu(b)
                        if i == 1:
                            columns_out(b, F1)
                        if 2 <= i < T + 2:
                            f1_exp(b, i - 2)
                        if 3 <= i < T + 3:
                            f1_turned(b, i - 3)
                        if i == T + 4:
                            f1_project(b)
                        if i == T + 5:
                            f1_attend(b)
                        if i == T + 8:
                            columns_out(b, G2)
                            g2_project(b)
                        if i == T + 10:
                            columns_out(b, F2)
                            f2_project(b)
                        if i == T + 11:
                            f2_softplus(b)
                        if i == T + 11 and b == 1:
                            turns(f2_gate)
                            turns(f2_silu)
                            turns(f2_log)
                        if i == T + 13:
                            f2_rows(b)
                        if i == T + 14:
                            f2_decays(b)
                        if i == T + 16:
                            f2_square(b)
                        if i == T + 17:
                            columns_out(b, G3)
                            g3_project(b, 0)

                    for b, i in mid_order:
                        mid_step(b, i)
                    for layer in range(2):
                        if layer:
                            turns(g3_project, layer)
                        for n in range(T * AH + 2):
                            for b in lanes:
                                if n < T * AH:
                                    g3_exp(b, layer, n)
                                if n >= 2 and n % 2:
                                    g3_turned(b, layer, n - 2)
                        turns(g3_gather, layer)
                    turns(columns_out, F3)
                    for k in range(FH // P):
                        turns(f3_hidden, k)

                @block.vector
                def _(v):
                    own = Steps(v, s["v_step"])

                    def tt(o, a, c, op):
                        return v.tensor_tensor(o, a, c, op)

                    def ts(o, a, s1, op0, s2=None, op1=ALU.bypass, **k):
                        return v.tensor_scalar(o, a, s1, s2, op0, op1, **k)

                    def stt(o, a, s1, c, op0, op1, **k):
                        return v.scalar_tensor_tensor(out=o, in0=a, scalar=s1, in1=c, op0=op0, op1=op1, **k)

                    def tiles(ap, n=T):
                        return ap.rearrange("p (t d) -> p t d", t=n)

                    def layernorm(b, n, src, twice=False):
                        rows = XLN[b] if n == NEXT else XN[b]
                        for t in range(T):
                            last = v.bn_stats(stats[b][:, t, :], src[:, t, 0:D])
                        own(last)
                        own.wait()
                        for t in range(T):
                            last = v.bn_aggr(mv[b][:, t, :], stats[b][:, t, :])
                        own(last)
                        own.wait()
                        scale, shift = (1 + EPS, EPS * EPS) if twice else (1.0, EPS)
                        ts(ve[b][:, :], mv[b][:, :, 1], scale, ALU.mult, shift, ALU.add).then_inc(s[f"var_ready{b}"], 1)
                        v.wait_ge(s[f"rstd_ready{b}"], LN_COUNT[n])
                        for t in range(T):
                            last = ts(rows[:, t, 0:D], src[:, t, 0:D], mv[b][:, t, 0:1], ALU.subtract, rstd[b][:, t:t + 1], ALU.mult)
                        if n != NEXT:
                            last.then_inc(s[f"xn_ready{b}"], 1)

                    def new_x(b, k, ins):
                        ins.then_inc(s[f"x_new{b}"], 1)
                        v.wait_ge(s[f"x_new{b}"], k + 1)

                    def g0_masks(b):
                        ts(AF[b][:, :, :], ADJ[b][:, :, :], 0, ALU.not_equal).then_inc(s["masks_ready"], 1)

                    def g1_masks(b):
                        ts(NM[b][:, :, :], ADJ[b][:, :, :], 0, ALU.is_gt, 1.0, ALU.subtract)

                    def g0_messages(b, k):
                        v.wait_ge(s["aggr_psum"], nth(k, b))
                        v.tensor_copy(cut(b, G0_AG, N), ps(b, 1)).then_inc(s["aggr_ready"], 1)

                    def g0_gates(b, k):
                        h, r, z, u = XT[b][:, :], cut(b, G0_R, N), cut(b, G0_Z, N), cut(b, G0_U, N)
                        v.wait_ge(s["r_ready"], nth(k, b))
                        v.wait_ge(s["n_psum"], nth(k, b))
                        own(stt(u, ps(b, 0), W("g0_bhh")[:, 2:3], r, ALU.add, ALU.mult))
                        own.wait()
                        tt(u, u, ps(b, 1), ALU.add).then_inc(s["u_ready"], 1)
                        v.wait_ge(s["n_ready"], nth(k, b))
                        own(tt(r, h, u, ALU.subtract))
                        own.wait()
                        own(tt(r, r, z, ALU.mult))
                        own.wait()
                        tt(h, u, r, ALU.add).then_inc(s["h_ready"], 1)

                    def g0_end(b):
                        v.wait_ge(s["h_back"], b + 1)
                        new_x(b, 0, tt(X[b][:, :, :], XIN[b][:, :, :], tiles(ps(b, 0)), ALU.add))

                    def f0_start(b):
                        layernorm(b, F0, X[b], twice=True)

                    def f0_gate(b):
                        te = T * EXPERTS
                        lg, sel, ls, th = cut(b, F0_LG, te), cut(b, F0_SEL, te), cut(b, F0_LS, te), cut(b, F0_TH, te)
                        gt, eq, rk, sm, gate = cut(b, F0_GT, 256), cut(b, F0_EQ, 256), cut(b, F0_RK, te), cut(b, F0_S, T), cut(b, F0_GATE, te)
                        full = [P, T, EXPERTS, EXPERTS]
                        v.wait_ge(s["logit_psum"], b + 1)
                        own(tt(tiles(lg), tiles(ps(b, 3))[:, :, 0:EXPERTS], spread(W("f0_br"), 1, [P, T, EXPERTS]), ALU.add))
                        own.wait()
                        rivals, mine = spread(tiles(lg), 2, full), spread(tiles(lg), 3, full)
                        g4, e4 = (a.rearrange("p (t e f) -> p t e f", t=T, e=EXPERTS) for a in (gt, eq))
                        tt(g4, rivals, mine, ALU.is_gt)
                        own(tt(e4, rivals, mine, ALU.is_equal))
                        own.wait()
                        before = spread(W("before"), 1, [P, T, EXPERTS * EXPERTS])
                        own(tt(tiles(eq), tiles(eq), before, ALU.mult))
                        own.wait()
                        own(tt(gt, gt, eq, ALU.add))
                        own.wait()
                        own(v.tensor_reduce(tiles(rk), g4, AX, ALU.add))
                        own.wait()
                        own(ts(sel, rk, 1.5, ALU.is_lt))
                        own.wait()
                        own(tt(ls, lg, sel, ALU.mult))
                        own.wait()
                        own(v.tensor_reduce(sm, tiles(ls), AX, ALU.add))
                        own.wait()
                        stt(tiles(th), spread(sm, 2, [P, T, EXPERTS]), -0.5, tiles(lg), ALU.mult, ALU.add).then_inc(s["half_gap"], 1)

                    def f0_gate_end(b):
                        te = T * EXPERTS
                        sel, th, gate = cut(b, F0_SEL, te), cut(b, F0_TH, te), cut(b, F0_GATE, te)
                        v.wait_ge(s["gate_tanh"], b + 1)
                        own(ts(th, th, 0.5, ALU.mult, 0.5, ALU.add))
                        own.wait()
                        tt(gate, th, sel, ALU.mult).then_inc(s["gate_ready"], 1)

                    def f0_gate_columns(b):
                        v.wait_ge(s["gT_psum"], b + 1)
                        v.tensor_copy(cut(b, F0_GATET, N, EXPERTS), ps(b, 3, N, EXPERTS)).then_inc(s["gT_ready"], 1)

                    def f0_bias(b):
                        v.wait_ge(s["combined"], mixed(GATE_TURN, b))
                        v.wait_ge(s["b2_psum"], b + 1)
                        tt(X[b][:, :, :], X[b][:, :, :], tiles(ps(b, 2)), ALU.add).then_inc(s["b2_added"], 1)

                    def f0_combine(b, e):
                        v.wait_ge(s["y_psum"], expert(e, b))
                        if e == 0:
                            v.wait_ge(s["gate_ready"], b + 1)
                        elif e == GATE_TURN + 1:
                            v.wait_ge(s["b2_added"], b + 1)
                        else:
                            v.wait_ge(s["combined"], mixed(e - 1, b))
                        for t in range(T):
                            x = X[b][:, t, :]
                            last = stt(x, ps(b, 3 - e % 2, D, P, t * D), cut(b, F0_GATE + t * EXPERTS + e, 1), x, ALU.mult, ALU.add)
                        if e < EXPERTS - 1:
                            last.then_inc(s["combined"], 1)
                        else:
                            new_x(b, 1, last)

                    def g1_project(b):
                        v.wait_ge(s["wh_psum"], b + 1)
                        v.tensor_copy(cut(b, G1_F, T), first_column(ps(b, 2))).then_inc(s["f_ready"], 1)

                    def g1_scores(b, t):
                        z, u = cut(b, G1_Z + t % 2 * N, N), cut(b, G1_U + t % 2 * N, N)
                        v.wait_ge(s["z1_ready"], g1_tile(t, b))
                        if t >= 2:
                            v.wait_ge(s["p1_ready"], g1_tile(t - 2, b))
                        own(stt(u, z, 0.2, z, ALU.mult, ALU.max))
                        own.wait()
                        v.tensor_reduce(cut(b, G1_MX + t, 1), u, AX, ALU.max, negate=True).then_inc(s["u1_ready"], 1)

                    def g1_end(b):
                        ri = cut(b, G1_RI, T)
                        v.wait_ge(s["p1_ready"], g1_tile(T - 1, b))
                        own(v.reciprocal(ri, cut(b, G1_SUM, T)))
                        own.wait()
                        v.wait_ge(s["o1_psum"], b + 1)
                        for t in range(T):
                            ts(cut(b, G1_POS + t * D, D), ps(b, 0, D, P, t * D), ri[:, t:t + 1], ALU.mult, 0.0, ALU.max)
                        for t in range(T):
                            last = ts(cut(b, G1_NEG + t * D, D), ps(b, 0, D, P, t * D), ri[:, t:t + 1], ALU.mult, 0.0, ALU.min)
                        last.then_inc(s["o1_neg"], 1)
                        v.wait_ge(s["o1_neg"], b + 1)
                        own(tt(X[b][:, :, :], X[b][:, :, :], tiles(cut(b, G1_POS, N)), ALU.add))
                        own.wait()
                        v.wait_ge(s["elu_exp"], b + 1)
                        new_x(b, 2, stt(X[b][:, :, :], tiles(cut(b, G1_NEG, N)), -1.0, X[b][:, :, :], ALU.add, ALU.add))

                    def heads(ap):
                        return ap.rearrange("p (h g) -> p h g", g=SG)

                    def f1_logits(b, t):
                        sw, mx = cut(b, F1_SW + t * N, N), cut(b, F1_MX + t * SH, SH)
                        v.wait_ge(s["sl_psum"], f1_tile(t, b))
                        own(v.tensor_reduce(mx, heads(ps(b, t % 2)), AX, ALU.max))
                        own.wait()
                        tt(heads(sw), heads(ps(b, t % 2)), spread(mx, 2, [P, SH, SG]), ALU.subtract).then_inc(s["sl_shifted"], 1)

                    def f1_sums(b, t):
                        sw, sm, ri = cut(b, F1_SW + t * N, N), cut(b, F1_SUM + t * SH, SH), cut(b, F1_RI + t * SH, SH)
                        v.wait_ge(s["sl_exp"], f1_tile(t, b))
                        own(v.tensor_reduce(sm, heads(sw), AX, ALU.add))
                        own.wait()
                        v.reciprocal(ri, sm).then_inc(s["sl_rsum"], 1)

                    def f1_tokens(b):
                        den, rd, rat = cut(b, F1_DEN, PAIRS), cut(b, F1_RD, PAIRS), cut(b, F1_RAT, PAIRS)
                        v.wait_ge(s["tok_psum"], b + 1)
                        for k in range(PAIRS):
                            last = ts(den[:, k:k + 1], ps(b, k // 2, 1, P, k % 2 * 256 + D), 1e-5, ALU.add)
                        own(last)
                        own.wait()
                        own(v.reciprocal(rd, den))
                        own.wait()
                        for k in range(PAIRS):
                            ts(cut(b, F1_SN + k * D, D), ps(b, k // 2, D, P, k % 2 * 256), rd[:, k:k + 1], ALU.mult)
                            last = ts(rat[:, k:k + 1], ps(b, k // 2, 1, P, k % 2 * 256 + D), rd[:, k:k + 1], ALU.mult)
                        own(last)
                        own.wait()
                        rm = cut(b, F1_RM, PAIRS * SH).rearrange("p (k h) -> p k h", h=SH)
                        tt(rm, W("own_head").rearrange("p (k h) -> p k h", h=SH), spread(rat, 2, [P, PAIRS, SH]), ALU.mult)\
                            .then_inc(s["sn_ready"], 1)

                    def f1_project(b):
                        v.wait_ge(s["ratio_psum"], b + 1)
                        v.tensor_copy(cut(b, F1_RR, N, SH), ps(b, 3, N, SH)).then_inc(s["ratio_ready"], 1)
                        v.wait_ge(s["tk_psum"], b + 1)
                        v.tensor_copy(cut(b, F1_TK, N, SD), ps(b, 0, N, SD)).then_inc(s["tk_ready"], 1)

                    def f1_attend(b):
                        mx, e = cut(b, F1_EMX, PAIRS), cut(b, F1_E, PAIRS * SG)
                        v.wait_ge(s["sc_psum"], b + 1)
                        own(v.tensor_reduce(mx, heads(ps(b, 0, PAIRS * SG)), AX, ALU.max))
                        own.wait()
                        tt(heads(e), heads(ps(b, 0, PAIRS * SG)), spread(mx, 2, [P, PAIRS, SG]), ALU.subtract).then_inc(s["sc_shifted"], 1)

                    def f1_mix(b):
                        e, es, er = cut(b, F1_E, PAIRS * SG), cut(b, F1_ES, PAIRS), cut(b, F1_ER, PAIRS)
                        v.wait_ge(s["sc_exp"], b + 1)
                        own(v.tensor_reduce(es, heads(e), AX, ALU.add))
                        own.wait()
                        own(v.reciprocal(er, es))
                        v.wait_ge(s["eT_psum"], b + 1)
                        v.tensor_copy(cut(b, F1_ET, N, SG), ps(b, 1, N, SG)).then_inc(s["eT_ready"], 1)
                        own.wait()
                        v.wait_ge(s["u_psum"], b + 1)
                        tt(tiles(cut(b, F1_U, N), PAIRS), tiles(ps(b, 0), PAIRS), spread(er, 2, [P, PAIRS, D]), ALU.mult).then_inc(s["us_ready"], 1)

                    def f1_end(b):
                        v.wait_ge(s["so_psum"], b + 1)
                        v.wait_ge(s["bout_added"], b + 1)
                        new_x(b, 3, tt(X[b][:, :, :], X[b][:, :, :], tiles(ps(b, 1)), ALU.add))

                    def g2_end(b):
                        up, o = cut(b, G2_UP, N), cut(b, G2_O, N)
                        rd, pos, c = cut(b, G2_RD, T), cut(b, G2_POS, T), cut(b, G2_C, T)
                        v.wait_ge(s["upd_psum"], b + 1)
                        own(tt(tiles(up), tiles(ps(b, 2)), spread(W("g2_bias"), 1, [P, T, D]), ALU.add))
                        v.wait_ge(s["msg_psum"], b + 1)
                        for j in range(T):
                            deg = ps(b, 3 * (j // 2), 1, P, j % 2 * 256 + D)
                            ts(rd[:, j:j + 1], deg, 1.0, ALU.max)
                            last = ts(pos[:, j:j + 1], deg, 0.0, ALU.is_gt)
                        own(last)
                        own.wait()
                        own(v.reciprocal(rd, rd))
                        own.wait()
                        own(tt(c, rd, pos, ALU.mult))
                        own.wait()
                        for j in range(T):
                            last = stt(o[:, tile(j)], ps(b, 3 * (j // 2), D, P, j % 2 * 256), c[:, j:j + 1], up[:, tile(j)], ALU.mult, ALU.add)
                        own(last)
                        own.wait()
                        new_x(b, 4, stt(X[b][:, :, :], tiles(o), 0.0, X[b][:, :, :], ALU.max, ALU.add))

                    def small(b, k):
                        return cut(b, F2_S + 16 * k, 16)

                    def f2_conv(b):
                        cin = cut(b, F2_CIN, 3 * CW).rearrange("p (k n) -> p k n", k=3)
                        v.memset(cin[:, :, 0:PAD], 0.0)
                        v.wait_ge(s["dt_psum"], b + 1)
                        own(tt(tiles(small(b, 0)), tiles(ps(b, 0))[:, :, P - MH:P], spread(W("f2_dtb"), 1, [P, T, MH]), ALU.add))
                        own.wait()
                        stt(small(b, 1), small(b, 0), -1.0, small(b, 0), ALU.mult, ALU.min).then_inc(s["dt_v"], 1)
                        v.wait_ge(s["xbc_ready"], b + 1)
                        for tap in range(PAD):
                            for k in (2, 0, 1):
                                xs, w = cut(b, F2_XS + k * N, N), W("f2_convw")[:, k * TAPS + tap:k * TAPS + tap + 1]
                                last = stt(xs, cin[:, k, tap:tap + N], w, xs, ALU.mult, ALU.add)
                                if tap == PAD - 1:
                                    last.then_inc(s["conv_ready"], 1)
                            if tap < PAD - 1:
                                own(last)
                                own.wait()

                    def f2_softplus(b):
                        v.wait_ge(s["dt_e"], b + 1)
                        ts(small(b, 2), small(b, 1), 1.0, ALU.add).then_inc(s["dt_u"], 1)

                    def f2_decay(b):
                        vv, e, u, ln, d, z, q, dt, da = (small(b, k) for k in range(9))
                        v.wait_ge(s["dt_u"], b + 1)
                        ts(d, u, -1.0, ALU.add, 1e-30, ALU.max)
                        own(stt(z, u, 1.0, e, ALU.is_equal, ALU.mult))
                        own.wait()
                        own(v.reciprocal(d, d))
                        own(stt(z, vv, 0.0, z, ALU.max, ALU.add))
                        own.wait()
                        own(tt(d, d, e, ALU.mult))
                        own.wait()
                        v.wait_ge(s["dt_ln"], b + 1)
                        own(tt(q, d, ln, ALU.mult))
                        own.wait()
                        own(tt(dt, q, z, ALU.add))
                        own.wait()
                        tt(tiles(da), tiles(dt), spread(M("f2_nega"), 1, [P, T, MH]), ALU.mult).then_inc(s["da_ready"], 1)

                    def f2_cumulate(b):
                        v.wait_ge(s["ac_psum"], b + 1)
                        v.tensor_copy(small(b, 9), ps(b, 0, 16)).then_inc(s["ac_ready"], 1)

                    def f2_turn(b):
                        dt = small(b, 7)
                        v.wait_ge(s["xs_T"], b + 1)
                        xd = cut(b, F2_XD, T * MI).rearrange("p (c h d) -> p c h d", c=T, h=MH)
                        for k in range(2):
                            mine = tiles(dt)[:, :, 2 * k:2 * k + 2]
                            tt(xd[:, :, 2 * k:2 * k + 2, :], ps(b, 1 + k).rearrange("p (c h d) -> p c h d", c=T, h=2),
                               spread(mine, 3, [P, T, 2, MD]), ALU.mult)
                        bb = cut(b, F2_BB, N).rearrange("p (c q n) -> p c q n", c=T, q=2)
                        b_rows = tiles(ps(b, 3))[:, :, 0:MS]
                        v.tensor_copy(bb, spread(b_rows, 2, [P, T, 2, MS])).then_inc(s["xd_ready"], 1)
                        v.wait_ge(s["gt_psum"], b + 1)
                        tt(tiles(cut(b, F2_GM, N)), tiles(ps(b, 0)), spread(W("tri"), 1, [P, T, P]), ALU.mult).then_inc(s["gm_ready"], 1)

                    def f2_rows(b):
                        for n, c in enumerate((1, 2, 3, 0)):
                            v.wait_ge(s["re_ready"], T * b + n + 1)
                            for h in range(MH):
                                a = F2_S + 9 * 16 + c * MH + h
                                last = ts(cut(b, F2_E + (c * MH + h) * P, P), ps(b, c, P, P, h * P), SC[b][:, a:a + 1], ALU.subtract, 0.0, ALU.min)
                            last.then_inc(s["dd_ready"], 1)

                    def f2_weigh(b):
                        e = cut(b, F2_E, T * N)
                        v.wait_ge(s["e_ready"], 2 * b + 2)
                        n = (T - 1) * MH
                        xd, xdd = (cut(b, at, n * MD).rearrange("p (h d) -> p h d", d=MD) for at in (F2_XD, F2_XDD))
                        to_end = e.rearrange("p (h n) -> p h n", n=P)[:, 0:n, P - 1:P]
                        tt(xdd, xd, to_end.to_broadcast([P, n, MD]), ALU.mult).then_inc(s["xdd_ready"], 1)
                        v.wait_ge(s["xdd_ready"], b + 1)
                        for q in range(2):
                            e4 = cut(b, F2_E + 2 * q * N, 2 * N).rearrange("p (c h n) -> p c h n", c=2, h=MH)
                            gm = cut(b, F2_GM + 2 * q * P, 2 * P).rearrange("p (c n) -> p c n", c=2)
                            tt(e4, e4, spread(gm, 2, [P, 2, MH, P]), ALU.mult).then_inc(s["mt_ready"], 1)

                    def f2_state(b):
                        v.wait_ge(s["pv_zero"], b + 1)
                        for c in range(T - 1):
                            v.wait_ge(s["st_psum"], (T - 1) * b + (T - 1 if c else 1))
                            if c:
                                v.wait_ge(s["pv_ready"], (T - 1) * b + c)
                            for half in range(2):
                                rows = slice(half * MS, (half + 1) * MS)
                                for k in range(2):
                                    at = F2_PV + c * MI + k * P + half * MD
                                    st = SC[b][rows, at:at + MD]
                                    at_psum = (c + 1) % 2 * MI + k * P + half * MD
                                    more = PS[b][(c + 1) // 2][rows, at_psum:at_psum + MD]
                                    if c == 0:
                                        last = v.tensor_copy(st, more)
                                    else:
                                        h = 2 * k + half
                                        last = stt(st, SC[b][rows, at - MI:at - MI + MD], AF[b][rows, c, h * P + P - 1:h * P + P], more, ALU.mult, ALU.add)
                            last.then_inc(s["pv_ready"], 1)

                    def f2_finish(b):
                        v.wait_ge(s["yt_psum"], b + 1)
                        for k in range(2):
                            last = stt(cut(b, F2_YG + k * N, N), cut(b, F2_XS + k * N, N), W("f2_d")[:, k:k + 1], ps(b, 2 + k), ALU.mult, ALU.add)
                        own(last)
                        own.wait()
                        tt(cut(b, F2_YG, 2 * N), cut(b, F2_YG, 2 * N), cut(b, F2_Z, 2 * N), ALU.mult).then_inc(s["yg_ready"], 1)

                    def f2_end(b):
                        v.wait_ge(s["ym_psum"], b + 1)
                        ts(small(b, 10)[:, 0:T], first_column(ps(b, 1)), 1.0 / MI, ALU.mult, EPS, ALU.add).then_inc(s["ms_ready"], 1)
                        v.wait_ge(s["rs_ready"], b + 1)
                        v.wait_ge(s["blin_added"], b + 1)
                        for t in range(T):
                            x = X[b][:, t, :]
                            last = stt(x, ps(b, 0, D, P, t * D), small(b, 11)[:, t:t + 1], x, ALU.mult, ALU.add)
                        new_x(b, 5, last)

                    def g3_project(b, layer):
                        v.wait_ge(s["qkv_psum"], nth(layer, b))
                        ts(cut(b, G3_K, N), ps(b, 2), W(f"g3_bk{layer}"), ALU.add)
                        tt(tiles(cut(b, G3_V, N)), tiles(ps(b, 3)), spread(W(f"g3_bv{layer}"), 1, [P, T, D]), ALU.add).then_inc(s["kv_ready"], 1)

                    def g3_max(b, layer, n):
                        k = layer * T * AH + n
                        v.wait_ge(s["att_psum"], nth(k, b))
                        v.tensor_reduce(cut(b, G3_MX + n, 1), ps(b, n % 2), AX, ALU.max, negate=True).then_inc(s["att_max"], 1)

                    def g3_sum(b, layer, n):
                        k = layer * T * AH + n
                        v.wait_ge(s["att_exp"], nth(k, b))
                        v.reciprocal(cut(b, G3_RI + n, 1), cut(b, G3_SUM + n, 1)).then_inc(s["att_rsum"], 1)

                    def g3_turned(b, layer, n):
                        k = layer * T * AH + n
                        v.wait_ge(s["pT_psum"], nth(k, b))
                        if n == 2 * AH:
                            v.wait_ge(s["pv_psum"], nth(2 * layer, b))
                        pt = weights_T(b, n % AH).rearrange("p (j n) -> p j n", j=T)
                        v.tensor_copy(pt[:, :, tile(n // AH % 2)], ps(b, 2).rearrange("p (j n) -> p j n", j=T)).then_inc(s["pT_even"], 1)

                    def g3_end(b):
                        o = cut(b, G3_O, N)
                        v.wait_ge(s["g3_psum"], b + 1)
                        own(tt(tiles(o), tiles(ps(b, 0)), spread(W("g3_bout"), 1, [P, T, D]), ALU.add))
                        own.wait()
                        new_x(b, 6, stt(X[b][:, :, :], tiles(o), 0.0, X[b][:, :, :], ALU.max, ALU.add))

                    def f3_router(b):
                        v.wait_ge(s["w3_psum"], b + 1)
                        ts(cut(b, F3_W, T), first_column(ps(b, 3)), W("f3_br"), ALU.add).then_inc(s["w3_ready"], 1)

                    def f3_rank(b):
                        w, cnt, sc = cut(b, F3_W, T), cut(b, F3_CNT, 3 * T), cut(b, F3_SC, T)
                        v.wait_ge(s["w3_ready"], b + 1)
                        own(v.memset(cnt, 0.0))
                        own.wait()
                        v.wait_ge(s["row3_psum"], b + 1)
                        for t in range(T):
                            cmp = cut(b, F3_CMP + t * (N + P), N + P)
                            if t:
                                ts(cmp[:, 0:t * P], ps(b, 2, t * P), w[:, t:t + 1], ALU.is_ge, None, ALU.add, accum_out=cnt[:, 3 * t:3 * t + 1])
                            ts(cmp[:, t * P:N], ps(b, 2, N - t * P, P, t * P), w[:, t:t + 1], ALU.is_gt, None, ALU.add,
                               accum_out=cnt[:, 3 * t + 1:3 * t + 2])
                            last = stt(cmp[:, N:N + P], ps(b, 2, P, P, t * P), w[:, t:t + 1], W("lower"), ALU.is_equal, ALU.mult,
                                       accum_out=cnt[:, 3 * t + 2:3 * t + 3])
                        own(last)
                        own.wait()
                        own(v.tensor_reduce(sc, cnt.rearrange("p (t k) -> p t k", t=T), AX, ALU.add))
                        own.wait()
                        stt(sc, sc, KEPT - 0.5, w, ALU.is_lt, ALU.mult).then_inc(s["scale3_ready"], 1)

                    def f3_end(b):
                        y = cut(b, F3_Y, N)
                        v.wait_ge(s["y3_psum"], b + 1)
                        own(tt(tiles(y), tiles(ps(b, 3)), spread(W("f3_b2"), 1, [P, T, D]), ALU.add))
                        own.wait()
                        v.wait_ge(s["scale3_ready"], b + 1)
                        v.wait_ge(s["xn_added"], b + 1)
                        for t in range(T):
                            x = X[b][:, t, :]
                            last = stt(x, y[:, tile(t)], cut(b, F3_SC + t, 1), x, ALU.mult, ALU.add)
                        last.then_inc(s[f"x_new{b}"], 1)

                    def turns(g, *args):
                        for b in lanes:
                            g(b, *args)

                    turns(g0_masks)
                    for k in range(GNN0_STEPS):
                        for b in lanes:
                            g0_messages(b, k)
                            if k == 0:
                                g1_masks(b)
                            if k == GNN0_STEPS - 1 and b:
                                g0_end(b - 1)
                                f0_start(b - 1)
                            g0_gates(b, k)
                    def f0_expert(b, e):
                        if e == GATE_TURN:
                            f0_gate_columns(b)
                        f0_combine(b, e)
                        if e == GATE_TURN:
                            f0_bias(b)
                        if e == EXPERTS - 1:
                            layernorm(b, G1, X[b])

                    f0_gate(0)
                    g0_end(1)
                    f0_start(1)
                    f0_gate_end(0)
                    for e in range(EXPERTS + F0_LAG):
                        if e < EXPERTS:
                            f0_expert(0, e)
                        if e == F0_LAG - 1:
                            f0_gate(1)
                            f0_gate_end(1)
                        if e == F0_LAG + 1:
                            v.wait_ge(s["next_x_loaded"], 16 * LANES)
                            layernorm(0, NEXT, XIN[0])
                        if e == F0_LAG + 2:
                            layernorm(1, NEXT, XIN[1])
                        if e == EXPERTS + F0_LAG - 1:
                            g1_project(0)
                        if e >= F0_LAG:
                            f0_expert(1, e - F0_LAG)
                    for t in range(T + G1_LAG):
                        if t < T:
                            g1_scores(0, t)
                        if t == G1_LAG - 1:
                            g1_project(1)
                        if t >= G1_LAG:
                            g1_scores(1, t - G1_LAG)
                    def mid_step(b, i):
                        if i == 0:
                            g1_end(b)
                            layernorm(b, F1, X[b])
                        if 1 <= i < T + 1:
                            f1_logits(b, i - 1)
                        if 2 <= i < T + 2:
                            f1_sums(b, i - 2)
                        if i == T + 3:
                            f1_tokens(b)
                        if i == T + 4:
                            f1_project(b)
                        if i == T + 5:
                            f1_attend(b)
                        if i == T + 6:
                            f1_mix(b)
                        if i == T + 7:
                            f1_end(b)
                            layernorm(b, G2, X[b])
                        if i == T + 9:
                            g2_end(b)
                            layernorm(b, F2, X[b])
                        if i == T + 11:
                            f2_conv(b)
                            f2_softplus(b)
                        if i == T + 12:
                            f2_decay(b)
                            f2_cumulate(b)
                            f2_turn(b)
                        if i == T + 13:
                            f2_rows(b)
                        if i == T + 14:
                            f2_weigh(b)
                            f2_state(b)
                        if i == T + 15:
                            f2_finish(b)
                        if i == T + 16:
                            f2_end(b)
                            layernorm(b, G3, X[b])
                        if i == T + 17:
                            g3_project(b, 0)

                    for b, i in mid_order:
                        mid_step(b, i)
                    for layer in range(2):
                        if layer:
                            turns(g3_project, layer)
                        for n in range(T * AH + 2):
                            for b in lanes:
                                if n < T * AH:
                                    g3_max(b, layer, n)
                                if 1 <= n <= T * AH:
                                    g3_sum(b, layer, n - 1)
                                if n >= 2 and n % 2 == 0:
                                    g3_turned(b, layer, n - 2)
                    for b in lanes:
                        g3_end(b)
                        layernorm(b, F3, X[b])
                    turns(f3_router)
                    turns(f3_rank)
                    turns(f3_end)

                @block.gpsimd
                def _(g):
                    def root(b, n):
                        g.wait_ge(s[f"var_ready{b}"], LN_COUNT[n])
                        g.tensor_tensor(rstd[b][:, :], ve[b][:, :], minus_half[:, :], ALU.pow).then_inc(s[f"rstd_ready{b}"], 1)

                    def add_to_x(b, row, done):
                        g.tensor_tensor(X[b][:, :, :], X[b][:, :, :], spread(row, 1, [P, T, D]), ALU.add).then_inc(done, 1)

                    def f1_normalise(b, t):
                        sw = cut(b, F1_SW + t * N, N).rearrange("p (h g) -> p h g", g=SG)
                        g.wait_ge(s["sl_rsum"], f1_tile(t, b))
                        g.tensor_tensor(sw, sw, spread(cut(b, F1_RI + t * SH, SH), 2, [P, SH, SG]), ALU.mult).then_inc(s["sw_ready"], 1)

                    def g2_adjacency(b):
                        g.wait_ge(s["aggr_psum"], nth(GNN0_STEPS - 1, b))
                        g.tensor_copy(AF[b][:, :, :], ADJ[b][:, :, :]).then_inc(s["adjf_ready"], 1)

                    def f2_reading(b):
                        g.wait_ge(s["re_ready"], T * b + T)
                        g.wait_ge(s[f"cc_ready{b}"], 32)
                        g.wait_ge(s["pv_zero"], b + 1)
                        re = AF[b][:, :, :].rearrange("p c (h n) -> p c h n", h=MH)
                        for half in range(2):
                            rows = slice(half * MS, (half + 1) * MS)
                            cc = SC[b][rows, F2_CC + P:F2_CC + T * P].rearrange("p (c n) -> p c n", c=T - 1)
                            ce = SC[b][rows, F2_CE:F2_CE + (T - 1) * MI].rearrange("p (c k n) -> p c k n", c=T - 1, k=2)
                            g.tensor_tensor(ce, re[rows, 1:T, half::2, :], spread(cc, 2, [MS, T - 1, 2, P]), ALU.mult).then_inc(s["ce_ready"], 1)
                            g.wait_ge(s["ce_ready"], 2 * b + half + 1)

                    def g3_normalise(b, layer, n):
                        k = layer * T * AH + n
                        p = cut(b, G3_P + n % G3_RING * N, N)
                        g.wait_ge(s["att_rsum"], nth(k, b))
                        g.tensor_scalar(p, p, cut(b, G3_RI + n, 1), 1.0, ALU.mult, ALU.mult).then_inc(s["att_p"], 1)

                    for b in lanes:
                        root(b, F0)
                    for b in lanes:
                        root(b, NEXT)
                    for b in lanes:
                        g2_adjacency(b)
                    for b in lanes:
                        root(b, G1)
                    def mid_step(b, i):
                        if i == 0:
                            root(b, F1)
                            g.wait_ge(s[f"xn_ready{b}"], F1)
                            add_to_x(b, W("f1_bout"), s["bout_added"])
                        if 2 <= i < T + 2:
                            f1_normalise(b, i - 2)
                        if i == T + 7:
                            root(b, G2)
                        if i == T + 9:
                            root(b, F2)
                        if i == T + 10:
                            g.wait_ge(s[f"xn_ready{b}"], F2)
                            add_to_x(b, W("f2_blin"), s["blin_added"])
                        if i == T + 13:
                            g.wait_ge(s["gm_ready"], b + 1)
                            g.memset(cut(b, F2_PV, (T - 1) * MI), 0.0).then_inc(s["pv_zero"], 1)
                            f2_reading(b)
                        if i == T + 16:
                            g.wait_ge(s["ms_ready"], b + 1)
                            g.tensor_tensor(cut(b, F2_S + 11 * 16, T), cut(b, F2_S + 10 * 16, T), minus_half[:, :], ALU.pow).then_inc(s["rs_ready"], 1)
                            root(b, G3)
                            g.wait_ge(s[f"xn_ready{b}"], G3)
                            g.memset(cut(b, G3_QZ, AH * N), 0.0).then_inc(s["qz_zero"], 1)

                    for b, i in mid_order:
                        mid_step(b, i)
                    for layer in range(2):
                        for n in range(T * AH):
                            for b in lanes:
                                g3_normalise(b, layer, n)
                    for b in lanes:
                        root(b, F3)
                    for b in lanes:
                        g.wait_ge(s[f"xn_ready{b}"], F3)
                        g.tensor_tensor(X[b][:, :, :], X[b][:, :, :], XN[b][:, :, 0:D], ALU.add).then_inc(s["xn_added"], 1)

            nc.gpsimd.sem_clear(range(first_sem, last_sem + 1))
            nc.all_engine_barrier()


def lay_out(inputs):
    def rows(a, n=P):
        return np.broadcast_to(np.asarray(a, np.float32).reshape(1, -1), (n, np.asarray(a).size))

    def cols(a):
        return np.asarray(a, np.float32).reshape(-1, P).T

    def k_tiles(a):
        a = np.asarray(a, np.float32)
        return a.reshape(-1, P, a.shape[-1]).transpose(1, 0, 2).reshape(P, -1)

    g = {k: np.asarray(v) for k, v in inputs.items()}
    index = np.arange(P)
    parts = {
        "ident": np.eye(P), "tri": index[:, None] <= index[None, :], "lower": index[:, None] > index[None, :],
        "ones": np.ones((P, P)),
        "before": rows(np.arange(EXPERTS)[None, :] < np.arange(EXPERTS)[:, None]),
        "own_head": (2 * np.arange(PAIRS)[None, :, None] + (index // SG)[:, None, None]
                     == np.arange(SH)[None, None, :]).reshape(P, -1),
        "g0_wT": g["L0_gnn_weight"].transpose(2, 0, 1).reshape(D, -1),
        "g0_wih": g["L0_gnn_w_ih"].T, "g0_whh": g["L0_gnn_w_hh"].T,
        "g0_bih": cols(g["L0_gnn_b_ih"]), "g0_bhh": cols(g["L0_gnn_b_hh"]),
        "f0_gamma": cols(g["L0_ffn_gamma"]), "f0_beta": cols(g["L0_ffn_beta"]),
        "f0_wr": np.pad(g["L0_ffn_Wr"], ((0, 0), (0, P - EXPERTS))), "f0_br": rows(g["L0_ffn_br"]),
        "f0_w1": g["L0_ffn_W1"].transpose(1, 0, 2).reshape(D, -1), "f0_b1": cols(g["L0_ffn_b1"]),
        "f0_w2": k_tiles(g["L0_ffn_W2"].reshape(EXPERTS * EXPERT_H, D)), "f0_b2": g["L0_ffn_b2"],
        "g1_w": g["L1_gnn_W"], "g1_wT": g["L1_gnn_W"].T, "g1_a": cols(g["L1_gnn_a"]),
        "f1_wfx": g["L1_ffn_W_fx"], "f1_bfx": g["L1_ffn_b_fx"].reshape(SH, SD), "f1_bout": rows(g["L1_ffn_b_out"]),
        "f1_wxT": g["L1_ffn_W_x"].reshape(D, SH, SD).transpose(2, 1, 0).reshape(SD, -1),
        "f1_wslice": g["L1_ffn_W_slice"], "f1_bx": g["L1_ffn_b_x"].reshape(SH, SD).T, "f1_bslice": rows(g["L1_ffn_b_slice"]),
        "f1_temp": rows(g["L1_ffn_temperature"]),
        "f1_wqT": g["L1_ffn_W_q"].T, "f1_wkT": g["L1_ffn_W_k"].T, "f1_wvT": g["L1_ffn_W_v"].T,
        "f1_wout": g["L1_ffn_W_out"].reshape(SH, SD, D).transpose(1, 0, 2).reshape(SD, -1),
        "g2_wmsg": g["L2_gnn_W_msg"], "g2_wupd": g["L2_gnn_W_upd"], "g2_bias": rows(g["L2_gnn_bias"]),
        "f2_win": g["L2_ffn_W_in"],
        "f2_convw": g["L2_ffn_conv_w"].reshape(3, P, TAPS).transpose(1, 0, 2).reshape(P, -1), "f2_convb": cols(g["L2_ffn_conv_b"]),
        "f2_dtb": rows(g["L2_ffn_dt_bias"]), "f2_alog": rows(g["L2_ffn_A_log"]),
        "f2_d": cols(np.repeat(g["L2_ffn_D"], MD)), "f2_normw": cols(g["L2_ffn_norm_w"]),
        "f2_woutT": g["L2_ffn_W_out"].T, "f2_wlin": g["L2_ffn_W_lin"], "f2_blin": rows(g["L2_ffn_b_lin"]),
        "g3_wout": k_tiles(g["L3_gnn_Wout"]), "g3_bout": rows(g["L3_gnn_bout"]),
        "f3_wr": np.broadcast_to(g["L3_ffn_wr"], (P, P)), "f3_br": rows(g["L3_ffn_br"]), "f3_w1": g["L3_ffn_w1"], "f3_b1": cols(g["L3_ffn_b1"]),
        "f3_w2": k_tiles(g["L3_ffn_w2"]), "f3_b2": rows(g["L3_ffn_b2"]),
    }
    for n in range(2):
        for q in "qkv":
            parts[f"g3_w{q}{n}"] = k_tiles(g[f"L3_gnn_W{q}{n}"])
        for q in "qk":
            parts[f"g3_b{q}{n}"] = cols(g[f"L3_gnn_b{q}{n}"])
        parts[f"g3_bv{n}"] = rows(g[f"L3_gnn_bv{n}"])
    packs = []
    for table in (WEIGHTS, RAW):
        at, width = columns_of(table)
        pack = np.zeros((P, width), np.float32)
        for name, n_rows, n_cols in table:
            pack[0:n_rows, at[name][0]:at[name][0] + n_cols] = parts[name]
        packs.append(pack)
    return packs


def kernel(**inputs):
    import concourse.bacc as bacc
    from concourse.bass_utils import run_bass_kernel_spmd

    weights, raw = lay_out(inputs)
    arrays = {
        "x": np.ascontiguousarray(inputs["x"]), "adj": np.ascontiguousarray(inputs["adj"]),
        "weights": weights, "raw": raw,
    }
    nc = bacc.Bacc("TRN2", target_bir_lowering=False, num_devices=1)
    aps = [nc.dram_tensor(k, a.shape, mybir.dt.from_np(a.dtype), kind="ExternalInput").ap() for k, a in arrays.items()]
    out = nc.dram_tensor("out", arrays["x"].shape, F32, kind="ExternalOutput").ap()
    build(nc, *aps, out)
    result = run_bass_kernel_spmd(nc, [arrays], core_ids=[0])
    return result.results[0]["out"]
```
